# Optimizing a Trainium2 kernel written in Bass

```python
import numpy as np
import jax
import jax.numpy as jnp

def _softmax(x, axis=-1):
    return jax.nn.softmax(x, axis=axis)

def _gelu(x):
    return jax.nn.gelu(x, approximate=True)

def _silu(x):
    return jax.nn.silu(x)

def _sigmoid(x):
    return jax.nn.sigmoid(x)

def _layernorm(x, axis=-1, eps=1e-05):
    m = jnp.mean(x, axis=axis, keepdims=True)
    v = jnp.var(x, axis=axis, keepdims=True)
    return (x - m) / jnp.sqrt(v + eps)

def _scatter_add(tgt, idx, src, axis=0):
    return tgt.at[idx].add(src)

def _segment_sum(src, seg, n):
    return jax.ops.segment_sum(src, seg, n)
kernel_name = 'mk_gnn_resnorm_d4_gnn_r64_0c5959'

def setup_inputs(seed: int=0):
    np.random.seed(seed)
    _w = jnp.asarray

    def _rec_inputs():
        import jax
        import jax.numpy as jnp
        _gk = jax.random.key(seed)
        x = -0.0005121 + 1.001 * jax.random.normal(jax.random.fold_in(_gk, 1), (100000, 32), jnp.float32)
        src = jax.random.randint(jax.random.fold_in(_gk, 2), (25000,), 0, 100000, jnp.int32)
        dst = jnp.minimum((100000 * jax.random.uniform(jax.random.fold_in(_gk, 3), (25000,)) ** 2.0).astype(jnp.int32), 99999)
        _o = jnp.argsort(dst, stable=True)
        src = src[_o]
        dst = dst[_o]
        edge_attr_10 = jax.random.uniform(jax.random.fold_in(_gk, 12), (25000, 10), jnp.float32, 0.0, 1)
        edge_attr_3 = 0.00109039 + 0.999626 * jax.random.normal(jax.random.fold_in(_gk, 13), (25000, 3), jnp.float32)
        edge_weight = jax.random.uniform(jax.random.fold_in(_gk, 15), (25000,), jnp.float32, 0.0, 1)
        return (x, src, dst, edge_attr_10, edge_attr_3, edge_weight)
    x, src, dst, edge_attr_10, edge_attr_3, edge_weight = _rec_inputs()

    def _L0_gnn_setup():
        import jax, jax.numpy as jnp
        import numpy as np
        N_NODES = 100000
        N_EDGES = 25000
        F_IN = 32
        F_OUT = 32
        key = jax.random.key(seed)
        kx, kr, kc, kv, kw = jax.random.split(key, 5)
        x = jax.random.normal(kx, (N_NODES, F_IN), dtype=jnp.float32)
        rows = jnp.sort(jax.random.randint(kr, (N_EDGES,), 0, N_NODES, dtype=jnp.int64))
        cols = jax.random.randint(kc, (N_EDGES,), 0, N_NODES, dtype=jnp.int64)
        vals = jax.random.uniform(kv, (N_EDGES,), dtype=jnp.float32)
        weight = jax.random.normal(kw, (F_IN, F_OUT), dtype=jnp.float32) / np.sqrt(F_IN)
        return {'x': x, 'rows': rows, 'cols': cols, 'vals': vals, 'weight': weight}
    _L0_gnn_all = _L0_gnn_setup()
    _L0_gnn_in = {k: v for k, v in _L0_gnn_all.items() if k in ('weight',)}
    del _L0_gnn_all

    def _L1_gnn_setup():
        import jax, jax.numpy as jnp
        import numpy as np
        N = 100000
        E = 25000
        F_IN = 32
        F_OUT = 32
        key = jax.random.key(seed)
        k1, k2, k3, k4, k5 = jax.random.split(key, 5)
        x = jax.random.normal(k1, (N, F_IN), dtype=jnp.float32)
        edge_src = jax.random.randint(k2, (E,), 0, N, dtype=jnp.int32)
        edge_dst = jax.random.randint(k3, (E,), 0, N, dtype=jnp.int32)
        bound = 1.0 / np.sqrt(2 * F_IN)
        W = jax.random.uniform(k4, (2 * F_IN, F_OUT), minval=-bound, maxval=bound, dtype=jnp.float32)
        b = jax.random.uniform(k5, (F_OUT,), minval=-bound, maxval=bound, dtype=jnp.float32)
        return {'x': x, 'W': W, 'b': b, 'edge_src': edge_src, 'edge_dst': edge_dst}
    _L1_gnn_all = _L1_gnn_setup()
    _L1_gnn_in = {k: v for k, v in _L1_gnn_all.items() if k in ('W', 'b')}
    del _L1_gnn_all

    def _L2_gnn_setup():
        import jax, jax.numpy as jnp
        import numpy as np
        N, E = (100000, 25000)
        F_IN, H, F_OUT = (32, 64, 32)
        K, T = (3, 2)
        EPS = 1e-05

        def gcn_norm(src, dst, ew, num_nodes):
            deg = jax.ops.segment_sum(ew, dst, num_segments=num_nodes)
            dinv = jnp.where(deg > 0, jax.lax.rsqrt(deg), 0.0)
            return dinv[src] * ew * dinv[dst]

        def arma_conv(x, src, dst, norm, init_w, w, root_w, b):
            n = x.shape[0]
            out = jnp.einsum('nf,kfg->kng', x, init_w)
            n_layers = root_w.shape[0]
            for t in range(n_layers):
                if t > 0:
                    out = jnp.einsum('kng,kgh->knh', out, w[t - 1])
                msg = out[:, src, :] * norm[None, :, None]
                agg = jax.ops.segment_sum(msg.transpose(1, 0, 2), dst, num_segments=n)
                out = agg.transpose(1, 0, 2)
                out = out + jnp.einsum('nf,kfg->kng', x, root_w[t]) + b[t]
                out = jax.nn.relu(out)
            return out.mean(axis=0)
        key = jax.random.key(seed)
        ks = jax.random.split(key, 17)

        def p(k, shape, scale=0.1):
            return jax.random.normal(k, shape, dtype=jnp.float32) * scale
        return {'x': jax.random.normal(ks[0], (N, F_IN), dtype=jnp.float32), 'edge_index': jax.random.randint(ks[1], (2, E), 0, N), 'weights': jax.random.uniform(ks[2], (E,), dtype=jnp.float32), 'c1_init': p(ks[3], (K, F_IN, H)), 'c1_w': p(ks[4], (T - 1, K, H, H)), 'c1_root': p(ks[5], (T, K, F_IN, H)), 'c1_b': p(ks[6], (T, K, 1, H)), 'c2_init': p(ks[7], (K, H, H)), 'c2_w': p(ks[8], (T - 1, K, H, H)), 'c2_root': p(ks[9], (T, K, H, H)), 'c2_b': p(ks[10], (T, K, 1, H)), 'c3_init': p(ks[11], (K, H, F_OUT)), 'c3_w': p(ks[12], (T - 1, K, F_OUT, F_OUT)), 'c3_root': p(ks[13], (T, K, H, F_OUT)), 'c3_b': p(ks[14], (T, K, 1, F_OUT)), 'bn_gamma': jnp.ones((F_OUT,), jnp.float32), 'bn_beta': jnp.zeros((F_OUT,), jnp.float32)}
    _L2_gnn_all = _L2_gnn_setup()
    _L2_gnn_in = {k: v for k, v in _L2_gnn_all.items() if k in ('c1_init', 'c1_w', 'c1_root', 'c1_b', 'c2_init', 'c2_w', 'c2_root', 'c2_b', 'c3_init', 'c3_w', 'c3_root', 'c3_b', 'bn_gamma', 'bn_beta')}
    del _L2_gnn_all

    def _L3_gnn_setup():
        import jax, jax.numpy as jnp
        import numpy as np
        MUL = 16
        MOUT = 8
        TANH_GAIN = 1.593
        INV_SQRT3 = 0.5773502691896258
        PW_S = 0.17677669529663687
        PW_V = 0.25

        def _w3j_121():
            s2, s6 = (2 ** 0.5, 6 ** 0.5)
            M = np.zeros((5, 3, 3))
            M[0, 0, 1] = M[0, 1, 0] = 1 / s2
            M[1, 1, 2] = M[1, 2, 1] = 1 / s2
            M[2] = np.diag([-1.0, -1.0, 2.0]) / s6
            M[3, 0, 2] = M[3, 2, 0] = 1 / s2
            M[4] = np.diag([1.0, -1.0, 0.0]) / s2
            return jnp.asarray(np.transpose(M, (1, 0, 2)) / 5 ** 0.5, jnp.float32)
        W3J121 = _w3j_121()

        def _sph(edge_vec):
            n = edge_vec / jnp.linalg.norm(edge_vec, axis=1, keepdims=True)
            x, y, z = (n[:, 0], n[:, 1], n[:, 2])
            y1 = 3.0 ** 0.5 * n
            s15 = 15.0 ** 0.5
            y2 = jnp.stack([s15 * x * y, s15 * y * z, 5.0 ** 0.5 / 2 * (3 * z * z - 1), s15 * x * z, s15 / 2 * (x * x - y * y)], axis=1)
            return (y1, y2)

        def _forward(x, edge_src, edge_dst, edge_vec, emb, norm, W1, W2):
            N, E = (x.shape[0], edge_src.shape[0])
            xs = jnp.concatenate([x[edge_src, :8], x[edge_dst, :8]], axis=1)
            xv = jnp.concatenate([x[edge_src, 8:].reshape(E, 8, 3), x[edge_dst, 8:].reshape(E, 8, 3)], axis=1)
            y1, y2 = _sph(edge_vec)
            h = 2.0 ** 0.5 * jax.nn.relu(emb @ W1 / 10.0 ** 0.5)
            w = (h @ W2 / 16.0 ** 0.5).reshape(E, 7, MUL, MOUT)
            wa_s, wb_s, wa_g, wb_g, wc, wd, we = [w[:, i] for i in range(7)]
            s_out = PW_S * (jnp.einsum('eu,euw->ew', xs, wa_s) + INV_SQRT3 * jnp.einsum('eui,ei,euw->ew', xv, y1, wb_s))
            g_out = PW_S * (jnp.einsum('eu,euw->ew', xs, wa_g) + INV_SQRT3 * jnp.einsum('eui,ei,euw->ew', xv, y1, wb_g))
            v_out = PW_V * (INV_SQRT3 * jnp.einsum('eu,ek,euw->ewk', xs, y1, wc) + INV_SQRT3 * jnp.einsum('eui,euw->ewi', xv, wd) + jnp.einsum('eui,ea,iak,euw->ewk', xv, y2, W3J121, we))
            s_act = TANH_GAIN * jnp.tanh(s_out)
            gates = TANH_GAIN * jnp.tanh(g_out)
            edge_ftr = jnp.concatenate([s_act, (gates[:, :, None] * v_out).reshape(E, 24)], axis=1) * norm[:, None]
            return jax.ops.segment_sum(edge_ftr, edge_dst, num_segments=N)
        key = jax.random.key(seed)
        ks = jax.random.split(key, 8)
        N, E = (50000, 300000)
        return {'x': jax.random.normal(ks[0], (N, 32), jnp.float32), 'edge_src': jax.random.randint(ks[1], (E,), 0, N), 'edge_dst': jax.random.randint(ks[2], (E,), 0, N), 'edge_vec': jax.random.normal(ks[3], (E, 3), jnp.float32), 'emb': jax.random.uniform(ks[4], (E, 10), jnp.float32), 'norm': jax.random.uniform(ks[5], (E,), jnp.float32), 'W1': jax.random.normal(ks[6], (10, 16), jnp.float32), 'W2': jax.random.normal(ks[7], (16, 896), jnp.float32)}
    _L3_gnn_all = _L3_gnn_setup()
    _L3_gnn_in = {k: v for k, v in _L3_gnn_all.items() if k in ('W1', 'W2')}
    del _L3_gnn_all
    return {'x': x, 'src': src, 'dst': dst, 'edge_attr_10': edge_attr_10, 'edge_attr_3': edge_attr_3, 'edge_weight': edge_weight, 'L0_gnn_weight': _L0_gnn_in['weight'], 'L1_gnn_W': _L1_gnn_in['W'], 'L1_gnn_b': _L1_gnn_in['b'], 'L2_gnn_c1_init': _L2_gnn_in['c1_init'], 'L2_gnn_c1_w': _L2_gnn_in['c1_w'], 'L2_gnn_c1_root': _L2_gnn_in['c1_root'], 'L2_gnn_c1_b': _L2_gnn_in['c1_b'], 'L2_gnn_c2_init': _L2_gnn_in['c2_init'], 'L2_gnn_c2_w': _L2_gnn_in['c2_w'], 'L2_gnn_c2_root': _L2_gnn_in['c2_root'], 'L2_gnn_c2_b': _L2_gnn_in['c2_b'], 'L2_gnn_c3_init': _L2_gnn_in['c3_init'], 'L2_gnn_c3_w': _L2_gnn_in['c3_w'], 'L2_gnn_c3_root': _L2_gnn_in['c3_root'], 'L2_gnn_c3_b': _L2_gnn_in['c3_b'], 'L2_gnn_bn_gamma': _L2_gnn_in['bn_gamma'], 'L2_gnn_bn_beta': _L2_gnn_in['bn_beta'], 'L3_gnn_W1': _L3_gnn_in['W1'], 'L3_gnn_W2': _L3_gnn_in['W2']}

def reference(x, src, dst, edge_attr_10, edge_attr_3, edge_weight, L0_gnn_weight, L1_gnn_W, L1_gnn_b, L2_gnn_c1_init, L2_gnn_c1_w, L2_gnn_c1_root, L2_gnn_c1_b, L2_gnn_c2_init, L2_gnn_c2_w, L2_gnn_c2_root, L2_gnn_c2_b, L2_gnn_c3_init, L2_gnn_c3_w, L2_gnn_c3_root, L2_gnn_c3_b, L2_gnn_bn_gamma, L2_gnn_bn_beta, L3_gnn_W1, L3_gnn_W2):
    import jax
    import jax.numpy as jnp

    def _L0_gnn_ref(x, rows, cols, vals, weight):
        import jax, jax.numpy as jnp
        import numpy as np
        N_NODES = 100000
        N_EDGES = 25000
        F_IN = 32
        F_OUT = 32
        gathered = x[cols] * vals[:, None]
        z = jax.ops.segment_sum(gathered, rows, num_segments=x.shape[0])
        return z @ weight

    def _L1_gnn_ref(x, W, b, edge_src, edge_dst):
        import jax, jax.numpy as jnp
        import numpy as np
        N = 100000
        E = 25000
        F_IN = 32
        F_OUT = 32
        n = x.shape[0]
        msgs = x[edge_src]
        summed = jax.ops.segment_sum(msgs, edge_dst, num_segments=n)
        cnt = jax.ops.segment_sum(jnp.ones_like(edge_dst, dtype=x.dtype), edge_dst, num_segments=n)
        neigh_mean = summed / jnp.maximum(cnt, 1.0)[:, None]
        h = jnp.concatenate([x, neigh_mean], axis=1)
        return jax.nn.relu(h @ W + b)

    def _L2_gnn_ref(x, edge_index, weights, c1_init, c1_w, c1_root, c1_b, c2_init, c2_w, c2_root, c2_b, c3_init, c3_w, c3_root, c3_b, bn_gamma, bn_beta):
        import jax, jax.numpy as jnp
        import numpy as np
        N, E = (100000, 25000)
        F_IN, H, F_OUT = (32, 64, 32)
        K, T = (3, 2)
        EPS = 1e-05

        def gcn_norm(src, dst, ew, num_nodes):
            deg = jax.ops.segment_sum(ew, dst, num_segments=num_nodes)
            dinv = jnp.where(deg > 0, jax.lax.rsqrt(deg), 0.0)
            return dinv[src] * ew * dinv[dst]

        def arma_conv(x, src, dst, norm, init_w, w, root_w, b):
            n = x.shape[0]
            out = jnp.einsum('nf,kfg->kng', x, init_w)
            n_layers = root_w.shape[0]
            for t in range(n_layers):
                if t > 0:
                    out = jnp.einsum('kng,kgh->knh', out, w[t - 1])
                msg = out[:, src, :] * norm[None, :, None]
                agg = jax.ops.segment_sum(msg.transpose(1, 0, 2), dst, num_segments=n)
                out = agg.transpose(1, 0, 2)
                out = out + jnp.einsum('nf,kfg->kng', x, root_w[t]) + b[t]
                out = jax.nn.relu(out)
            return out.mean(axis=0)
        src, dst = (edge_index[0], edge_index[1])
        norm = gcn_norm(src, dst, weights, x.shape[0])
        h = jax.nn.relu(arma_conv(x, src, dst, norm, c1_init, c1_w, c1_root, c1_b))
        h = jax.nn.relu(arma_conv(h, src, dst, norm, c2_init, c2_w, c2_root, c2_b))
        h = arma_conv(h, src, dst, norm, c3_init, c3_w, c3_root, c3_b)
        mean = h.mean(axis=0)
        var = h.var(axis=0)
        h = (h - mean) * jax.lax.rsqrt(var + EPS) * bn_gamma + bn_beta
        return jax.nn.relu(h)

    def _L3_gnn_ref(x, edge_src, edge_dst, edge_vec, emb, norm, W1, W2):
        import jax, jax.numpy as jnp
        import numpy as np
        MUL = 16
        MOUT = 8
        TANH_GAIN = 1.593
        INV_SQRT3 = 0.5773502691896258
        PW_S = 0.17677669529663687
        PW_V = 0.25

        def _w3j_121():
            s2, s6 = (2 ** 0.5, 6 ** 0.5)
            M = np.zeros((5, 3, 3))
            M[0, 0, 1] = M[0, 1, 0] = 1 / s2
            M[1, 1, 2] = M[1, 2, 1] = 1 / s2
            M[2] = np.diag([-1.0, -1.0, 2.0]) / s6
            M[3, 0, 2] = M[3, 2, 0] = 1 / s2
            M[4] = np.diag([1.0, -1.0, 0.0]) / s2
            return jnp.asarray(np.transpose(M, (1, 0, 2)) / 5 ** 0.5, jnp.float32)
        W3J121 = _w3j_121()

        def _sph(edge_vec):
            n = edge_vec / jnp.linalg.norm(edge_vec, axis=1, keepdims=True)
            x, y, z = (n[:, 0], n[:, 1], n[:, 2])
            y1 = 3.0 ** 0.5 * n
            s15 = 15.0 ** 0.5
            y2 = jnp.stack([s15 * x * y, s15 * y * z, 5.0 ** 0.5 / 2 * (3 * z * z - 1), s15 * x * z, s15 / 2 * (x * x - y * y)], axis=1)
            return (y1, y2)

        def _forward(x, edge_src, edge_dst, edge_vec, emb, norm, W1, W2):
            N, E = (x.shape[0], edge_src.shape[0])
            xs = jnp.concatenate([x[edge_src, :8], x[edge_dst, :8]], axis=1)
            xv = jnp.concatenate([x[edge_src, 8:].reshape(E, 8, 3), x[edge_dst, 8:].reshape(E, 8, 3)], axis=1)
            y1, y2 = _sph(edge_vec)
            h = 2.0 ** 0.5 * jax.nn.relu(emb @ W1 / 10.0 ** 0.5)
            w = (h @ W2 / 16.0 ** 0.5).reshape(E, 7, MUL, MOUT)
            wa_s, wb_s, wa_g, wb_g, wc, wd, we = [w[:, i] for i in range(7)]
            s_out = PW_S * (jnp.einsum('eu,euw->ew', xs, wa_s) + INV_SQRT3 * jnp.einsum('eui,ei,euw->ew', xv, y1, wb_s))
            g_out = PW_S * (jnp.einsum('eu,euw->ew', xs, wa_g) + INV_SQRT3 * jnp.einsum('eui,ei,euw->ew', xv, y1, wb_g))
            v_out = PW_V * (INV_SQRT3 * jnp.einsum('eu,ek,euw->ewk', xs, y1, wc) + INV_SQRT3 * jnp.einsum('eui,euw->ewi', xv, wd) + jnp.einsum('eui,ea,iak,euw->ewk', xv, y2, W3J121, we))
            s_act = TANH_GAIN * jnp.tanh(s_out)
            gates = TANH_GAIN * jnp.tanh(g_out)
            edge_ftr = jnp.concatenate([s_act, (gates[:, :, None] * v_out).reshape(E, 24)], axis=1) * norm[:, None]
            return jax.ops.segment_sum(edge_ftr, edge_dst, num_segments=N)
        return _forward(x, edge_src, edge_dst, edge_vec, emb, norm, W1, W2)
    edge_index = jnp.stack([src, dst])
    x = _layernorm(x + _L0_gnn_ref(x, src, dst, edge_weight, L0_gnn_weight), axis=-1)
    x = _layernorm(x + _L1_gnn_ref(x, L1_gnn_W, L1_gnn_b, src, dst), axis=-1)
    x = _layernorm(x + _L2_gnn_ref(x, edge_index, edge_weight, L2_gnn_c1_init, L2_gnn_c1_w, L2_gnn_c1_root, L2_gnn_c1_b, L2_gnn_c2_init, L2_gnn_c2_w, L2_gnn_c2_root, L2_gnn_c2_b, L2_gnn_c3_init, L2_gnn_c3_w, L2_gnn_c3_root, L2_gnn_c3_b, L2_gnn_bn_gamma, L2_gnn_bn_beta), axis=-1)
    x = _layernorm(x + _L3_gnn_ref(x, src, dst, edge_attr_3, edge_attr_10, edge_weight, L3_gnn_W1, L3_gnn_W2), axis=-1)
    return x

_drawn_inputs = setup_inputs


def setup_inputs(seed=0):
    import zlib

    import numpy as np

    out = dict(_drawn_inputs(seed))
    spreads = {'L2_gnn_bn_gamma': (1.0, 0.2), 'L2_gnn_bn_beta': (0.0, 0.1)}
    factors = {}
    for name, (base, spread) in spreads.items():
        noise = np.random.default_rng([zlib.crc32(name.encode()), seed]).standard_normal(out[name].shape)
        drawn = base * np.exp(spread * noise) if base else spread * noise
        out[name] = jnp.asarray(drawn.astype(out[name].dtype))
    for name, factor in factors.items():
        out[name] = (out[name] * factor).astype(out[name].dtype)
    return out
```

```python
import concourse.bass as bass
from concourse import mybir
from contextlib import ExitStack

F32 = mybir.dt.float32
I32 = mybir.dt.int32
U8 = mybir.dt.uint8
ALU = mybir.AluOpType
ACT = mybir.ActivationFunctionType
AX = mybir.AxisListType.X

P = 125
C = 4
PG = P * C
LEAD = 2
FAR = 1 << 20
EPS = 1e-5


def over(ap, n):
    return ap.unsqueeze(ap.ndim).broadcast_to(list(ap.shape) + [n])


class Phase(ExitStack):

    def __init__(self, nc):
        super().__init__()
        self.nc, self.sems, self.blk = nc, [], None

    def open(self):
        self.blk = self.nc.Block()
        return self.blk.__enter__()

    def close_sems(self):
        with self.nc.Block() as block:
            @block.sync
            def _(sp):
                for s in self.sems:
                    sp.sem_clear(s)

    def __exit__(self, *error):
        if self.blk is not None:
            self.blk.__exit__(*error)
        if error[0] is None:
            self.close_sems()
        return super().__exit__(*error)


class Links:

    def __init__(self, eng, sem):
        self.eng, self.sem, self.base, self.n, self.i, self.per = eng, sem, 0, 0, 0, 0

    def turn(self, i, per):
        self.i, self.per, self.n = i, per, 0

    def __call__(self, ins):
        ins.then_inc(self.sem, 1)
        self.n += 1
        self.eng.wait_ge(self.sem, self.i * self.per + self.base + self.n)

    def end(self, turns):
        assert self.n == self.per, (self.n, self.per)
        self.base += turns * self.per
        self.i = self.per = self.n = 0


def gnn_kernel(nc, a, out):
    x, src, dst = a["x"], a["src"], a["dst"]
    N, F = x.shape
    E = src.shape[0]
    T = E // P
    NG = T // C
    H = a["L2_gnn_c1_init"].shape[2]
    K = a["L2_gnn_c1_init"].shape[0]
    NIL = E
    SW = F + 2
    ROW = T // 2
    SUB = 4
    ND = N // (PG * SUB)
    NPP = N // P // ND
    TINY = 1e-30
    MUL, MOUT, PATHS = 16, 8, 7

    ctx = ExitStack()

    with ctx:
        def sb(name, shape, dt=F32, c=ctx):
            return c.enter_context(nc.sbuf_tensor(name, shape, dt))

        def pb(name, shape, c):
            return c.enter_context(nc.psum_tensor(name, shape, F32))

        def sem(name, c=ctx):
            s = c.enter_context(nc.semaphore(name))
            if c is not ctx:
                c.sems.append(s)
            return s

        def dram(name, shape, dt=F32):
            return nc.dram_tensor(name, shape, dt, kind="Internal").ap()

        ytab = dram("ytab", [N + P, F])
        slot_tab = dram("slot_tab", [N, 1], I32)
        same_row = dram("same_row", [E], U8)
        mtab = dram("mtab", [E + 1, SW])
        atab = [dram("a1tab", [E + 1, F]), dram("a2tab", [E + 1, H]), dram("a3tab", [E + 1, H])]
        htab = [dram("h1tab", [E, H]), dram("h2tab", [E, H]), dram("xhtab", [E, 2 * F])]
        btab = [dram("b1tab", [E, H]), dram("b2tab", [E, H]), dram("xbtab", [E, 2 * F])]
        x2d = dram("x2d", [N, F])
        h3d = dram("h3d", [N, F])

        def rows(tab, g, n=C):
            return tab[0:E, :].rearrange("(p t) f -> p t f", p=P)[:, bass.ds(g * C, n), :]

        def nodes(tab, g):
            return tab[0:N, :].rearrange("(g p n) f -> g p n f", g=ND, p=P)[bass.ds(g, 1)].rearrange("g p n f -> p (g n) f")

        ident = sb("ident", [128, 128])
        ones = sb("ones", [128, 128])
        lower = sb("lower", [128, P])
        trash = sb("trash", [128, 1])
        epsc = sb("epsc", [128, 1])
        zero = sb("zero", [128, 1])
        src_i = sb("src_i", [128, T], I32)
        dst_i = sb("dst_i", [128, T + C], I32)
        last_i = sb("last_i", [128, T], I32)
        rid_i = sb("rid_i", [128, T], I32)
        slot_i = sb("slot_i", [128, T], I32)
        slot_t = sb("slot_t", [128, T], I32)
        src_f = sb("src_f", [128, T])
        ew = sb("ew", [128, T])
        norm = sb("norm", [128, T])
        dinv_t = sb("dinv_t", [128, T])
        same_b = sb("same_b", [128, E], U8)
        stat = sb("stat", [128, 2, F])
        w0 = sb("w0", [F, F])
        w1e = sb("w1e", [2 * F + 1, F])
        w1d = sb("w1d", [F + 1, F])
        fins, hs = [F, H, H], [H, H, F]
        wbias = []
        wroot0 = []
        wroot1 = []
        wblk = []
        for n in range(3):
            k0 = 2 * F + 1 if n == 0 else H + 1
            wbias.append(sb(f"wbias{n}", [k0, K * hs[n]]))
            wroot0.append(None if n == 0 else sb(f"wroot0_{n}", [H, K * hs[n]]))
            wroot1.append(sb(f"wroot1_{n}", [fins[n] + 1, K * hs[n]]))
            wblk.append([sb(f"wblka{n}", [128 if hs[n] == H else K * F, 2 * H if hs[n] == H else K * F]),
                         sb(f"wblkb{n}", [H, H]) if hs[n] == H else None])
        wl1 = sb("wl1", [10, MUL])
        wl2 = sb("wl2", [MUL, PATHS * MUL * MOUT])
        wmix = sb("wmix", [MUL, 3 * MOUT * 2 * MUL])
        wvec = sb("wvec", [MUL, MOUT * MUL])
        gamma = sb("gamma", [128, F])
        beta = sb("beta", [128, F])
        x2s = sb("x2s", [128, T, F])
        x2t = sb("x2t", [128, T, F])

        pool_tick, act_tick, dve_tick, pe_tick, sp_tick = (sem(f"{e}_tick") for e in ("pool", "act", "dve", "pe", "sp"))

        gathered = [sem(f"gathered{s}") for s in range(2)]
        added, slotted = sem("added"), sem("slotted")
        g_base = [0, 0]

        def done(g):
            return g + 1 + LEAD

        def free(g):
            return g - 1 + LEAD

        def free1(g):
            return g + LEAD

        def credit(eng, *sems):
            for s in sems:
                eng.sem_inc(s, LEAD)

        def center(link, c, sm, sq, v, x):
            link(nc.vector.reduce_sum(sm, x, AX))
            link(nc.vector.scalar_tensor_tensor(c, over(sm, F), -1.0 / F, x, ALU.mult, ALU.add))
            link(nc.vector.tensor_tensor(sq, c, c, ALU.mult))
            return nc.vector.reduce_sum(v, sq, AX)

        def deviation(sd, v):
            return nc.scalar.activation(sd, v, ACT.Sqrt, bias=epsc[0:P, 0:1], scale=1.0 / F)

        with Phase(nc) as ph:
            loaded = sem("loaded", ph)
            made = sem("made", ph)
            zeroed = sem("zeroed", ph)
            init_done = sem("init_done", ph)
            nils = sb("nils", [P, N // P], I32, ph)
            zrow = sb("zrow", [128, H], F32, ph)
            block = ph.open()
            n_loads = [0]

            @block.vector
            def _(dve):
                nc.vector.memset(ones[:], 1.0)
                nc.vector.memset(epsc[:], EPS)
                nc.vector.memset(zero[:], 0.0)
                nc.vector.memset(dst_i[:], 0)
                nc.vector.memset(stat[:], 0.0)
                nc.vector.memset(zrow[:], 0.0)
                nc.vector.memset(nils[:], NIL)
                for n in range(3):
                    nc.vector.memset(wblk[n][0][:], 0.0)
                nc.vector.memset(w0[:], 0.0).then_inc(zeroed, 1)

            @block.gpsimd
            def _(pool):
                nc.gpsimd.memset(ident[:], 0.0).then_inc(made, 1)
                nc.gpsimd.memset(lower[:], 0.0).then_inc(made, 1)
                pool.wait_ge(made, 2)
                nc.gpsimd.affine_select(out=ident[:], in_=ident[:], compare_op=ALU.not_equal, fill=1.0, base=0,
                                        pattern=[[-1, 128]], channel_multiplier=1)
                nc.gpsimd.affine_select(out=lower[:], in_=lower[:], compare_op=ALU.is_ge, fill=1.0, base=0,
                                        pattern=[[1, P]], channel_multiplier=-1)
                nc.gpsimd.iota(trash[:], pattern=[[0, 1]], base=N, channel_multiplier=1,
                               allow_small_or_imprecise_dtypes=True)
                nc.gpsimd.iota(rid_i[:], pattern=[[1, T]], base=0, channel_multiplier=T)

            @block.sync
            def _(sp):
                def load(to, of):
                    sp.dma_start(to, of).then_inc(loaded, 16)
                    n_loads[0] += 1

                sp.wait_ge(zeroed, 1)
                load(w0[:], a["L0_gnn_weight"])
                load(w1e[0:2 * F, :], a["L1_gnn_W"])
                load(w1e[2 * F:2 * F + 1, :], a["L1_gnn_b"].rearrange("(o f) -> o f", o=1))
                load(w1d[0:F, :], a["L1_gnn_W"][0:F, :])
                load(w1d[F:F + 1, :], a["L1_gnn_b"].rearrange("(o f) -> o f", o=1))
                for n in range(3):
                    init, w, root, b = (a[f"L2_gnn_c{n + 1}_{s}"] for s in ("init", "w", "root", "b"))
                    h, f = hs[n], fins[n]
                    kb = wbias[n].shape[0] - 1
                    kv = lambda t: t.rearrange("f (k g) -> f k g", k=K)
                    load(kv(wbias[n][kb - f:kb, :]), init.rearrange("k f g -> f k g"))
                    load(kv(wbias[n][kb:kb + 1, :]), b[0].rearrange("k o g -> o k g"))
                    load(kv((wbias[n] if n == 0 else wroot0[n])[0:f, :]), root[0].rearrange("k f g -> f k g"))
                    load(kv(wroot1[n][0:f, :]), root[1].rearrange("k f g -> f k g"))
                    load(kv(wroot1[n][f:f + 1, :]), b[1].rearrange("k o g -> o k g"))
                    for k in range(K):
                        if h == H and k == 2:
                            load(wblk[n][1][:, :], w[0, k])
                        else:
                            load(wblk[n][0][k * h:(k + 1) * h, k * h:(k + 1) * h], w[0, k])
                load(wl1[:], a["L3_gnn_W1"])
                load(wl2[:], a["L3_gnn_W2"])
                load(gamma[:], a["L2_gnn_bn_gamma"].partition_broadcast(128))
                load(beta[:], a["L2_gnn_bn_beta"].partition_broadcast(128))
                inits = [(ytab[0:N, :].rearrange("(p n) f -> p (n f)", p=P), x.rearrange("(p n) f -> p (n f)", p=P)),
                         (ytab[N:N + P, :], zrow[0:P, 0:F]),
                         (slot_tab.rearrange("(p n) o -> p (n o)", p=P), nils[:]),
                         (mtab[NIL:NIL + 1, :], zrow[0:1, 0:SW])]
                inits += [(atab[n][NIL:NIL + 1, :], zrow[0:1, 0:fins[n]]) for n in range(3)]
                for to, of in inits:
                    sp.dma_start(to, of).then_inc(init_done, 16)
                sp.wait_ge(loaded, 16 * n_loads[0])
                sp.wait_ge(init_done, 16 * len(inits))

        with Phase(nc) as ph:
            folded = sem("folded", ph)
            block = ph.open()

            @block.scalar
            def _(act):
                for n in range(3):
                    for w in (wroot1[n], wblk[n][0], wblk[n][1]):
                        if w is not None:
                            nc.scalar.mul(w[:], w[:], 1.0 / K)
                nc.scalar.mul(wl1[:], wl1[:], 0.2 ** 0.5)

            @block.vector
            def _(dve):
                ps, pv = 0.17677669529663687 / MUL ** 0.5, 0.25 / MUL ** 0.5
                path = lambda i: wl2[:, i * MUL * MOUT:(i + 1) * MUL * MOUT].rearrange("j (u w) -> j w u", u=MUL)
                mix = wmix[:].rearrange("j (o w h u) -> j o w h u", o=3, w=MOUT, h=2)
                vec = wvec[:].rearrange("j (w u) -> j w u", w=MOUT)
                for o, h, i, c in ((0, 0, 0, ps), (0, 1, 1, ps), (1, 0, 2, ps), (1, 1, 3, ps), (2, 0, 4, pv), (2, 1, 6, pv * 1.5 ** 0.5)):
                    nc.vector.tensor_scalar(mix[:, o, :, h], path(i), c, None, ALU.mult)
                nc.vector.tensor_scalar(vec, path(5), pv * 0.5773502691896258, None, ALU.mult).then_inc(folded, 1)
                dve.wait_ge(folded, 1)
                nc.vector.scalar_tensor_tensor(vec, path(6), -pv * 1.5 ** 0.5 / 3, vec, ALU.mult, ALU.add).then_inc(folded, 1)

        with Phase(nc) as ph:
            loaded = sem("rows_loaded", ph)
            filled = sem("rows_filled", ph)
            stored = sem("same_stored", ph)
            bcast = sem("same_bcast", ph)
            dlink = sem("prep_link", ph)
            row_ready = sem("row_ready", ph)
            turned = sem("turned", ph)
            taken = sem("taken", ph)
            ri = sb("ri", [ROW, 2, 2, P], I32, ph)
            edge_i = sb("edge_i", [ROW, 2, 2], I32, ph)
            rf = sb("rf", [ROW, 2, P + 2], F32, ph)
            cols = sb("cols", [ROW, 7, 2, P], F32, ph)
            same_f = sb("same_f", [ROW, 2, P], U8, ph)
            nl = sb("nl", [ROW, 2, P], F32, ph)
            pt = pb("prep_t", [128, 2, 512], ph)
            same_s = sb("same_s", [ROW, 2, P], F32, ph)
            nlast = sb("nlast", [ROW, 2, P], F32, ph)
            deg_l, fprod, bprod, rid_r, rid_m, rid_l = (
                sb(n, [ROW, 2, P], F32, ph) for n in ("deg_l", "fprod", "bprod", "rid_r", "rid_m", "rid_l"))
            no = sb("no", [ROW, P], F32, ph)
            ends = sb("ends", [1, 4, T], F32, ph)
            carry = sb("carry", [1, 2, T + 1], F32, ph)
            cin = sb("cin", [ROW, 2, 2], F32, ph)
            dlink2, dlink3 = sem("prep_link2", ph), sem("prep_link3", ph)
            half = lambda v: v.rearrange("(h q p) -> q h p", h=2, p=P)

            block = nc.Block()
            block.__enter__()

            @block.sync
            def _(sp):
                sp.wait_ge(filled, 1)
                sp.dma_start(ri[:, 0], half(src)).then_inc(loaded, 16)
                sp.dma_start(ri[:, 1], half(dst)).then_inc(loaded, 16)
                sp.dma_start(cols[:, 4], half(a["edge_weight"])).then_inc(loaded, 16)
                flat = dst.rearrange("(t p) -> t p", p=P)
                sp.dma_start(edge_i[1:ROW, 0, 0:1], flat[0:ROW - 1, P - 1:P], allow_slow_non_contiguous=True).then_inc(loaded, 16)
                sp.dma_start(edge_i[0:ROW, 1, 0:1], flat[ROW - 1:T - 1, P - 1:P], allow_slow_non_contiguous=True).then_inc(loaded, 16)
                sp.dma_start(edge_i[0:ROW, 0, 1:2], flat[1:ROW + 1, 0:1], allow_slow_non_contiguous=True).then_inc(loaded, 16)
                sp.dma_start(edge_i[0:ROW - 1, 1, 1:2], flat[ROW + 1:T, 0:1], allow_slow_non_contiguous=True).then_inc(loaded, 16)
                sp.wait_ge(row_ready, 1)
                sp.dma_start(half(same_row), same_f[:]).then_inc(stored, 16)
                sp.wait_ge(stored, 16)
                sp.dma_start(same_b[:], same_row.partition_broadcast(128)).then_inc(bcast, 16)
                sp.wait_ge(bcast, 16)

            @block.vector
            def _(dve):
                link = Links(dve, dlink)
                nc.vector.memset(edge_i[:], -1).then_inc(filled, 1)
                dve.wait_ge(filled, 1)
                dve.wait_ge(loaded, 7 * 16)
                nc.vector.tensor_copy(cols[:, 0], ri[:, 0])
                nc.vector.tensor_copy(rf[:, :, 0:1], edge_i[:, :, 0:1])
                nc.vector.tensor_copy(rf[:, :, P + 1:P + 2], edge_i[:, :, 1:2])
                nc.vector.tensor_copy(cols[:, 1], ri[:, 1])
                link(nc.vector.tensor_copy(rf[:, :, 1:P + 1], ri[:, 1]))
                nc.vector.memset(no[:], 0.0)
                nc.vector.tensor_tensor(same_s[:], rf[:, :, 1:P + 1], rf[:, :, 0:P], ALU.is_equal)
                nc.vector.tensor_tensor(nlast[:], rf[:, :, 1:P + 1], rf[:, :, 2:P + 2], ALU.is_equal)
                nc.vector.tensor_tensor(same_f[:], rf[:, :, 1:P + 1], rf[:, :, 0:P], ALU.is_equal).then_inc(row_ready, 1)
                link(nc.vector.tensor_tensor(nl[:], rf[:, :, 1:P + 1], rf[:, :, 2:P + 2], ALU.is_equal))
                nc.vector.tensor_scalar(cols[:, 3], nl[:], -1.0, 1.0, ALU.mult, ALU.add)
                link(nc.vector.tensor_scalar(nl[:], nl[:], float(FAR), None, ALU.mult))
                nc.vector.tensor_tensor(cols[:, 2], rf[:, :, 1:P + 1], nl[:], ALU.add).then_inc(row_ready, 1)
            block.__exit__(None, None, None)


            def ends_to_row(name, cols_of):
                with Phase(nc) as b:
                    there = sem(name, b)
                    blk = b.open()

                    @blk.tensor
                    def _(pe):
                        for n, col in enumerate(cols_of):
                            for h in range(2):
                                last = nc.tensor.transpose(pt[0:1, n // 2, (n % 2 * 2 + h) * ROW:(n % 2 * 2 + h + 1) * ROW],
                                                           col[:, h], ident[0:ROW, 0:ROW])
                        last.then_inc(there, 1)

                    @blk.vector
                    def _(dve):
                        dve.wait_ge(there, 1)
                        for n in range(len(cols_of)):
                            nc.vector.tensor_copy(ends[0:1, n], pt[0:1, n // 2, n % 2 * T:(n % 2 + 1) * T])

            def row_to_ends(name, n_rows):
                with Phase(nc) as b:
                    there = sem(name, b)
                    blk = b.open()

                    @blk.tensor
                    def _(pe):
                        for n in range(n_rows):
                            for h in range(2):
                                last = nc.tensor.transpose(pt[0:ROW, 0, n * 2 + h:n * 2 + h + 1],
                                                           carry[0:1, n, 1 + h * ROW:1 + (h + 1) * ROW], ident[0:1, 0:1])
                        last.then_inc(there, 1)

                    @blk.vector
                    def _(dve):
                        dve.wait_ge(there, 1)
                        nc.vector.tensor_copy(cin[:, 0:n_rows], pt[0:ROW, 0, 0:2 * n_rows].rearrange("r (n h) -> r n h", h=2))

            scan = nc.vector.tensor_tensor_scan
            with nc.Block() as b1:
                @b1.gpsimd
                def _(pool):
                    nc.gpsimd.iota(rid_r[:], pattern=[[ROW, 2], [T, P]], base=0, channel_multiplier=1,
                                   allow_small_or_imprecise_dtypes=True)

                @b1.vector
                def _(dve):
                    nc.vector.memset(carry[:], 0.0)
                    for h in range(2):
                        scan(deg_l[:, h], same_s[:, h], cols[:, 4, h], 0.0, ALU.mult, ALU.add)
                        scan(fprod[:, h], same_s[:, h], no[:], 1.0, ALU.mult, ALU.add)
                        scan(bprod[:, h, ::-1], nlast[:, h, ::-1], no[:], 1.0, ALU.mult, ALU.add)
            with nc.Block() as b2:
                @b2.vector
                def _(dve):
                    nc.vector.tensor_tensor(rid_m[:], rid_r[:], cols[:, 3], ALU.mult).then_inc(dlink2, 1)
                    dve.wait_ge(dlink2, 1)
                    for h in range(2):
                        scan(rid_l[:, h, ::-1], nlast[:, h, ::-1], rid_m[:, h, ::-1], 0.0, ALU.mult, ALU.add)
            ends_to_row("e1", [deg_l[:, :, P - 1:P], fprod[:, :, P - 1:P], rid_l[:, :, 0:1], bprod[:, :, 0:1]])
            with nc.Block() as b3:
                @b3.vector
                def _(dve):
                    scan(carry[0:1, 0, 2:T + 1], ends[0:1, 1, 0:T - 1], ends[0:1, 0, 0:T - 1], 0.0, ALU.mult, ALU.add)
                    scan(carry[0:1, 1, 1:T][:, ::-1], ends[0:1, 3, 1:T][:, ::-1], ends[0:1, 2, 1:T][:, ::-1], 0.0, ALU.mult, ALU.add)
            row_to_ends("e2", 2)
            with nc.Block() as b4:
                @b4.vector
                def _(dve):
                    link = Links(dve, dlink3)
                    for h in range(2):
                        nc.vector.scalar_tensor_tensor(cols[:, 6, h], bprod[:, h], cin[:, 1, h:h + 1], rid_l[:, h], ALU.mult, ALU.add)
                        link(nc.vector.scalar_tensor_tensor(deg_l[:, h], fprod[:, h], cin[:, 0, h:h + 1], deg_l[:, h], ALU.mult, ALU.add))
                    link(nc.vector.tensor_tensor(deg_l[:], deg_l[:], cols[:, 3], ALU.mult))
                    for h in range(2):
                        scan(cols[:, 5, h, ::-1], nlast[:, h, ::-1], deg_l[:, h, ::-1], 0.0, ALU.mult, ALU.add)
            ends_to_row("e3", [cols[:, 5, :, 0:1], bprod[:, :, 0:1]])
            with nc.Block() as b5:
                @b5.vector
                def _(dve):
                    scan(carry[0:1, 0, 1:T][:, ::-1], ends[0:1, 1, 1:T][:, ::-1], ends[0:1, 0, 1:T][:, ::-1], 0.0, ALU.mult, ALU.add)
                    nc.vector.memset(carry[0:1, 0, T:T + 1], 0.0)
            row_to_ends("e4", 1)
            with nc.Block() as b6:
                @b6.vector
                def _(dve):
                    for h in range(2):
                        nc.vector.scalar_tensor_tensor(cols[:, 5, h], bprod[:, h], cin[:, 0, h:h + 1], cols[:, 5, h], ALU.mult, ALU.add)

            with nc.Block() as b7:
                @b7.vector
                def _(dve):
                    for q, to in enumerate((src_f, dst_i, last_i, ew, dinv_t, slot_t)):
                        for h in range(2):
                            n = 2 * q + h
                            dve.wait_ge(turned, n + 1)
                            last = nc.vector.tensor_copy(to[0:P, h * ROW:(h + 1) * ROW], pt[0:P, h, 0:ROW])
                            if q == 0:
                                last = nc.vector.tensor_copy(src_i[0:P, h * ROW:(h + 1) * ROW], pt[0:P, h, 0:ROW])
                            last.then_inc(taken, 1)

                @b7.tensor
                def _(pe):
                    for q, col in enumerate((0, 1, 2, 4, 5, 6)):
                        for h in range(2):
                            n = 2 * q + h
                            if n >= 2:
                                pe.wait_ge(taken, n - 1)
                            nc.tensor.transpose(pt[0:P, h, 0:ROW], cols[:, col, h], ident[0:ROW, 0:ROW]).then_inc(turned, 1)

        with Phase(nc) as ph:
            staged_d = [sem(f"l0_staged_d{s}", ph) for s in range(2)]
            staged = [sem(f"l0_staged{s}", ph) for s in range(2)]
            rep_made = sem("l0_rep_made", ph)
            rep_turned = sem("l0_rep_turned", ph)
            eq_made = sem("l0_eq_made", ph)
            idx_made = sem("l0_idx_made", ph)
            scaled = sem("l0_scaled", ph)
            summed = sem("l0_summed", ph)
            sum_taken = sem("l0_sum_taken", ph)
            mult = sem("l0_mult", ph)
            row_made = sem("l0_row_made", ph)
            used = sem("l0_used", ph)
            dlink = sem("l0_link", ph)
            stg_d = sb("l0_stg_d", [128, 2, C], I32, ph)
            stg = sb("l0_stg", [128, 2, 2, C], I32, ph)
            stg_a = sb("l0_stg_a", [128, 2, C], I32, ph)
            xt = sb("l0_xt", [128, 2, C, F], F32, ph)
            rep = sb("l0_rep", [128, 2, C, P], F32, ph)
            eq = sb("l0_eq", [128, 2, C, P], F32, ph)
            eql = sb("l0_eql", [128, C, P], F32, ph)
            dup = sb("l0_dup", [128, C], F32, ph)
            tmp = sb("l0_tmp", [128, C], F32, ph)
            xe = sb("l0_xe", [128, 2, C, F], F32, ph)
            zt = sb("l0_zt", [F, 2, PG], F32, ph)
            zrows = sb("l0_zrows", [128, 2, C, F], F32, ph)
            p_rep = pb("l0_p_rep", [128, 2, 512], ph)
            p_sum = pb("l0_p_sum", [128, 2, 512], ph)
            p_row = pb("l0_p_row", [128, 2, 512], ph)
            block = ph.open()

            @block.sync
            def _(sp):
                sp.dma_start(stg_d[0:P, 0], dst_i[0:P, 0:C]).then_inc(staged_d[0], 16)
                with sp.Fori(0, NG // 2) as i:
                    for s in range(2):
                        g = i * 2 + s
                        sp.wait_ge(scaled, free1(g))
                        sp.sem_inc(sp_tick, 1)
                        sp.dma_start(stg_d[0:P, 1 - s], dst_i[0:P, bass.ds(g * C + C, C)]).then_inc(staged_d[1 - s], 16)
                        sp.wait_ge(used, free(g))
                        sp.sem_inc(sp_tick, 1)
                        sp.dma_start(stg[0:P, s, 0], last_i[0:P, bass.ds(g * C, C)]).then_inc(staged[s], 16)
                        sp.dma_start(stg[0:P, s, 1], rid_i[0:P, bass.ds(g * C, C)]).then_inc(staged[s], 16)

            @block.gpsimd
            def _(pool):
                bound = pool.to_reg(N - 1)
                credit(pool, used)

                def gather(s, c):
                    pool.indirect_dma_start(out=xt[0:P, s, c], out_offset=None, in_=x, in_offset=bass.IndirectOffsetOnAxis(
                        ap=stg_d[0:P, s, c:c + 1], axis=0)).then_inc(gathered[s], 16)

                pool.wait_ge(staged_d[0], 16)
                pool.sem_inc(pool_tick, 1)
                for c in range(C):
                    gather(0, c)
                with pool.Fori(0, NG // 2) as i:
                    for s in range(2):
                        g = i * 2 + s
                        pool.wait_ge(staged_d[1 - s], (i + 1 + s) * 16)
                        pool.wait_ge(scaled, free1(g))
                        pool.sem_inc(pool_tick, 1)
                        for c in range(C):
                            gather(1 - s, c)
                        pool.wait_ge(row_made, done(g))
                        pool.wait_ge(idx_made, done(g))
                        pool.wait_ge(staged[s], (i + 1) * 32)
                        pool.sem_inc(pool_tick, 1)
                        for c in range(C):
                            pool.indirect_dma_start(out=ytab, out_offset=bass.IndirectOffsetOnAxis(ap=stg_a[0:P, s, c:c + 1], axis=0),
                                                    in_=zrows[0:P, s, c], in_offset=None, compute_op=ALU.add).then_inc(added, 16)
                            pool.indirect_dma_start(out=slot_tab, out_offset=bass.IndirectOffsetOnAxis(ap=stg[0:P, s, 0, c:c + 1], axis=0),
                                                    in_=stg[0:P, s, 1, c:c + 1], in_offset=None, bounds_check=bound,
                                                    oob_is_err=False).then_inc(slotted, 16)
                            pool.wait_ge(added, g * C * 16 + c * 16 + 16)
                            pool.sem_inc(pool_tick, 1)
                        pool.wait_ge(slotted, g * C * 16 + C * 16)
                        pool.sem_inc(pool_tick, 1)
                        pool.sem_inc(used, 1)
                pool.wait_ge(gathered[0], (NG // 2 + 1) * C * 16)

            @block.vector
            def _(dve):
                link = Links(dve, dlink)
                credit(dve, rep_made, eq_made, idx_made, scaled)
                with dve.Fori(0, NG // 2) as i:
                    link.turn(i, 10)
                    for s in range(2):
                        g = i * 2 + s
                        mine = src_f[0:P, bass.ds(g * C, C)]
                        dve.wait_ge(rep_turned, free(g))
                        dve.sem_inc(dve_tick, 1)
                        nc.vector.tensor_scalar(rep[0:P, s], over(mine, P), 1.0, None, ALU.mult).then_inc(rep_made, 1)
                        dve.wait_ge(rep_turned, done(g))
                        dve.wait_ge(summed, free(g))
                        dve.sem_inc(dve_tick, 1)
                        pr = p_rep[0:P, s, 0:PG].rearrange("p (c q) -> p c q", c=C)
                        link(nc.vector.tensor_tensor(eq[0:P, s], pr, over(mine, P), ALU.is_equal))
                        link(nc.vector.tensor_tensor(eql[0:P], eq[0:P, s], lower[0:P, :].unsqueeze(1).broadcast_to([P, C, P]), ALU.mult))
                        dve.sem_inc(eq_made, 1)
                        nc.vector.tensor_scalar(tmp[0:P], mine, -1.0, trash[0:P, 0:1], ALU.mult, ALU.add)
                        link(nc.vector.reduce_sum(dup[0:P], eql[0:P], AX))
                        link(nc.vector.scalar_tensor_tensor(tmp[0:P], dup[0:P], 1.0, tmp[0:P], ALU.min, ALU.mult))
                        dve.wait_ge(used, free(g))
                        dve.sem_inc(dve_tick, 1)
                        link(nc.vector.tensor_tensor(stg_a[0:P, s], tmp[0:P], mine, ALU.add))
                        dve.sem_inc(idx_made, 1)
                        dve.wait_ge(gathered[s], (i + 1) * C * 16)
                        dve.sem_inc(dve_tick, 1)
                        nc.vector.tensor_tensor(xe[0:P, s], xt[0:P, s], over(ew[0:P, bass.ds(g * C, C)], F), ALU.mult).then_inc(scaled, 1)
                link.end(NG // 2)

            @block.tensor
            def _(pe):
                credit(pe, rep_turned, summed, mult)
                with pe.Fori(0, NG // 2) as i:
                    for s in range(2):
                        g = i * 2 + s
                        pe.wait_ge(rep_made, done(g))
                        pe.wait_ge(eq_made, free(g))
                        pe.sem_inc(pe_tick, 1)
                        for c in range(C):
                            last = nc.tensor.transpose(p_rep[0:P, s, c * P:(c + 1) * P], rep[0:P, s, c], ident[0:P, 0:P])
                        last.then_inc(rep_turned, 1)
                        pe.wait_ge(eq_made, done(g))
                        pe.wait_ge(scaled, done(g))
                        pe.wait_ge(sum_taken, free(g))
                        pe.sem_inc(pe_tick, 1)
                        for c in range(C):
                            last = nc.tensor.matmul(p_sum[0:F, s, c * P:(c + 1) * P], xe[0:P, s, c], eq[0:P, s, c], start=True, stop=True)
                        last.then_inc(summed, 1)
                        pe.wait_ge(sum_taken, done(g))
                        pe.wait_ge(row_made, free(g))
                        pe.sem_inc(pe_tick, 1)
                        for c in range(C):
                            last = nc.tensor.matmul(p_row[0:P, s, c * F:(c + 1) * F], zt[:, s, c * P:(c + 1) * P], w0[:], start=True, stop=True)
                        last.then_inc(mult, 1)

            @block.scalar
            def _(act):
                credit(act, sum_taken, row_made)
                with act.Fori(0, NG // 2) as i:
                    for s in range(2):
                        g = i * 2 + s
                        act.wait_ge(summed, done(g))
                        act.wait_ge(mult, free(g))
                        act.sem_inc(act_tick, 1)
                        nc.scalar.copy(zt[:, s], p_sum[0:F, s, 0:PG]).then_inc(sum_taken, 1)
                        act.wait_ge(mult, done(g))
                        act.wait_ge(used, free(g))
                        act.sem_inc(act_tick, 1)
                        nc.scalar.copy(zrows[0:P, s], p_row[0:P, s, 0:C * F].rearrange("p (c f) -> p c f", c=C)).then_inc(row_made, 1)

        g_base[0] += (NG // 2 + 1) * C * 16
        g_base[1] += NG // 2 * C * 16


        with Phase(nc) as ph:
            staged = [sem(f"l1_staged{s}", ph) for s in range(2)]
            stored = [sem(f"l1_stored{s}", ph) for s in range(2)]
            var_made, dev_made, read, rs_made, scanned, sums_made, xt_made = (
                sem(f"l1_{n}", ph) for n in ("var_made", "dev_made", "read", "rs_made", "scanned", "sums_made", "xt_made"))
            turned, backed, fm_turned, mult = (sem(f"l1_{n}", ph) for n in ("turned", "backed", "fm_turned", "mult"))
            fm_taken, used = sem("l1_fm_taken", ph), sem("l1_used", ph)
            dlink = sem("l1_link", ph)
            stg = sb("l1_stg", [128, 2, 2, C], I32, ph)
            gy = sb("l1_gy", [128, 2, 2 * C, F], F32, ph)
            gs = sb("l1_gs", [128, 2, C], I32, ph)
            cb = sb("l1_cb", [128, 2 * C, F], F32, ph)
            sq = sb("l1_sq", [128, 2 * C, F], F32, ph)
            sm = sb("l1_sm", [128, 2 * C], F32, ph)
            va = sb("l1_va", [128, 2 * C], F32, ph)
            sd = sb("l1_sd", [128, 2 * C], F32, ph)
            rc = sb("l1_rc", [128, 2 * C], F32, ph)
            rs = sb("l1_rs", [128, 2, C, SW], F32, ph)
            sc = sb("l1_sc", [SW, 2, PG], F32, ph)
            mrow = sb("l1_mrow", [128, 2, C, SW], F32, ph)
            xt = sb("l1_xt", [128, 2, C, 2 * F + 1], F32, ph)
            xf = sb("l1_xf", [2 * F + 1, 2, PG], F32, ph)
            u = sb("l1_u", [128, C, F], F32, ph)
            p_t = pb("l1_p_t", [128, 2, 512], ph)
            p_b = pb("l1_p_b", [128, 2, 512], ph)
            p_f = pb("l1_p_f", [128, 2, 512], ph)
            p_m = pb("l1_p_m", [128, 2, 512], ph)
            block = ph.open()

            @block.sync
            def _(sp):
                with sp.Fori(0, NG // 2) as i:
                    for s in range(2):
                        g = i * 2 + s
                        sp.wait_ge(read, free(g))
                        sp.sem_inc(sp_tick, 1)
                        sp.dma_start(stg[0:P, s, 0], src_i[0:P, bass.ds(g * C, C)]).then_inc(staged[s], 16)
                        sp.dma_start(stg[0:P, s, 1], dst_i[0:P, bass.ds(g * C, C)]).then_inc(staged[s], 16)

            @block.gpsimd
            def _(pool):
                with pool.Fori(0, NG // 2) as i:
                    for s in range(2):
                        g = i * 2 + s
                        pool.wait_ge(staged[s], (i + 1) * 32)
                        pool.wait_ge(read, free(g))
                        pool.sem_inc(pool_tick, 1)
                        for tab, to, k in ((ytab, gy[0:P, s, 0:C], 0), (ytab, gy[0:P, s, C:2 * C], 1),
                                           (slot_tab, gs[0:P, s].unsqueeze(2), 0)):
                            for c in range(C):
                                pool.indirect_dma_start(out=to[:, c], out_offset=None, in_=tab, in_offset=bass.IndirectOffsetOnAxis(
                                    ap=stg[0:P, s, k, c:c + 1], axis=0)).then_inc(gathered[s], 16)

            @block.vector
            def _(dve):
                link = Links(dve, dlink)
                credit(dve, var_made, read, rs_made, scanned, sums_made, xt_made)
                for s in range(2):
                    nc.vector.memset(rs[:, s, :, F:F + 1], 1.0)
                    nc.vector.memset(xt[:, s, :, 2 * F:2 * F + 1], 1.0)
                link(nc.vector.memset(sc[:, 1, PG - 1:PG], 0.0))
                link.base = 1
                with dve.Fori(0, NG // 2) as i:
                    link.turn(i, 2 * 13)
                    for s in range(2):
                        g = i * 2 + s
                        cols = bass.ds(g * C, C)
                        dve.wait_ge(gathered[s], (i + 1) * 3 * C * 16 + g_base[s])
                        dve.wait_ge(turned, free(g))
                        dve.wait_ge(fm_turned, free(g))
                        dve.sem_inc(dve_tick, 1)
                        nc.vector.tensor_scalar(slot_i[0:P, cols], gs[0:P, s], 0, None, ALU.add)
                        center(link, cb[0:P], sm[0:P], sq[0:P], va[0:P], gy[0:P, s]).then_inc(var_made, 1)
                        dve.sem_inc(read, 1)
                        dve.wait_ge(dev_made, i * 4 + 2 * s + 1)
                        dve.sem_inc(dve_tick, 1)
                        link(nc.vector.reciprocal(rc[0:P], sd[0:P]))
                        nc.vector.tensor_tensor(rs[0:P, s, :, 0:F], cb[0:P, 0:C], over(rc[0:P, 0:C], F), ALU.mult)
                        nc.vector.tensor_tensor(x2s[0:P, cols, :], cb[0:P, 0:C], over(rc[0:P, 0:C], F), ALU.mult)
                        nc.vector.tensor_tensor(xt[0:P, s, :, 0:F], cb[0:P, C:2 * C], over(rc[0:P, C:2 * C], F), ALU.mult)
                        nc.vector.tensor_scalar(rs[0:P, s, :, F + 1], ew[0:P, cols], 1.0, None, ALU.mult).then_inc(rs_made, 1)
                        dve.wait_ge(turned, done(g))
                        dve.wait_ge(backed, free(g))
                        dve.sem_inc(dve_tick, 1)
                        link(nc.vector.tensor_tensor_scan(sc[:, s], same_b[0:SW, bass.ds(g * PG, PG)], p_t[0:SW, s, 0:PG],
                                                          sc[:, 1 - s, PG - 1:PG], ALU.mult, ALU.add))
                        dve.sem_inc(scanned, 1)
                        dve.wait_ge(backed, done(g))
                        dve.wait_ge(stored[s], (i + 1) * 16)
                        dve.sem_inc(dve_tick, 1)
                        sums = p_b[0:P, s, 0:C * SW].rearrange("p (c f) -> p c f", c=C)
                        nc.vector.tensor_copy(mrow[0:P, s], sums).then_inc(sums_made, 1)
                        link(nc.vector.tensor_scalar(sm[0:P, 0:C], sums[:, :, F], 1.0, None, ALU.max))
                        link(nc.vector.reciprocal(rc[0:P, 0:C], sm[0:P, 0:C]))
                        nc.vector.tensor_tensor(xt[0:P, s, :, F:2 * F], sums[:, :, 0:F], over(rc[0:P, 0:C], F), ALU.mult).then_inc(xt_made, 1)
                        dve.wait_ge(mult, done(g))
                        dve.sem_inc(dve_tick, 1)
                        link(nc.vector.scalar_tensor_tensor(u[0:P], p_m[0:P, s, 0:C * F].rearrange("p (c f) -> p c f", c=C), 0.0,
                                                            xt[0:P, s, :, 0:F], ALU.max, ALU.add))
                        center(link, cb[0:P, 0:C], sm[0:P, 0:C], sq[0:P, 0:C], va[0:P, 0:C], u[0:P]).then_inc(var_made, 1)
                        dve.sem_inc(used, 1)
                        dve.wait_ge(dev_made, i * 4 + 2 * s + 2)
                        dve.sem_inc(dve_tick, 1)
                        link(nc.vector.reciprocal(rc[0:P, 0:C], sd[0:P, 0:C]))
                        link(nc.vector.tensor_tensor(x2t[0:P, cols, :], cb[0:P, 0:C], over(rc[0:P, 0:C], F), ALU.mult))
                link.end(NG // 2)

            @block.tensor
            def _(pe):
                credit(pe, turned, backed, fm_turned, mult)
                with pe.Fori(0, NG // 2) as i:
                    for s in range(2):
                        g = i * 2 + s
                        pe.wait_ge(rs_made, done(g))
                        pe.wait_ge(scanned, free(g))
                        pe.sem_inc(pe_tick, 1)
                        for c in range(C):
                            last = nc.tensor.transpose(p_t[0:SW, s, c * P:(c + 1) * P], rs[0:P, s, c], ident[0:P, 0:P])
                        last.then_inc(turned, 1)
                        pe.wait_ge(scanned, done(g))
                        pe.wait_ge(xt_made, free(g))
                        pe.sem_inc(pe_tick, 1)
                        for c in range(C):
                            last = nc.tensor.transpose(p_b[0:P, s, c * SW:(c + 1) * SW], sc[:, s, c * P:(c + 1) * P], ident[0:SW, 0:SW])
                        last.then_inc(backed, 1)
                        pe.wait_ge(xt_made, done(g))
                        pe.wait_ge(fm_taken, free(g))
                        pe.sem_inc(pe_tick, 1)
                        for c in range(C):
                            last = nc.tensor.transpose(p_f[0:2 * F + 1, s, c * P:(c + 1) * P], xt[0:P, s, c], ident[0:P, 0:P])
                        last.then_inc(fm_turned, 1)
                        pe.wait_ge(fm_taken, done(g))
                        pe.wait_ge(used, g + 1)
                        pe.sem_inc(pe_tick, 1)
                        for c in range(C):
                            last = nc.tensor.matmul(p_m[0:P, s, c * F:(c + 1) * F], xf[:, s, c * P:(c + 1) * P], w1e[:], start=True, stop=True)
                        last.then_inc(mult, 1)

            @block.scalar
            def _(act):
                credit(act, fm_taken)
                act.sem_inc(stored[0], 16)
                act.sem_inc(stored[1], 16)
                act.sem_inc(used, LEAD)
                with act.Fori(0, NG // 2) as i:
                    for s in range(2):
                        g = i * 2 + s
                        act.wait_ge(var_made, i * 4 + 2 * s + 1 + LEAD)
                        act.sem_inc(act_tick, 1)
                        deviation(sd[0:P], va[0:P]).then_inc(dev_made, 1)
                        act.wait_ge(sums_made, done(g))
                        act.sem_inc(act_tick, 1)
                        act.dma_start(rows(mtab, g), mrow[0:P, s]).then_inc(stored[s], 16)
                        act.wait_ge(fm_turned, done(g))
                        act.wait_ge(mult, free(g))
                        act.sem_inc(act_tick, 1)
                        nc.scalar.copy(xf[:, s], p_f[0:2 * F + 1, s, 0:PG]).then_inc(fm_taken, 1)
                        act.wait_ge(var_made, i * 4 + 2 * s + 2 + LEAD)
                        act.sem_inc(act_tick, 1)
                        deviation(sd[0:P, 0:C], va[0:P, 0:C]).then_inc(dev_made, 1)
                for s in range(2):
                    act.wait_ge(stored[s], (NG // 2 + 1) * 16)

        for s in range(2):
            g_base[s] += NG // 2 * 3 * C * 16
        with Phase(nc) as ph:
            staged = [sem(f"c_staged{s}", ph) for s in range(2)]
            var_made, dev_made, xt_made, fm_turned, fm_taken, mult, used = (
                sem(f"c_{n}", ph) for n in ("var_made", "dev_made", "xt_made", "fm_turned", "fm_taken", "mult", "used"))
            dlink = sem("c_link", ph)
            stg = sb("c_stg", [128, 2, C], I32, ph)
            gm = sb("c_gm", [128, 2, C, SW], F32, ph)
            cb = sb("c_cb", [128, C, F], F32, ph)
            sq = sb("c_sq", [128, C, F], F32, ph)
            sm, va, sd, rc = (sb(f"c_{n}", [128, C], F32, ph) for n in ("sm", "va", "sd", "rc"))
            xt = sb("c_xt", [128, 2, C, 2 * F + 1], F32, ph)
            xf = sb("c_xf", [2 * F + 1, 2, PG], F32, ph)
            u = sb("c_u", [128, C, F], F32, ph)
            p_f = pb("c_p_f", [128, 2, 512], ph)
            p_m = pb("c_p_m", [128, 2, 512], ph)
            block = ph.open()

            @block.sync
            def _(sp):
                with sp.Fori(0, NG // 2) as i:
                    for s in range(2):
                        g = i * 2 + s
                        sp.wait_ge(xt_made, free(g))
                        sp.sem_inc(sp_tick, 1)
                        sp.dma_start(stg[0:P, s], slot_i[0:P, bass.ds(g * C, C)]).then_inc(staged[s], 16)

            @block.gpsimd
            def _(pool):
                with pool.Fori(0, NG // 2) as i:
                    for s in range(2):
                        g = i * 2 + s
                        pool.wait_ge(staged[s], (i + 1) * 16)
                        pool.wait_ge(xt_made, free(g))
                        pool.sem_inc(pool_tick, 1)
                        for c in range(C):
                            pool.indirect_dma_start(out=gm[0:P, s, c], out_offset=None, in_=mtab, in_offset=bass.IndirectOffsetOnAxis(
                                ap=stg[0:P, s, c:c + 1], axis=0)).then_inc(gathered[s], 16)

            @block.vector
            def _(dve):
                link = Links(dve, dlink)
                credit(dve, var_made, xt_made, used)
                for s in range(2):
                    nc.vector.memset(xt[:, s, :, 2 * F:2 * F + 1], 1.0)
                with dve.Fori(0, NG // 2) as i:
                    link.turn(i, 2 * 8)
                    for s in range(2):
                        g = i * 2 + s
                        cols = bass.ds(g * C, C)
                        dve.wait_ge(gathered[s], (i + 1) * C * 16 + g_base[s])
                        dve.wait_ge(fm_turned, free(g))
                        dve.sem_inc(dve_tick, 1)
                        nc.vector.tensor_scalar(norm[0:P, cols], gm[0:P, s, :, F + 1], 1.0, None, ALU.mult)
                        nc.vector.tensor_scalar(xt[0:P, s, :, 0:F], x2s[0:P, cols, :], 1.0, None, ALU.mult)
                        link(nc.vector.tensor_scalar(sm[0:P], gm[0:P, s, :, F], 1.0, None, ALU.max))
                        link(nc.vector.reciprocal(rc[0:P], sm[0:P]))
                        nc.vector.tensor_tensor(xt[0:P, s, :, F:2 * F], gm[0:P, s, :, 0:F], over(rc[0:P], F), ALU.mult).then_inc(xt_made, 1)
                        dve.wait_ge(mult, done(g))
                        dve.sem_inc(dve_tick, 1)
                        link(nc.vector.scalar_tensor_tensor(u[0:P], p_m[0:P, s, 0:C * F].rearrange("p (c f) -> p c f", c=C), 0.0,
                                                            xt[0:P, s, :, 0:F], ALU.max, ALU.add))
                        center(link, cb[0:P], sm[0:P], sq[0:P], va[0:P], u[0:P]).then_inc(var_made, 1)
                        dve.sem_inc(used, 1)
                        dve.wait_ge(dev_made, g + 1)
                        dve.sem_inc(dve_tick, 1)
                        link(nc.vector.reciprocal(rc[0:P], sd[0:P]))
                        link(nc.vector.tensor_tensor(x2s[0:P, cols, :], cb[0:P], over(rc[0:P], F), ALU.mult))
                link.end(NG // 2)

            @block.tensor
            def _(pe):
                credit(pe, fm_turned, mult)
                with pe.Fori(0, NG // 2) as i:
                    for s in range(2):
                        g = i * 2 + s
                        pe.wait_ge(xt_made, done(g))
                        pe.wait_ge(fm_taken, free(g))
                        pe.sem_inc(pe_tick, 1)
                        for c in range(C):
                            last = nc.tensor.transpose(p_f[0:2 * F + 1, s, c * P:(c + 1) * P], xt[0:P, s, c], ident[0:P, 0:P])
                        last.then_inc(fm_turned, 1)
                        pe.wait_ge(fm_taken, done(g))
                        pe.wait_ge(used, free(g))
                        pe.sem_inc(pe_tick, 1)
                        for c in range(C):
                            last = nc.tensor.matmul(p_m[0:P, s, c * F:(c + 1) * F], xf[:, s, c * P:(c + 1) * P], w1e[:], start=True, stop=True)
                        last.then_inc(mult, 1)

            @block.scalar
            def _(act):
                credit(act, fm_taken)
                with act.Fori(0, NG // 2) as i:
                    for s in range(2):
                        g = i * 2 + s
                        act.wait_ge(fm_turned, done(g))
                        act.wait_ge(mult, free(g))
                        act.sem_inc(act_tick, 1)
                        nc.scalar.copy(xf[:, s], p_f[0:2 * F + 1, s, 0:PG]).then_inc(fm_taken, 1)
                        act.wait_ge(var_made, done(g))
                        act.sem_inc(act_tick, 1)
                        deviation(sd[0:P], va[0:P]).then_inc(dev_made, 1)

        for s in range(2):
            g_base[s] += NG // 2 * C * 16
        with Phase(nc) as ph:
            made, rooted = sem("n_made", ph), sem("n_rooted", ph)
            x2_stored = sem("x2_stored", ph)
            dlink = sem("n_link", ph)
            dg = sb("n_dg", [128, 2, T], F32, ph)
            some = sb("n_some", [128, 2, T], F32, ph)
            block = ph.open()

            @block.vector
            def _(dve):
                link = Links(dve, dlink)
                for k, d in enumerate((norm, dinv_t)):
                    nc.vector.tensor_scalar(some[0:P, k], d[0:P], 0.0, None, ALU.is_gt)
                    last = nc.vector.tensor_scalar(dg[0:P, k], d[0:P], TINY, None, ALU.max)
                last.then_inc(made, 1)
                dve.wait_ge(rooted, 1)
                link(nc.vector.reciprocal(dg[0:P], dg[0:P]))
                link(nc.vector.tensor_tensor(dg[0:P], dg[0:P], some[0:P], ALU.mult))
                link(nc.vector.tensor_tensor(norm[0:P], dg[0:P, 0], ew[0:P], ALU.mult))
                link(nc.vector.tensor_tensor(norm[0:P], norm[0:P], dg[0:P, 1], ALU.mult))

            @block.sync
            def _(sp):
                for tab, v in ((htab[2], x2t), (btab[2], x2s)):
                    sp.dma_start(tab.rearrange("(p t) f -> p t f", p=P)[:, :, F:2 * F], v[0:P]).then_inc(x2_stored, 16)
                sp.wait_ge(x2_stored, 32)

            @block.scalar
            def _(act):
                act.wait_ge(made, 1)
                nc.scalar.activation(dg[0:P], dg[0:P], ACT.Sqrt).then_inc(rooted, 1)

        hsp = sb("hsp", [128, T, H])
        for n in range(3):
            f, h, hp = fins[n], hs[n], hs[n - 1]
            W = K * h
            wide = F if n == 2 else 0
            with Phase(nc) as ph:
                nm = f"p{n}_"
                staged = [sem(f"{nm}staged{s}", ph) for s in range(2)]
                filled = [sem(f"{nm}filled{s}", ph) for s in range(2)]
                a_stored = [sem(f"{nm}a_stored{s}", ph) for s in range(2)]
                b_stored = [sem(f"{nm}b_stored{s}", ph) for s in range(2)]
                xs_made, turned, scanned, backed, a_taken, x_turned, x_taken, mult, relued, b_made = (
                    sem(nm + v, ph) for v in ("xs_made", "turned", "scanned", "backed", "a_taken", "x_turned",
                                              "x_taken", "mult", "relued", "b_made"))
                dlink = sem(nm + "link", ph)
                stg = sb(nm + "stg", [128, 2, C], I32, ph)
                gx = sb(nm + "gx", [128, 2, C, f], F32, ph)
                xs = sb(nm + "xs", [128, 2, C, f], F32, ph)
                xb = sb(nm + "xb", [128, 2, C, f + 1], F32, ph)
                sc = sb(nm + "sc", [f, 2, PG], F32, ph)
                arow = sb(nm + "arow", [128, 2, C, f], F32, ph)
                xf = sb(nm + "xf", [f + 1, 2, PG], F32, ph)
                hk = sb(nm + "hk", [128, 2, C, W], F32, ph)
                brow = sb(nm + "brow", [128, 2, C, h], F32, ph)
                p_t = pb(nm + "p_t", [128, 2, 512], ph)
                p_b = pb(nm + "p_b", [128, 512], ph)
                p_f = pb(nm + "p_f", [128, 512], ph)
                p_h = pb(nm + "p_h", [128, 2, 2, 512], ph)
                block = ph.open()

                @block.sync
                def _(sp):
                    if n == 0:
                        return
                    with sp.Fori(0, NG // 2) as i:
                        for s in range(2):
                            g = i * 2 + s
                            sp.wait_ge(xs_made, free(g))
                            sp.sem_inc(sp_tick, 1)
                            sp.dma_start(stg[0:P, s], slot_i[0:P, bass.ds(g * C, C)]).then_inc(staged[s], 16)
                            sp.dma_start(gx[0:P, s], rows(btab[n - 1], g)).then_inc(filled[s], 16)

                @block.gpsimd
                def _(pool):
                    if n == 0:
                        return
                    bound = pool.to_reg(E - 1)
                    with pool.Fori(0, NG // 2) as i:
                        for s in range(2):
                            pool.wait_ge(staged[s], (i + 1) * 16)
                            pool.wait_ge(filled[s], (i + 1) * 16)
                            pool.sem_inc(pool_tick, 1)
                            for c in range(C):
                                pool.indirect_dma_start(out=gx[0:P, s, c], out_offset=None, in_=htab[n - 1],
                                                        in_offset=bass.IndirectOffsetOnAxis(ap=stg[0:P, s, c:c + 1], axis=0),
                                                        bounds_check=bound, oob_is_err=False).then_inc(gathered[s], 16)

                @block.vector
                def _(dve):
                    link = Links(dve, dlink)
                    credit(dve, xs_made, scanned, b_made)
                    for s in range(2):
                        nc.vector.memset(xb[:, s, :, f:f + 1], 1.0)
                    link(nc.vector.memset(sc[:, 1, PG - 1:PG], 0.0))
                    link.base = 1
                    with dve.Fori(0, NG // 2) as i:
                        link.turn(i, 2 * 2)
                        for s in range(2):
                            g = i * 2 + s
                            cols = bass.ds(g * C, C)
                            dve.wait_ge(turned, free(g))
                            dve.wait_ge(x_turned, free(g))
                            dve.sem_inc(dve_tick, 1)
                            if n:
                                dve.wait_ge(gathered[s], (i + 1) * C * 16 + g_base[s])
                                dve.sem_inc(dve_tick, 1)
                            x_in = gx[0:P, s] if n else x2s[0:P, cols, :]
                            nm_b = over(norm[0:P, cols], f)
                            nc.vector.tensor_scalar(xb[0:P, s, :, 0:f], x_in, 1.0, None, ALU.mult)
                            if n:
                                nc.vector.tensor_tensor(hsp[0:P, cols, :], x_in, nm_b, ALU.mult)
                            nc.vector.tensor_tensor(xs[0:P, s], x_in, nm_b, ALU.mult).then_inc(xs_made, 1)
                            dve.wait_ge(turned, done(g))
                            dve.wait_ge(backed, free(g))
                            dve.sem_inc(dve_tick, 1)
                            link(nc.vector.tensor_tensor_scan(sc[:, s], same_b[0:f, bass.ds(g * PG, PG)], p_t[0:f, s, 0:PG],
                                                              sc[:, 1 - s, PG - 1:PG], ALU.mult, ALU.add))
                            dve.sem_inc(scanned, 1)
                            dve.wait_ge(relued, done(g))
                            dve.wait_ge(b_stored[s], (i + 1) * 16)
                            dve.sem_inc(dve_tick, 1)
                            link(nc.vector.tensor_tensor(brow[0:P, s], hk[0:P, s, :, 0:h], hk[0:P, s, :, h:2 * h], ALU.add))
                            nc.vector.tensor_tensor(brow[0:P, s], brow[0:P, s], hk[0:P, s, :, 2 * h:3 * h], ALU.add).then_inc(b_made, 1)
                    link.end(NG // 2)

                @block.tensor
                def _(pe):
                    credit(pe, turned, backed, x_turned, mult)
                    with pe.Fori(0, NG // 2) as i:
                        for s in range(2):
                            g = i * 2 + s
                            pe.wait_ge(xs_made, done(g))
                            pe.wait_ge(scanned, free(g))
                            pe.wait_ge(x_taken, free1(g))
                            pe.sem_inc(pe_tick, 1)
                            for c in range(C):
                                last = nc.tensor.transpose(p_t[0:f, s, c * P:(c + 1) * P], xs[0:P, s, c], ident[0:P, 0:P])
                            last.then_inc(turned, 1)
                            for c in range(C):
                                last = nc.tensor.transpose(p_f[0:f + 1, c * P:(c + 1) * P], xb[0:P, s, c], ident[0:P, 0:P])
                            last.then_inc(x_turned, 1)
                            pe.wait_ge(x_taken, done(g))
                            pe.wait_ge(relued, free(g))
                            pe.sem_inc(pe_tick, 1)
                            for c in range(C):
                                last = nc.tensor.matmul(p_h[0:P, s, c // 2, c % 2 * W:(c % 2 + 1) * W], xf[:, s, c * P:(c + 1) * P],
                                                        wroot1[n][:], start=True, stop=True)
                            last.then_inc(mult, 1)
                            pe.wait_ge(scanned, done(g))
                            pe.wait_ge(a_taken, free1(g))
                            pe.sem_inc(pe_tick, 1)
                            for c in range(C):
                                last = nc.tensor.transpose(p_b[0:P, c * f:(c + 1) * f], sc[:, s, c * P:(c + 1) * P], ident[0:f, 0:f])
                            last.then_inc(backed, 1)

                @block.scalar
                def _(act):
                    credit(act, a_taken, x_taken, relued)
                    for s in range(2):
                        act.sem_inc(a_stored[s], 16)
                        act.sem_inc(b_stored[s], 16)
                    with act.Fori(0, NG // 2) as i:
                        for s in range(2):
                            g = i * 2 + s
                            act.wait_ge(x_turned, done(g))
                            act.wait_ge(mult, free(g))
                            act.sem_inc(act_tick, 1)
                            nc.scalar.copy(xf[:, s], p_f[0:f + 1, 0:PG]).then_inc(x_taken, 1)
                            act.wait_ge(backed, done(g))
                            act.wait_ge(a_stored[s], (i + 1) * 16)
                            act.sem_inc(act_tick, 1)
                            nc.scalar.copy(arow[0:P, s], p_b[0:P, 0:C * f].rearrange("p (c f) -> p c f", c=C)).then_inc(a_taken, 1)
                            act.wait_ge(mult, done(g))
                            act.wait_ge(b_made, free(g))
                            act.wait_ge(a_taken, done(g))
                            act.sem_inc(act_tick, 1)
                            act.dma_start(rows(atab[n], g), arow[0:P, s]).then_inc(a_stored[s], 16)
                            nc.scalar.activation(hk[0:P, s].rearrange("p (b c) w -> p b (c w)", b=2), p_h[0:P, s, :, 0:2 * W],
                                                 ACT.Relu).then_inc(relued, 1)
                            act.wait_ge(b_made, done(g))
                            act.sem_inc(act_tick, 1)
                            act.dma_start(rows(btab[n], g)[:, :, 0:h], brow[0:P, s]).then_inc(b_stored[s], 16)
                    for s in range(2):
                        act.wait_ge(a_stored[s], (NG // 2 + 1) * 16)
                        act.wait_ge(b_stored[s], (NG // 2 + 1) * 16)

            if n:
                for s in range(2):
                    g_base[s] += NG // 2 * C * 16
            with Phase(nc) as ph:
                nm = f"e{n}_"
                M1 = 2 * h if h == H else W
                parts = [(0, M1)] + ([(M1, h)] if h == H else [])
                fx = (2 * F + 1) if n == 0 else f + 1
                staged = [sem(f"{nm}staged{s}", ph) for s in range(2)]
                t_loaded = [sem(f"{nm}t_loaded{s}", ph) for s in range(2)]
                h_stored = [sem(f"{nm}h_stored{s}", ph) for s in range(2)]
                xa_made, a_turned, t_turned, a_taken, t_taken, msg, relu0, scanned, mult, relued, h_made = (
                    sem(nm + v, ph) for v in ("xa_made", "a_turned", "t_turned", "a_taken", "t_taken", "msg", "relu0",
                                              "scanned", "mult", "relued", "h_made"))
                s_turned, s_taken = sem(nm + "s_turned", ph), sem(nm + "s_taken", ph)
                dlink = sem(nm + "link", ph)
                stg = sb(nm + "stg", [128, 2, C], I32, ph)
                ga = sb(nm + "ga", [128, 2, C, f], F32, ph)
                xa = sb(nm + "xa", [128, 2, C, fx], F32, ph)
                xh = sb(nm + "xh", [128, 2, C, f], F32, ph) if n else None
                xt = sb(nm + "xt", [128, 2, C, f + 1], F32, ph)
                fa = sb(nm + "fa", [fx, 2, PG], F32, ph)
                fh = sb(nm + "fh", [f, 2, PG], F32, ph) if n else None
                ft = sb(nm + "ft", [f + 1, 2, PG], F32, ph)
                m = [sb(f"{nm}m{k}", [w, PG], F32, ph) for k, (_, w) in enumerate(parts)]
                sc = [sb(f"{nm}sc{k}", [w, 2, PG], F32, ph) for k, (_, w) in enumerate(parts)]
                hk = sb(nm + "hk", [128, 2, C, W], F32, ph)
                hrow = sb(nm + "hrow", [128, 2, C, h], F32, ph)
                p_x = pb(nm + "p_x", [128, 2, 512], ph)
                p_o = [pb(f"{nm}p_o{k}", [128, 512], ph) for k in range(2)]
                p_h = pb(nm + "p_h", [128, 2, 2, 512], ph)
                block = ph.open()

                @block.sync
                def _(sp):
                    with sp.Fori(0, NG // 2) as i:
                        for s in range(2):
                            g = i * 2 + s
                            sp.wait_ge(xa_made, free(g))
                            sp.sem_inc(sp_tick, 1)
                            sp.dma_start(stg[0:P, s], slot_i[0:P, bass.ds(g * C, C)]).then_inc(staged[s], 16)
                            if n:
                                sp.wait_ge(t_turned, free(g))
                                sp.sem_inc(sp_tick, 1)
                                sp.dma_start(xt[0:P, s, :, 0:f], rows(htab[n - 1], g)).then_inc(t_loaded[s], 16)

                @block.gpsimd
                def _(pool):
                    with pool.Fori(0, NG // 2) as i:
                        for s in range(2):
                            g = i * 2 + s
                            pool.wait_ge(staged[s], (i + 1) * 16)
                            pool.wait_ge(xa_made, free(g))
                            pool.sem_inc(pool_tick, 1)
                            for c in range(C):
                                pool.indirect_dma_start(out=ga[0:P, s, c], out_offset=None, in_=atab[n],
                                                        in_offset=bass.IndirectOffsetOnAxis(ap=stg[0:P, s, c:c + 1], axis=0)
                                                        ).then_inc(gathered[s], 16)

                @block.vector
                def _(dve):
                    link = Links(dve, dlink)
                    credit(dve, xa_made, scanned, h_made)
                    for s in range(2):
                        nc.vector.memset(xt[:, s, :, f:f + 1], 1.0)
                    for k in range(len(parts)):
                        link(nc.vector.memset(sc[k][:, 1, PG - 1:PG], 0.0))
                    link.base = len(parts)
                    with dve.Fori(0, NG // 2) as i:
                        link.turn(i, 2 * (1 + len(parts)))
                        for s in range(2):
                            g = i * 2 + s
                            cols = bass.ds(g * C, C)
                            dve.wait_ge(gathered[s], (i + 1) * C * 16 + g_base[s])
                            dve.wait_ge(a_turned, free(g))
                            dve.sem_inc(dve_tick, 1)
                            if n:
                                dve.wait_ge(s_turned, free(g))
                                dve.sem_inc(dve_tick, 1)
                            else:
                                dve.wait_ge(t_turned, free(g))
                                dve.sem_inc(dve_tick, 1)
                            nm_b = norm[0:P, cols]
                            if n == 0:
                                nc.vector.tensor_tensor(xa[0:P, s, :, 0:F], x2s[0:P, cols, :], over(nm_b, F), ALU.mult)
                                nc.vector.tensor_scalar(xt[0:P, s, :, 0:F], x2t[0:P, cols, :], 1.0, None, ALU.mult)
                            else:
                                nc.vector.tensor_scalar(xh[0:P, s], hsp[0:P, cols, :], 1.0, None, ALU.mult)
                            nc.vector.tensor_scalar(xa[0:P, s, :, fx - 1], nm_b, 1.0, None, ALU.mult)
                            nc.vector.tensor_tensor(xa[0:P, s, :, fx - 1 - f:fx - 1], ga[0:P, s], over(nm_b, f), ALU.mult).then_inc(xa_made, 1)
                            dve.wait_ge(relu0, done(g))
                            dve.wait_ge(mult, free(g))
                            dve.sem_inc(dve_tick, 1)
                            for k, (_, w) in enumerate(parts):
                                link(nc.vector.tensor_tensor_scan(sc[k][:, s], same_b[0:w, bass.ds(g * PG, PG)], m[k][:],
                                                                  sc[k][:, 1 - s, PG - 1:PG], ALU.mult, ALU.add))
                            dve.sem_inc(scanned, 1)
                            dve.wait_ge(relued, done(g))
                            dve.wait_ge(h_stored[s], (i + 1) * 16)
                            dve.sem_inc(dve_tick, 1)
                            link(nc.vector.tensor_tensor(hrow[0:P, s], hk[0:P, s, :, 0:h], hk[0:P, s, :, h:2 * h], ALU.add))
                            nc.vector.tensor_tensor(hrow[0:P, s], hrow[0:P, s], hk[0:P, s, :, 2 * h:3 * h], ALU.add).then_inc(h_made, 1)
                    link.end(NG // 2)

                @block.tensor
                def _(pe):
                    credit(pe, a_turned, t_turned, s_turned, msg, mult)
                    with pe.Fori(0, NG // 2) as i:
                        for s in range(2):
                            g = i * 2 + s
                            pe.wait_ge(xa_made, done(g))
                            pe.wait_ge(a_taken, free1(g))
                            pe.sem_inc(pe_tick, 1)
                            for c in range(C):
                                last = nc.tensor.transpose(p_x[0:fx, 0, c * P:(c + 1) * P], xa[0:P, s, c], ident[0:P, 0:P])
                            last.then_inc(a_turned, 1)
                            if n:
                                pe.wait_ge(t_taken, free1(g))
                                pe.sem_inc(pe_tick, 1)
                                for c in range(C):
                                    last = nc.tensor.transpose(p_x[0:f, 1, c * P:(c + 1) * P], xh[0:P, s, c], ident[0:P, 0:P])
                                last.then_inc(s_turned, 1)
                                pe.wait_ge(s_taken, done(g))
                                pe.wait_ge(t_loaded[s], (i + 1) * 16)
                                pe.sem_inc(pe_tick, 1)
                            else:
                                pe.wait_ge(t_taken, free1(g))
                                pe.sem_inc(pe_tick, 1)
                            for c in range(C):
                                last = nc.tensor.transpose(p_x[0:f + 1, 1, c * P:(c + 1) * P], xt[0:P, s, c], ident[0:P, 0:P])
                            last.then_inc(t_turned, 1)
                            pe.wait_ge(a_taken, done(g))
                            pe.wait_ge(relu0, free1(g))
                            pe.sem_inc(pe_tick, 1)
                            for k, (o, w) in enumerate(parts):
                                if n:
                                    nc.tensor.matmul(p_o[k][0:w, 0:PG], wroot0[n][:, o:o + w], fh[:, s], start=True, stop=False)
                                last = nc.tensor.matmul(p_o[k][0:w, 0:PG], wbias[n][:, o:o + w], fa[:, s], start=(n == 0), stop=True)
                            last.then_inc(msg, 1)
                            pe.wait_ge(t_taken, done(g))
                            pe.wait_ge(scanned, done(g))
                            pe.wait_ge(relued, free(g))
                            pe.sem_inc(pe_tick, 1)
                            for c in range(C):
                                for k, (o, w) in enumerate(parts):
                                    to = p_h[0:P, s, c // 2, c % 2 * W + o:c % 2 * W + o + w]
                                    nc.tensor.matmul(to, ft[:, s, c * P:(c + 1) * P], wroot1[n][:, o:o + w], start=True, stop=False)
                                    last = nc.tensor.matmul(to, sc[k][:, s, c * P:(c + 1) * P], wblk[n][k][:], start=False, stop=True)
                            last.then_inc(mult, 1)

                @block.scalar
                def _(act):
                    credit(act, a_taken, t_taken, s_taken, relu0, relued)
                    for s in range(2):
                        act.sem_inc(h_stored[s], 16)
                    with act.Fori(0, NG // 2) as i:
                        for s in range(2):
                            g = i * 2 + s
                            act.wait_ge(a_turned, done(g))
                            act.wait_ge(msg, free(g))
                            act.sem_inc(act_tick, 1)
                            nc.scalar.copy(fa[:, s], p_x[0:fx, 0, 0:PG]).then_inc(a_taken, 1)
                            if n:
                                act.wait_ge(s_turned, done(g))
                                act.sem_inc(act_tick, 1)
                                nc.scalar.copy(fh[:, s], p_x[0:f, 1, 0:PG]).then_inc(s_taken, 1)
                            act.wait_ge(t_turned, done(g))
                            act.wait_ge(mult, free(g))
                            act.sem_inc(act_tick, 1)
                            nc.scalar.copy(ft[:, s], p_x[0:f + 1, 1, 0:PG]).then_inc(t_taken, 1)
                            act.wait_ge(msg, done(g))
                            act.wait_ge(scanned, free1(g))
                            act.sem_inc(act_tick, 1)
                            for k, (_, w) in enumerate(parts):
                                last = nc.scalar.activation(m[k][:], p_o[k][0:w, 0:PG], ACT.Relu)
                            last.then_inc(relu0, 1)
                            act.wait_ge(mult, done(g))
                            act.wait_ge(h_made, free(g))
                            act.sem_inc(act_tick, 1)
                            nc.scalar.activation(hk[0:P, s].rearrange("p (b c) w -> p b (c w)", b=2), p_h[0:P, s, :, 0:2 * W],
                                                 ACT.Relu).then_inc(relued, 1)
                            act.wait_ge(h_made, done(g))
                            act.sem_inc(act_tick, 1)
                            act.dma_start(rows(htab[n], g)[:, :, 0:h], hrow[0:P, s]).then_inc(h_stored[s], 16)
                    for s in range(2):
                        act.wait_ge(h_stored[s], (NG // 2 + 1) * 16)

            for s in range(2):
                g_base[s] += NG // 2 * C * 16
        with Phase(nc) as ph:
            loaded = [sem(f"d_loaded{s}", ph) for s in range(2)]
            stored = [sem(f"d_stored{s}", ph) for s in range(2)]
            em_made, turned, taken, mult, relued, summed, var_made, dev_made, read, out_made = (
                sem("d_" + v, ph) for v in ("em_made", "turned", "taken", "mult", "relued", "summed", "var_made",
                                            "dev_made", "read", "out_made"))
            dlink = sem("d_link", ph)
            R = SUB * C
            yt = sb("d_yt", [128, 2, R, F], F32, ph)
            sl = sb("d_sl", [128, 2, R], I32, ph)
            cb = sb("d_cb", [128, R, F], F32, ph)
            sq = sb("d_sq", [128, R, F], F32, ph)
            sm, va, sd, rc = (sb(f"d_{v}", [128, R], F32, ph) for v in ("sm", "va", "sd", "rc"))
            no_edge = sb("d_no_edge", [128, R], F32, ph)
            u = sb("d_u", [128, R, F], F32, ph)
            x1 = sb("d_x1", [128, R, F], F32, ph)
            x2 = sb("d_x2", [128, 2, R, F], F32, ph)
            h12 = [sb(f"d_h{k}", [128, R, H], F32, ph) for k in (1, 2)]
            h3 = sb("d_h3", [128, 2, R, F], F32, ph)
            hm = sb("d_hm", [128, R, F], F32, ph)
            acc = sb("d_acc", [128, 2, R, F], F32, ph)
            xf = [sb("d_xf0", [F + 1, SUB, PG], F32, ph), sb("d_xf1", [H + 1, SUB, PG], F32, ph)]
            hk = sb("d_hk", [128, 2, C, K * H], F32, ph)
            p_t = pb("d_p_t", [128, 2, 512], ph)
            p_m = pb("d_p_m", [128, 2, 2, 512], ph)
            block = ph.open()
            Q = 4 * SUB
            ems = (x1, x2, h12[0], h12[1])
            wts = (w1d, wroot1[0], wroot1[1], wroot1[2])

            @block.sync
            def _(sp):
                with sp.Fori(0, ND // 2) as i:
                    for s in range(2):
                        g = i * 2 + s
                        sp.wait_ge(read, free(g))
                        sp.sem_inc(sp_tick, 1)
                        sp.dma_start(yt[0:P, s], nodes(ytab, g)).then_inc(loaded[s], 16)
                        sp.dma_start(sl[0:P, s].unsqueeze(2), nodes(slot_tab, g)).then_inc(loaded[s], 16)

            @block.vector
            def _(dve):
                link = Links(dve, dlink)
                credit(dve, read, summed, out_made)
                nc.vector.memset(xf[0][F:F + 1], 1.0)
                nc.vector.memset(xf[1][H:H + 1], 1.0)
                link(nc.vector.memset(acc[:], 0.0))
                link.base = 1
                with dve.Fori(0, ND // 2) as i:
                    link.turn(i, 2 * (8 + 3 * SUB + 3))
                    for s in range(2):
                        g = i * 2 + s
                        dve.wait_ge(loaded[s], (i + 1) * 32)
                        dve.sem_inc(dve_tick, 1)
                        nc.vector.tensor_scalar(no_edge[0:P], sl[0:P, s], float(NIL), None, ALU.is_equal)
                        center(link, cb[0:P], sm[0:P], sq[0:P], va[0:P], yt[0:P, s]).then_inc(var_made, 1)
                        dve.sem_inc(read, 1)
                        dve.wait_ge(dev_made, g * 2 + 1)
                        dve.sem_inc(dve_tick, 1)
                        link(nc.vector.reciprocal(rc[0:P], sd[0:P]))
                        nc.vector.tensor_tensor(x1[0:P], cb[0:P], over(rc[0:P], F), ALU.mult).then_inc(em_made, SUB)
                        for j in range(SUB):
                            cs = slice(j * C, (j + 1) * C)
                            dve.wait_ge(relued, g * Q + j + 1 + LEAD)
                            dve.sem_inc(dve_tick, 1)
                            nc.vector.tensor_tensor(u[0:P, cs], hk[0:P, j % 2, :, 0:F], x1[0:P, cs], ALU.add).then_inc(summed, 1)
                        dve.wait_ge(summed, g * Q + SUB + LEAD)
                        dve.wait_ge(stored[s], (i + 1) * 32)
                        dve.sem_inc(dve_tick, 1)
                        center(link, cb[0:P], sm[0:P], sq[0:P], va[0:P], u[0:P]).then_inc(var_made, 1)
                        dve.wait_ge(dev_made, g * 2 + 2)
                        dve.sem_inc(dve_tick, 1)
                        link(nc.vector.reciprocal(rc[0:P], sd[0:P]))
                        nc.vector.tensor_tensor(x2[0:P, s], cb[0:P], over(rc[0:P], F), ALU.mult).then_inc(em_made, SUB)
                        for k in range(3):
                            h = hs[k]
                            to = h12[k] if k < 2 else h3[:, s]
                            for j in range(SUB):
                                cs = slice(j * C, (j + 1) * C)
                                dve.wait_ge(relued, g * Q + (k + 1) * SUB + j + 1 + LEAD)
                                dve.sem_inc(dve_tick, 1)
                                a3 = [hk[0:P, j % 2, :, b * h:(b + 1) * h] for b in range(3)]
                                link(nc.vector.tensor_tensor(to[0:P, cs], a3[0], a3[1], ALU.add))
                                last = nc.vector.tensor_tensor(to[0:P, cs], to[0:P, cs], a3[2], ALU.add)
                                last.then_inc(summed, 1)
                                if k < 2:
                                    dve.wait_ge(summed, g * Q + (k + 1) * SUB + j + 1 + LEAD)
                                    dve.sem_inc(em_made, 1)
                        dve.wait_ge(summed, g * Q + Q + LEAD)
                        dve.sem_inc(dve_tick, 1)
                        dve.sem_inc(out_made, 1)
                        link(nc.vector.tensor_tensor(hm[0:P], h3[0:P, s], over(no_edge[0:P], F), ALU.mult))
                        nc.vector.tensor_tensor(acc[0:P, 0], acc[0:P, 0], hm[0:P], ALU.add)
                        link(nc.vector.tensor_tensor(cb[0:P], hm[0:P], h3[0:P, s], ALU.mult))
                        link(nc.vector.tensor_tensor(acc[0:P, 1], acc[0:P, 1], cb[0:P], ALU.add))
                link.end(ND // 2)
                for k in range(2):
                    last = nc.vector.reduce_sum(stat[0:P, k], acc[0:P, k].rearrange("p n f -> p f n"), AX)

            @block.tensor
            def _(pe):
                credit(pe, turned, mult)

                def turn(g, s, q):
                    k, j = q // SUB, q % SUB
                    f = F if k < 2 else H
                    em = ems[k][:, s] if k == 1 else ems[k]
                    pe.wait_ge(em_made, g * Q + q + 1)
                    pe.wait_ge(taken, g * Q + q - 1 + LEAD)
                    pe.sem_inc(pe_tick, 1)
                    for c in range(C):
                        last = nc.tensor.transpose(p_t[0:f, j % 2, c * P:(c + 1) * P], em[0:P, j * C + c], ident[0:P, 0:P])
                    last.then_inc(turned, 1)

                def product(g, q):
                    k, j = q // SUB, q % SUB
                    W = F if k == 0 else K * hs[k - 1]
                    pe.wait_ge(taken, g * Q + q + 1 + LEAD)
                    pe.wait_ge(relued, g * Q + q - 1 + LEAD)
                    pe.sem_inc(pe_tick, 1)
                    for c in range(C):
                        last = nc.tensor.matmul(p_m[0:P, j % 2, c // 2, c % 2 * W:(c % 2 + 1) * W],
                                                xf[k // 2][:, j, c * P:(c + 1) * P], wts[k][:], start=True, stop=True)
                    last.then_inc(mult, 1)

                with pe.Fori(0, ND // 2) as i:
                    for s in range(2):
                        g = i * 2 + s
                        for k in range(4):
                            for j in range(SUB):
                                turn(g, s, k * SUB + j)
                                if j:
                                    product(g, k * SUB + j - 1)
                            product(g, k * SUB + SUB - 1)

            @block.scalar
            def _(act):
                credit(act, taken, relued)
                for s in range(2):
                    act.sem_inc(stored[s], 32)

                def take(g, q):
                    k, j = q // SUB, q % SUB
                    f = F if k < 2 else H
                    act.wait_ge(turned, g * Q + q + 1 + LEAD)
                    act.sem_inc(act_tick, 1)
                    nc.scalar.copy(xf[k // 2][0:f, j], p_t[0:f, j % 2, 0:PG]).then_inc(taken, 1)

                def relu(g, q):
                    k, j = q // SUB, q % SUB
                    W = F if k == 0 else K * hs[k - 1]
                    act.wait_ge(mult, g * Q + q + 1 + LEAD)
                    act.wait_ge(summed, g * Q + q - 1 + LEAD)
                    act.sem_inc(act_tick, 1)
                    nc.scalar.activation(hk[0:P, j % 2].rearrange("p (b c) w -> p b c w", b=2)[:, :, :, 0:W],
                                         p_m[0:P, j % 2, :, 0:2 * W].rearrange("p b (c w) -> p b c w", c=2), ACT.Relu).then_inc(relued, 1)

                with act.Fori(0, ND // 2) as i:
                    for s in range(2):
                        g = i * 2 + s
                        for k in range(4):
                            if k < 2:
                                act.wait_ge(var_made, g * 2 + k + 1)
                                act.sem_inc(act_tick, 1)
                                deviation(sd[0:P], va[0:P]).then_inc(dev_made, 1)
                            for j in range(SUB):
                                take(g, k * SUB + j)
                                if j:
                                    relu(g, k * SUB + j - 1)
                            relu(g, k * SUB + SUB - 1)
                        act.wait_ge(out_made, g + 1 + LEAD)
                        act.sem_inc(act_tick, 1)
                        act.dma_start(nodes(x2d, g), x2[0:P, s]).then_inc(stored[s], 16)
                        act.dma_start(nodes(h3d, g), h3[0:P, s]).then_inc(stored[s], 16)
                for s in range(2):
                    act.wait_ge(stored[s], (ND // 2 + 1) * 32)

        with Phase(nc) as ph:
            loaded, summed, dev, multd, dlink = (sem("b_" + v, ph) for v in ("loaded", "summed", "dev", "mult", "link"))
            h3t = sb("b_h3t", [128, T, F], F32, ph)
            last_m = sb("b_last_m", [128, T], F32, ph)
            part = sb("b_part", [128, 2, F], F32, ph)
            tot = sb("b_tot", [128, 2, F], F32, ph)
            p_s = pb("b_p_s", [128, 512], ph)
            block = ph.open()

            @block.sync
            def _(sp):
                sp.dma_start(h3t[0:P], htab[2].rearrange("(p t) f -> p t f", p=P)[:, :, 0:F]).then_inc(loaded, 16)

            @block.vector
            def _(dve):
                link = Links(dve, dlink)
                flat = lambda v: v.rearrange("p k f -> p (k f)")
                link(nc.vector.tensor_scalar(last_m[0:P], last_i[0:P], float(N), None, ALU.is_lt))
                dve.wait_ge(loaded, 16)
                link(nc.vector.tensor_tensor(hsp[0:P, :, 0:F], h3t[0:P], over(last_m[0:P], F), ALU.mult))
                link(nc.vector.tensor_tensor(hsp[0:P, :, F:2 * F], hsp[0:P, :, 0:F], h3t[0:P], ALU.mult))
                for k in range(2):
                    last = nc.vector.reduce_sum(part[0:P, k], hsp[0:P, :, k * F:(k + 1) * F].rearrange("p t f -> p f t"), AX)
                link(last)
                nc.vector.tensor_tensor(flat(part[0:P]), flat(part[0:P]), flat(stat[0:P]), ALU.add).then_inc(summed, 1)
                dve.wait_ge(multd, 1)
                link(nc.vector.tensor_scalar(flat(tot[:]), p_s[:, 0:2 * F], 1.0 / N, None, ALU.mult))
                link(nc.vector.tensor_tensor(part[:, 0], tot[:, 0], tot[:, 0], ALU.mult))
                link(nc.vector.tensor_tensor(tot[:, 1], tot[:, 1], part[:, 0], ALU.subtract))
                nc.vector.tensor_scalar(tot[:, 1], tot[:, 1], 0.0, None, ALU.max).then_inc(summed, 1)
                dve.wait_ge(dev, 1)
                link(nc.vector.reciprocal(part[:, 1], part[:, 1]))
                link(nc.vector.tensor_tensor(stat[:, 0], part[:, 1], gamma[:], ALU.mult))
                link(nc.vector.tensor_tensor(part[:, 0], stat[:, 0], tot[:, 0], ALU.mult))
                link(nc.vector.tensor_tensor(stat[:, 1], beta[:], part[:, 0], ALU.subtract))

            @block.tensor
            def _(pe):
                pe.wait_ge(summed, 1)
                nc.tensor.matmul(p_s[:, 0:2 * F], ones[0:P, :], part[0:P].rearrange("p k f -> p (k f)"), start=True, stop=True).then_inc(multd, 1)

            @block.scalar
            def _(act):
                act.wait_ge(summed, 2)
                nc.scalar.activation(part[:, 1], tot[:, 1], ACT.Sqrt, bias=epsc[:, 0:1]).then_inc(dev, 1)

        def bn(link, t, h, n):
            row = lambda k: stat[0:P, k].unsqueeze(1).broadcast_to([P, n, F])
            link(nc.vector.tensor_tensor(t, h, row(0), ALU.mult))
            link(nc.vector.tensor_tensor(t, t, row(1), ALU.add))

        with Phase(nc) as ph:
            loaded = [sem(f"f_loaded{s}", ph) for s in range(2)]
            stored = [sem(f"f_stored{s}", ph) for s in range(2)]
            var_made, dev_made, read, out_made, dlink = (sem("f_" + v, ph) for v in ("var_made", "dev_made", "read", "out_made", "link"))
            R = SUB * C
            xin = sb("f_xin", [128, 2, R, F], F32, ph)
            hin = sb("f_hin", [128, 2, R, F], F32, ph)
            cb = sb("f_cb", [128, R, F], F32, ph)
            sq = sb("f_sq", [128, R, F], F32, ph)
            sm, va, sd, rc = (sb(f"f_{v}", [128, R], F32, ph) for v in ("sm", "va", "sd", "rc"))
            u = sb("f_u", [128, R, F], F32, ph)
            xo = sb("f_xo", [128, 2, R, F], F32, ph)
            block = ph.open()

            @block.sync
            def _(sp):
                with sp.Fori(0, ND // 2) as i:
                    for s in range(2):
                        g = i * 2 + s
                        sp.wait_ge(read, free(g))
                        sp.sem_inc(sp_tick, 1)
                        sp.dma_start(xin[0:P, s], nodes(x2d, g)).then_inc(loaded[s], 16)
                        sp.dma_start(hin[0:P, s], nodes(h3d, g)).then_inc(loaded[s], 16)

            @block.vector
            def _(dve):
                link = Links(dve, dlink)
                credit(dve, read)
                with dve.Fori(0, ND // 2) as i:
                    link.turn(i, 2 * 12)
                    for s in range(2):
                        g = i * 2 + s
                        dve.wait_ge(loaded[s], (i + 1) * 32)
                        dve.sem_inc(dve_tick, 1)
                        bn(link, u[0:P], hin[0:P, s], R)
                        link(nc.vector.scalar_tensor_tensor(u[0:P], u[0:P], 0.0, xin[0:P, s], ALU.max, ALU.add))
                        dve.sem_inc(read, 1)
                        center(link, cb[0:P], sm[0:P], sq[0:P], va[0:P], u[0:P]).then_inc(var_made, 1)
                        dve.wait_ge(dev_made, g * 2 + 1)
                        dve.wait_ge(stored[s], (i + 1) * 16)
                        dve.sem_inc(dve_tick, 1)
                        link(nc.vector.reciprocal(rc[0:P], sd[0:P]))
                        link(nc.vector.tensor_tensor(u[0:P], cb[0:P], over(rc[0:P], F), ALU.mult))
                        center(link, cb[0:P], sm[0:P], sq[0:P], va[0:P], u[0:P]).then_inc(var_made, 1)
                        dve.wait_ge(dev_made, g * 2 + 2)
                        dve.sem_inc(dve_tick, 1)
                        link(nc.vector.reciprocal(rc[0:P], sd[0:P]))
                        nc.vector.tensor_tensor(xo[0:P, s], cb[0:P], over(rc[0:P], F), ALU.mult).then_inc(out_made, 1)
                link.end(ND // 2)

            @block.scalar
            def _(act):
                for s in range(2):
                    act.sem_inc(stored[s], 16)
                with act.Fori(0, ND // 2) as i:
                    for s in range(2):
                        g = i * 2 + s
                        for k in range(2):
                            act.wait_ge(var_made, g * 2 + k + 1)
                            act.sem_inc(act_tick, 1)
                            deviation(sd[0:P], va[0:P]).then_inc(dev_made, 1)
                        act.wait_ge(out_made, g + 1)
                        act.sem_inc(act_tick, 1)
                        act.dma_start(nodes(out, g), xo[0:P, s]).then_inc(stored[s], 16)
                for s in range(2):
                    act.wait_ge(stored[s], (ND // 2 + 1) * 16)

        s_base = T * 16
        with Phase(nc) as ph:
            staged = [sem(f"j_staged{s}", ph) for s in range(2)]
            filled = [sem(f"j_filled{s}", ph) for s in range(2)]
            attrs = [sem(f"j_attrs{s}", ph) for s in range(2)]
            (var_made, dev_made, x3_made, e_turned, e_taken, hid, h_taken, w_mult, w_used, out_sum, tanhed, f_made,
             f_turned, scanned, backed, u_made, x4_made, placed, read) = (
                sem("j_" + v, ph) for v in ("var_made", "dev_made", "x3_made", "e_turned", "e_taken", "hid", "h_taken",
                                            "w_mult", "w_used", "out_sum", "tanhed", "f_made", "f_turned", "scanned",
                                            "backed", "u_made", "x4_made", "placed", "read"))
            dlink = sem("j_link", ph)
            M2 = 2 * MUL
            gx = sb("j_gx", [128, 2, 2 * C, 2 * F], F32, ph)
            stg = sb("j_stg", [128, 2, 3, C], I32, ph)
            e3 = sb("j_e3", [128, 2, C, 3], F32, ph)
            e10 = sb("j_e10", [128, 2, C, 10], F32, ph)
            cb = sb("j_cb", [128, 2 * C, F], F32, ph)
            sq = sb("j_sq", [128, 2 * C, F], F32, ph)
            u = sb("j_u", [128, 2 * C, F], F32, ph)
            sm = sb("j_sm", [128, 2 * C], F32, ph)
            va = sb("j_va", [128, 2 * C], F32, ph)
            sd = sb("j_sd", [128, 2 * C], F32, ph)
            rc = sb("j_rc", [128, 2 * C], F32, ph)
            n2 = sb("j_n2", [128, C], F32, ph)
            nd = sb("j_nd", [128, C], F32, ph)
            nr = sb("j_nr", [128, C], F32, ph)
            e3q = sb("j_e3q", [128, C, 3], F32, ph)
            nv = sb("j_nv", [128, C, 3], F32, ph)
            x3 = sb("j_x3", [128, 2 * C, F], F32, ph)
            ad = sb("j_ad", [128, C, M2], F32, ph)
            xv = sb("j_xv", [128, C, 3, MUL], F32, ph)
            xn = sb("j_xn", [128, C, 3, MUL], F32, ph)
            ef = sb("j_ef", [10, 2, PG], F32, ph)
            hf = sb("j_hf", [MUL, 2, PG], F32, ph)
            pr1 = sb("j_pr1", [128, 2, 2, 12, M2], F32, ph)
            pr2 = sb("j_pr2", [128, 2, 3, MOUT, MUL], F32, ph)
            o1 = sb("j_o1", [128, C, 24], F32, ph)
            o3 = sb("j_o3", [128, C, 3, MOUT], F32, ph)
            th = sb("j_th", [128, C, MUL], F32, ph)
            ew2 = sb("j_ew2", [128, C], F32, ph)
            vv = sb("j_vv", [128, C, MOUT, 3], F32, ph)
            fr = sb("j_fr", [128, 2, C, F], F32, ph)
            sc = sb("j_sc", [F, 2, PG], F32, ph)
            x4 = sb("j_x4", [128, 2, C, F], F32, ph)
            p_e = pb("j_p_e", [128, 512], ph)
            p_h = pb("j_p_h", [128, 512], ph)
            p_w = pb("j_p_w", [128, 2, 2, 512], ph)
            p_f = pb("j_p_f", [128, 512], ph)
            p_b = pb("j_p_b", [128, 512], ph)
            block = ph.open()
            GAIN = 1.593
            WC = 2 * C

            @block.sync
            def _(sp):
                edges = lambda v, g: v.rearrange("(t p) f -> p t f", p=P)[:, bass.ds(g * C, C), :]
                with sp.Fori(0, NG // 2) as i:
                    for s in range(2):
                        g = i * 2 + s
                        sp.wait_ge(read, free(g))
                        sp.wait_ge(placed, g + 1)
                        sp.sem_inc(sp_tick, 1)
                        sp.dma_start(stg[0:P, s, 0], slot_i[0:P, bass.ds(g * C, C)]).then_inc(staged[s], 16)
                        sp.dma_start(stg[0:P, s, 1], slot_t[0:P, bass.ds(g * C, C)]).then_inc(staged[s], 16)
                        sp.dma_start(stg[0:P, s, 2], last_i[0:P, bass.ds(g * C, C)]).then_inc(staged[s], 16)
                        sp.dma_start(gx[0:P, s, 0:C], rows(btab[2], g)).then_inc(filled[s], 16)
                        sp.dma_start(e3[0:P, s], edges(a["edge_attr_3"], g)).then_inc(attrs[s], 16)
                        sp.dma_start(e10[0:P, s], edges(a["edge_attr_10"], g)).then_inc(attrs[s], 16)

            @block.gpsimd
            def _(pool):
                pool.sem_inc(placed, 1)

                def place(s):
                    for c in range(C):
                        pool.indirect_dma_start(out=out, out_offset=bass.IndirectOffsetOnAxis(ap=stg[0:P, s, 2, c:c + 1], axis=0),
                                                in_=x4[0:P, s, c], in_offset=None, bounds_check=b_n,
                                                oob_is_err=False).then_inc(slotted, 16)

                b_e, b_n = pool.to_reg(E - 1), pool.to_reg(N - 1)

                def gather(s):
                    for k in range(2):
                        for c in range(C):
                            pool.indirect_dma_start(out=gx[0:P, s, k * C + c], out_offset=None, in_=htab[2],
                                                    in_offset=bass.IndirectOffsetOnAxis(ap=stg[0:P, s, k, c:c + 1], axis=0),
                                                    bounds_check=b_e, oob_is_err=False).then_inc(gathered[s], 16)

                with pool.Fori(0, NG // 2) as i:
                    for s in range(2):
                        g = i * 2 + s
                        pool.wait_ge(staged[s], (i + 1) * 48)
                        pool.wait_ge(filled[s], (i + 1) * 16)
                        pool.sem_inc(pool_tick, 1)
                        gather(s)
                        pool.wait_ge(x4_made, g + LEAD)
                        pool.sem_inc(pool_tick, 1)
                        place(1 - s)
                        pool.wait_ge(slotted, g * C * 16 + C * 16 + s_base)
                        pool.sem_inc(pool_tick, 1)
                        pool.sem_inc(placed, 1)
                pool.wait_ge(x4_made, NG + LEAD)
                pool.sem_inc(pool_tick, 1)
                place(1)
                pool.wait_ge(slotted, (NG + 1) * C * 16 + s_base)

            @block.vector
            def _(dve):
                link = Links(dve, dlink)
                nc.vector.memset(stg[:, 1, 2], FAR)
                nc.vector.memset(x4[:, 1], 0.0)
                link(nc.vector.memset(sc[:, 1, PG - 1:PG], 0.0))
                link.base = 1
                credit(dve, read, w_used, scanned, x4_made, f_made, u_made)
                with dve.Fori(0, NG // 2) as i:
                    link.turn(i, 2 * 30)
                    for s in range(2):
                        g = i * 2 + s
                        cols = bass.ds(g * C, C)
                        dve.wait_ge(gathered[s], (i + 1) * 2 * C * 16 + g_base[s])
                        dve.wait_ge(attrs[s], (i + 1) * 32)
                        dve.sem_inc(dve_tick, 1)
                        bn(link, u[0:P], gx[0:P, s, :, 0:F], 2 * C)
                        link(nc.vector.scalar_tensor_tensor(u[0:P], u[0:P], 0.0, gx[0:P, s, :, F:2 * F], ALU.max, ALU.add))
                        link(nc.vector.tensor_tensor(e3q[0:P], e3[0:P, s], e3[0:P, s], ALU.mult))
                        nc.vector.reduce_sum(n2[0:P], e3q[0:P], AX)
                        center(link, cb[0:P], sm[0:P], sq[0:P], va[0:P], u[0:P]).then_inc(var_made, 1)
                        dve.wait_ge(dev_made, g * 2 + 1)
                        dve.sem_inc(dve_tick, 1)
                        nc.vector.reciprocal(nr[0:P], nd[0:P])
                        link(nc.vector.reciprocal(rc[0:P], sd[0:P]))
                        nc.vector.tensor_tensor(nv[0:P], e3[0:P, s], over(nr[0:P], 3), ALU.mult)
                        link(nc.vector.tensor_tensor(x3[0:P], cb[0:P], over(rc[0:P], F), ALU.mult))
                        dve.sem_inc(read, 1)
                        for k in range(2):
                            half = slice(k * 8, k * 8 + 8)
                            nc.vector.tensor_copy(ad[0:P, :, half], x3[0:P, k * C:(k + 1) * C, 0:8])
                            last = nc.vector.tensor_copy(xv[0:P, :, :, half], x3[0:P, k * C:(k + 1) * C, 8:F].rearrange("p c (u k) -> p c k u", k=3))
                        link(last)
                        link(nc.vector.tensor_tensor(xn[0:P], xv[0:P], over(nv[0:P], MUL), ALU.mult))
                        link(nc.vector.reduce_sum(ad[0:P, :, MUL:M2], xn[0:P].rearrange("p c k u -> p c u k"), AX))
                        for c in range(C):
                            b = c % 2
                            dve.wait_ge(w_mult, g * C + c + 1 + WC)
                            dve.sem_inc(dve_tick, 1)
                            nc.vector.tensor_tensor(pr1[0:P, b], p_w[0:P, b, :, 0:384].rearrange("p b (o u) -> p b o u", u=M2),
                                                    ad[0:P, c].unsqueeze(1).unsqueeze(1).broadcast_to([P, 2, 12, M2]), ALU.mult)
                            link(nc.vector.tensor_tensor(pr2[0:P, b],
                                                         p_w[0:P, b, 1, 384:512].rearrange("p (w u) -> p w u", u=MUL).unsqueeze(1).broadcast_to([P, 3, MOUT, MUL]),
                                                         xv[0:P, c].unsqueeze(2).broadcast_to([P, 3, MOUT, MUL]), ALU.mult))
                            dve.sem_inc(w_used, 1)
                            nc.vector.reduce_sum(o1[0:P, c], pr1[0:P, b].rearrange("p b o u -> p (b o) u"), AX)
                            link(nc.vector.reduce_sum(o3[0:P, c], pr2[0:P, b], AX))
                        dve.sem_inc(out_sum, 1)
                        link(nc.vector.tensor_tensor(vv[0:P], over(o1[0:P, :, MUL:24], 3), nv[0:P].unsqueeze(2).broadcast_to([P, C, MOUT, 3]), ALU.mult))
                        nc.vector.tensor_scalar(ew2[0:P], ew[0:P, cols], GAIN, None, ALU.mult)
                        link(nc.vector.tensor_tensor(vv[0:P], vv[0:P], o3[0:P].rearrange("p c k w -> p c w k"), ALU.add))
                        dve.wait_ge(tanhed, g + 1)
                        dve.wait_ge(f_turned, free(g))
                        dve.sem_inc(dve_tick, 1)
                        link(nc.vector.tensor_tensor(th[0:P], th[0:P], over(ew2[0:P], MUL), ALU.mult))
                        nc.vector.tensor_copy(fr[0:P, s, :, 0:MOUT], th[0:P, :, 0:MOUT])
                        nc.vector.tensor_tensor(fr[0:P, s, :, MOUT:F].rearrange("p c (w k) -> p c w k", k=3), vv[0:P],
                                                over(th[0:P, :, MOUT:MUL], 3), ALU.mult).then_inc(f_made, 1)
                        dve.wait_ge(f_turned, done(g))
                        dve.wait_ge(backed, free(g))
                        dve.sem_inc(dve_tick, 1)
                        link(nc.vector.tensor_tensor_scan(sc[:, s], same_b[0:F, bass.ds(g * PG, PG)], p_f[0:F, 0:PG],
                                                          sc[:, 1 - s, PG - 1:PG], ALU.mult, ALU.add))
                        dve.sem_inc(scanned, 1)
                        dve.wait_ge(backed, done(g))
                        dve.wait_ge(placed, g + 1)
                        dve.sem_inc(dve_tick, 1)
                        link(nc.vector.tensor_tensor(u[0:P, 0:C], p_b[0:P, 0:C * F].rearrange("p (c f) -> p c f", c=C), x3[0:P, C:2 * C], ALU.add))
                        dve.sem_inc(u_made, 1)
                        center(link, cb[0:P, 0:C], sm[0:P, 0:C], sq[0:P, 0:C], va[0:P, 0:C], u[0:P, 0:C]).then_inc(var_made, 1)
                        dve.wait_ge(dev_made, g * 2 + 2)
                        dve.sem_inc(dve_tick, 1)
                        link(nc.vector.reciprocal(rc[0:P, 0:C], sd[0:P, 0:C]))
                        link(nc.vector.tensor_tensor(x4[0:P, s], cb[0:P, 0:C], over(rc[0:P, 0:C], F), ALU.mult))
                        dve.sem_inc(x4_made, 1)
                link.end(NG // 2)

            @block.tensor
            def _(pe):
                credit(pe, e_turned, hid, f_turned, backed)
                pe.sem_inc(w_mult, WC)
                with pe.Fori(0, NG // 2) as i:
                    for s in range(2):
                        g = i * 2 + s
                        pe.wait_ge(attrs[s], (i + 1) * 32)
                        pe.wait_ge(e_taken, free1(g))
                        pe.sem_inc(pe_tick, 1)
                        for c in range(C):
                            last = nc.tensor.transpose(p_e[0:10, c * P:(c + 1) * P], e10[0:P, s, c], ident[0:P, 0:P])
                        last.then_inc(e_turned, 1)
                        pe.wait_ge(e_taken, done(g))
                        pe.wait_ge(h_taken, free1(g))
                        pe.sem_inc(pe_tick, 1)
                        nc.tensor.matmul(p_h[0:MUL, 0:PG], wl1[:], ef[:, s], start=True, stop=True).then_inc(hid, 1)
                        pe.wait_ge(h_taken, done(g))
                        pe.sem_inc(pe_tick, 1)
                        for c in range(C):
                            pe.wait_ge(w_used, g * C + c - 1 + LEAD)
                            pe.sem_inc(pe_tick, 1)
                            hc = hf[:, s, c * P:(c + 1) * P]
                            nc.tensor.matmul(p_w[0:P, c % 2, 0, 0:384], hc, wmix[:, 0:384], start=True, stop=True)
                            nc.tensor.matmul(p_w[0:P, c % 2, 1, 0:384], hc, wmix[:, 384:768], start=True, stop=True)
                            nc.tensor.matmul(p_w[0:P, c % 2, 1, 384:512], hc, wvec[:], start=True, stop=True).then_inc(w_mult, 1)
                        pe.wait_ge(f_made, done(g))
                        pe.wait_ge(scanned, free1(g))
                        pe.sem_inc(pe_tick, 1)
                        for c in range(C):
                            last = nc.tensor.transpose(p_f[0:F, c * P:(c + 1) * P], fr[0:P, s, c], ident[0:P, 0:P])
                        last.then_inc(f_turned, 1)
                        pe.wait_ge(scanned, done(g))
                        pe.wait_ge(u_made, free1(g))
                        pe.sem_inc(pe_tick, 1)
                        for c in range(C):
                            last = nc.tensor.transpose(p_b[0:P, c * F:(c + 1) * F], sc[:, s, c * P:(c + 1) * P], ident[0:F, 0:F])
                        last.then_inc(backed, 1)

            @block.scalar
            def _(act):
                credit(act, e_taken, h_taken)
                with act.Fori(0, NG // 2) as i:
                    for s in range(2):
                        g = i * 2 + s
                        act.wait_ge(e_turned, done(g))
                        act.wait_ge(hid, free(g))
                        act.sem_inc(act_tick, 1)
                        nc.scalar.copy(ef[:, s], p_e[0:10, 0:PG]).then_inc(e_taken, 1)
                        act.wait_ge(hid, done(g))
                        act.wait_ge(w_mult, g * C - C + WC)
                        act.sem_inc(act_tick, 1)
                        nc.scalar.activation(hf[:, s], p_h[0:MUL, 0:PG], ACT.Relu).then_inc(h_taken, 1)
                        act.wait_ge(var_made, g * 2 + 1)
                        act.sem_inc(act_tick, 1)
                        nc.scalar.activation(nd[0:P], n2[0:P], ACT.Sqrt)
                        deviation(sd[0:P], va[0:P]).then_inc(dev_made, 1)
                        act.wait_ge(out_sum, g + 1)
                        act.sem_inc(act_tick, 1)
                        nc.scalar.activation(th[0:P], o1[0:P, :, 0:MUL], ACT.Tanh).then_inc(tanhed, 1)
                        act.wait_ge(var_made, g * 2 + 2)
                        act.sem_inc(act_tick, 1)
                        deviation(sd[0:P, 0:C], va[0:P, 0:C]).then_inc(dev_made, 1)


def kernel(**inputs):
    import numpy as np
    import concourse.bacc as bacc
    from concourse.bass_utils import run_bass_kernel_spmd

    nc = bacc.Bacc("TRN2", target_bir_lowering=False, num_devices=1)
    arrays, args = {}, {}
    for name, value in inputs.items():
        value = np.ascontiguousarray(value)
        arrays["in_" + name] = value
        args[name] = nc.dram_tensor("in_" + name, value.shape, mybir.dt.from_np(value.dtype), kind="ExternalInput").ap()
    shape = inputs["x"].shape
    out = nc.dram_tensor("out_0", shape, F32, kind="ExternalOutput").ap()
    gnn_kernel(nc, args, out)
    return run_bass_kernel_spmd(nc, [arrays], core_ids=[0]).results[0]["out_0"]
```

```python
import concourse.bass as bass
from concourse import mybir
from contextlib import ExitStack

F32 = mybir.dt.float32
I32 = mybir.dt.int32
U8 = mybir.dt.uint8
ALU = mybir.AluOpType
ACT = mybir.ActivationFunctionType
AX = mybir.AxisListType.X

P = 125
C = 4
PG = P * C
LEAD = 2
FAR = 1 << 20
EPS = 1e-5


def over(ap, n):
    return ap.unsqueeze(ap.ndim).broadcast_to(list(ap.shape) + [n])


class Phase(ExitStack):

    def __init__(self, nc):
        super().__init__()
        self.nc, self.sems, self.blk = nc, [], None

    def open(self):
        self.blk = self.nc.Block()
        return self.blk.__enter__()

    def close_sems(self):
        with self.nc.Block() as block:
            @block.sync
            def _(sp):
                for s in self.sems:
                    sp.sem_clear(s)

    def __exit__(self, *error):
        if self.blk is not None:
            self.blk.__exit__(*error)
        if error[0] is None:
            self.close_sems()
        return super().__exit__(*error)


class Links:

    def __init__(self, eng, sem):
        self.eng, self.sem, self.base, self.n, self.i, self.per = eng, sem, 0, 0, 0, 0

    def turn(self, i, per):
        self.i, self.per, self.n = i, per, 0

    def __call__(self, ins):
        ins.then_inc(self.sem, 1)
        self.n += 1
        self.eng.wait_ge(self.sem, self.i * self.per + self.base + self.n)

    def end(self, turns):
        assert self.n == self.per, (self.n, self.per)
        self.base += turns * self.per
        self.i = self.per = self.n = 0


def skewed(eng, groups, body, link=None, links=None):
    def alone(g, new, old, more):
        if link is not None:
            link.turn(0, links(new, old, more))
        body(g, g % 2, g // 2, new, old, more)
        if link is not None:
            link.end(1)

    turns = groups // 2 - 1
    alone(0, True, False, True)
    with eng.Fori(0, turns) as i:
        if link is not None:
            link.turn(i, 2 * links(True, True, True))
        body(i * 2 + 1, 1, i, True, True, True)
        body(i * 2 + 2, 0, i + 1, True, True, True)
        if link is not None:
            link.end(turns)
    alone(groups - 1, True, True, False)
    alone(groups, False, True, False)


def gnn_kernel(nc, a, out):
    x = a["x"]
    N, F = x.shape
    E = a["src"].shape[0]
    T = E // P
    NG = T // C
    H = a["L2_gnn_c1_init"].shape[2]
    K = a["L2_gnn_c1_init"].shape[0]
    NIL = E
    SW = F + 2
    ROW = T // 2
    SUB = 4
    ND = N // (PG * SUB)
    NPP = N // P // ND
    TINY = 1e-30
    MUL, MOUT, PATHS = 16, 8, 7

    ctx = ExitStack()

    with ctx:
        def sb(name, shape, dt=F32, c=ctx):
            return c.enter_context(nc.sbuf_tensor(name, shape, dt))

        def pb(name, shape, c):
            return c.enter_context(nc.psum_tensor(name, shape, F32))

        def sem(name, c=ctx):
            s = c.enter_context(nc.semaphore(name))
            if c is not ctx:
                c.sems.append(s)
            return s

        def dram(name, shape, dt=F32):
            return nc.dram_tensor(name, shape, dt, kind="Internal").ap()

        ytab = dram("ytab", [N + P, F])
        slot_tab = dram("slot_tab", [N, 1], I32)
        same_row = dram("same_row", [E], U8)
        mtab = dram("mtab", [E + 1, SW])
        atab = [dram("a1tab", [E + 1, F]), dram("a2tab", [E + 1, H]), dram("a3tab", [E + 1, H])]
        htab = [dram("h1tab", [E, H]), dram("h2tab", [E, H]), dram("xhtab", [E, 2 * F])]
        btab = [dram("b1tab", [E, H]), dram("b2tab", [E, H]), dram("xbtab", [E, 2 * F])]
        x2d = dram("x2d", [N, F])
        h3d = dram("h3d", [N, F])

        def rows(tab, g, n=C):
            return tab[0:E, :].rearrange("(p t) f -> p t f", p=P)[:, bass.ds(g * C, n), :]

        def nodes(tab, g):
            return tab[0:N, :].rearrange("(g p n) f -> g p n f", g=ND, p=P)[bass.ds(g, 1)].rearrange("g p n f -> p (g n) f")

        fields = ("src", "dst", "edge_weight", "edge_attr_10", "edge_attr_3")
        wide = [1, 1, 1, 10, 3]
        by_dst = [dram("by_dst_" + n, [E, w], a[n].dtype) for n, w in zip(fields, wide)]
        given = [a[n].rearrange("(e o) -> e o", o=1) if w == 1 else a[n] for n, w in zip(fields, wide)]
        src, dst, weight, attr10, attr3 = (v.rearrange("e o -> (e o)") if w == 1 else v for v, w in zip(by_dst, wide))

        pool_tick, act_tick, dve_tick, pe_tick, sp_tick = (sem(f"{e}_tick") for e in ("pool", "act", "dve", "pe", "sp"))

        gathered = [sem(f"gathered{s}") for s in range(2)]
        added, slotted = sem("added"), sem("slotted")
        g_base = [0, 0]

        def done(g):
            return g + 1 + LEAD

        def free(g):
            return g - 1 + LEAD

        def free1(g):
            return g + LEAD

        def credit(eng, *sems):
            for s in sems:
                eng.sem_inc(s, LEAD)

        unsorted = sb("unsorted", [1, 1], I32)
        with Phase(nc) as ph:
            copied, loaded, cleared, checked, joined = (sem("o_" + v, ph) for v in ("copied", "loaded", "cleared", "checked", "joined"))
            dlink = sem("o_link", ph)
            now = sb("o_now", [ROW, 2, P], I32, ph)
            near = sb("o_near", [ROW, 2, P], F32, ph)
            edge = sb("o_edge", [ROW, 2], I32, ph)
            some = sb("o_some", [ROW, 2], F32, ph)
            one = sb("o_one", [ROW, 1], F32, ph)
            p_c = pb("o_p_c", [128, 512], ph)
            block = ph.open()
            came = a["dst"]

            @block.sync
            def _(sp):
                for to, of, w in zip(by_dst, given, wide):
                    sp.dma_start(to.rearrange("(p t) w -> p (t w)", p=P), of.rearrange("(p t) w -> p (t w)", p=P)).then_inc(copied, 16)
                sp.wait_ge(cleared, 1)
                flat = came.rearrange("(t p) -> t p", p=P)
                sp.dma_start(now[:], came.rearrange("(h q p) -> q h p", h=2, p=P)).then_inc(loaded, 16)
                sp.dma_start(edge[1:ROW, 0:1], flat[0:ROW - 1, P - 1:P], allow_slow_non_contiguous=True).then_inc(loaded, 16)
                sp.dma_start(edge[0:ROW, 1:2], flat[ROW - 1:T - 1, P - 1:P], allow_slow_non_contiguous=True).then_inc(loaded, 16)
                sp.wait_ge(copied, 16 * len(by_dst))

            @block.vector
            def _(dve):
                link = Links(dve, dlink)
                nc.vector.memset(one[:], 1.0)
                nc.vector.memset(edge[:], -1).then_inc(cleared, 1)
                dve.wait_ge(loaded, 48)
                nc.vector.tensor_tensor(near[:, :, 0], now[:, :, 0], edge[:], ALU.is_lt)
                link(nc.vector.tensor_tensor(near[:, :, 1:P], now[:, :, 1:P], now[:, :, 0:P - 1], ALU.is_lt))
                link(nc.vector.reduce_sum(some[:], near[:], AX))
                nc.vector.tensor_tensor(some[:, 0:1], some[:, 0:1], some[:, 1:2], ALU.add).then_inc(checked, 1)
                dve.wait_ge(joined, 1)
                nc.vector.tensor_scalar(unsorted[:], p_c[0:1, 0:1], 0.0, None, ALU.is_gt)

            @block.tensor
            def _(pe):
                pe.wait_ge(checked, 1)
                nc.tensor.matmul(p_c[0:1, 0:1], some[:, 0:1], one[:], start=True, stop=True).then_inc(joined, 1)

        placed_rows = sem("placed_rows")
        with Phase(nc) as ph:
            loaded, made, ranked, staged, moved = (sem("r_" + v, ph) for v in ("loaded", "made", "ranked", "staged", "moved"))
            dlink = sem("r_link", ph)
            PART = E // 10
            all_dst = sb("r_all_dst", [128, E], I32, ph)
            cols = [sb(f"r_col{k}", [128, T, w], a[n].dtype, ph) for k, (n, w) in enumerate(zip(fields, wide))]
            at = sb("r_at", [128, PART], F32, ph)
            tile0 = sb("r_tile0", [128, T], F32, ph)
            part0 = sb("r_part0", [128, 10], F32, ph)
            mine = sb("r_mine", [128, 10], F32, ph)
            dcol = sb("r_dcol", [128, T], F32, ph)
            lower_at = sb("r_lower_at", [128, PART], F32, ph)
            sums = sb("r_sums", [128, 10], F32, ph)
            rank_i = sb("r_rank_i", [128, T], I32, ph)
            s_rank = sb("r_s_rank", [128, 1], I32, ph)
            s_row = [sb(f"r_s_row{k}", [128, w], a[n].dtype, ph) for k, (n, w) in enumerate(zip(fields, wide))]
            block = ph.open()

            @block.sync
            def _(sp):
                with sp.If(sp.value_load(unsorted[0:1, 0:1]) > 0):
                    sp.dma_start(all_dst[:], a["dst"].partition_broadcast(128)).then_inc(loaded, 16)
                    for to, of in zip(cols, given):
                        sp.dma_start(to[0:P], of.rearrange("(t p) w -> p t w", p=P), allow_slow_non_contiguous=True).then_inc(loaded, 16)
                    with sp.Fori(0, T) as t:
                        sp.wait_ge(ranked, t + 1)
                        sp.wait_ge(moved, t + 1)
                        sp.sem_inc(sp_tick, 1)
                        sp.dma_start(s_rank[0:P], rank_i[0:P, bass.ds(t, 1)]).then_inc(staged, 16)
                        for to, of in zip(s_row, cols):
                            sp.dma_start(to[0:P].unsqueeze(1), of[0:P, bass.ds(t, 1)]).then_inc(staged, 16)

            @block.gpsimd
            def _(pool):
                with pool.If(pool.value_load(unsorted[0:1, 0:1]) > 0):
                    nc.gpsimd.iota(at[:], pattern=[[1, PART]], base=0, channel_multiplier=0, allow_small_or_imprecise_dtypes=True)
                    nc.gpsimd.iota(tile0[:], pattern=[[P, T]], base=0, channel_multiplier=0, allow_small_or_imprecise_dtypes=True)
                    nc.gpsimd.iota(part0[:], pattern=[[-PART, 10]], base=0, channel_multiplier=1,
                                   allow_small_or_imprecise_dtypes=True).then_inc(made, 1)
                    pool.sem_inc(moved, 1)
                    with pool.Fori(0, T) as t:
                        pool.wait_ge(staged, (t + 1) * 16 * 6)
                        pool.sem_inc(pool_tick, 1)
                        for to, of in zip(by_dst, s_row):
                            pool.indirect_dma_start(out=to, out_offset=bass.IndirectOffsetOnAxis(ap=s_rank[0:P, 0:1], axis=0),
                                                    in_=of[0:P], in_offset=None).then_inc(placed_rows, 16)
                        pool.wait_ge(placed_rows, (t + 1) * 16 * 5)
                        pool.sem_inc(moved, 1)

            @block.vector
            def _(dve):
                with dve.If(dve.value_load(unsorted[0:1, 0:1]) > 0):
                    link = Links(dve, dlink)
                    dve.wait_ge(loaded, 16 * 6)
                    dve.wait_ge(made, 1)
                    link(nc.vector.tensor_copy(dcol[0:P], cols[1][0:P, :, 0]))
                    link.base = 1
                    with dve.Fori(0, T) as t:
                        link.turn(t, 4 * 10 + 3)
                        link(nc.vector.tensor_scalar(mine[0:P], part0[0:P], tile0[0:P, bass.ds(t, 1)], None, ALU.add))
                        own = dcol[0:P, bass.ds(t, 1)]
                        for q in range(10):
                            part = all_dst[0:P, q * PART:(q + 1) * PART]
                            link(nc.vector.tensor_scalar(lower_at[0:P], at[0:P], mine[0:P, q:q + 1], None, ALU.is_lt))
                            link(nc.vector.scalar_tensor_tensor(lower_at[0:P], part, own, lower_at[0:P], ALU.is_equal, ALU.mult))
                            link(nc.vector.scalar_tensor_tensor(lower_at[0:P], part, own, lower_at[0:P], ALU.is_lt, ALU.add))
                            link(nc.vector.reduce_sum(sums[0:P, q:q + 1], lower_at[0:P], AX))
                        link(nc.vector.reduce_sum(mine[0:P, 0:1], sums[0:P], AX))
                        link(nc.vector.tensor_scalar(rank_i[0:P, bass.ds(t, 1)], mine[0:P, 0:1], 0.0, None, ALU.add))
                        dve.sem_inc(ranked, 1)
                    link.end(T)

        ident = sb("ident", [128, 128])
        ones = sb("ones", [128, 128])
        lower = sb("lower", [128, P])
        trash = sb("trash", [128, 1])
        epsc = sb("epsc", [128, 1])
        zero = sb("zero", [128, 1])
        src_i = sb("src_i", [128, T], I32)
        dst_i = sb("dst_i", [128, T + C], I32)
        last_i = sb("last_i", [128, T], I32)
        rid_i = sb("rid_i", [128, T], I32)
        slot_i = sb("slot_i", [128, T], I32)
        slot_t = sb("slot_t", [128, T], I32)
        src_f = sb("src_f", [128, T])
        ew = sb("ew", [128, T])
        norm = sb("norm", [128, T])
        dinv_t = sb("dinv_t", [128, T])
        same_b = sb("same_b", [128, E], U8)
        stat = sb("stat", [128, 2, F])
        w0 = sb("w0", [F, F])
        w1e = sb("w1e", [2 * F + 1, F])
        w1d = sb("w1d", [F + 1, F])
        fins, hs = [F, H, H], [H, H, F]
        wbias = []
        wroot0 = []
        wroot1 = []
        wblk = []
        for n in range(3):
            k0 = 2 * F + 1 if n == 0 else H + 1
            wbias.append(sb(f"wbias{n}", [k0, K * hs[n]]))
            wroot0.append(None if n == 0 else sb(f"wroot0_{n}", [H, K * hs[n]]))
            wroot1.append(sb(f"wroot1_{n}", [fins[n] + 1, K * hs[n]]))
            wblk.append([sb(f"wblka{n}", [128 if hs[n] == H else K * F, 2 * H if hs[n] == H else K * F]),
                         sb(f"wblkb{n}", [H, H]) if hs[n] == H else None])
        wl1 = sb("wl1", [10, MUL])
        wl2 = sb("wl2", [MUL, PATHS * MUL * MOUT])
        wmix = sb("wmix", [MUL, 3 * MOUT * 2 * MUL])
        wvec = sb("wvec", [MUL, MOUT * MUL])
        gamma = sb("gamma", [128, F])
        beta = sb("beta", [128, F])
        x2s = sb("x2s", [128, T, F])
        x2t = sb("x2t", [128, T, F])

        def center(link, c, sm, sq, v, x):
            link(nc.vector.reduce_sum(sm, x, AX))
            link(nc.vector.scalar_tensor_tensor(c, over(sm, F), -1.0 / F, x, ALU.mult, ALU.add))
            link(nc.vector.tensor_tensor(sq, c, c, ALU.mult))
            return nc.vector.reduce_sum(v, sq, AX)

        def deviation(sd, v):
            return nc.scalar.activation(sd, v, ACT.Sqrt, bias=epsc[0:P, 0:1], scale=1.0 / F)

        with Phase(nc) as ph:
            loaded = sem("loaded", ph)
            made = sem("made", ph)
            zeroed = sem("zeroed", ph)
            init_done = sem("init_done", ph)
            nils = sb("nils", [P, N // P], I32, ph)
            zrow = sb("zrow", [128, H], F32, ph)
            block = ph.open()
            n_loads = [0]

            @block.vector
            def _(dve):
                nc.vector.memset(ones[:], 1.0)
                nc.vector.memset(epsc[:], EPS)
                nc.vector.memset(zero[:], 0.0)
                nc.vector.memset(dst_i[:], 0)
                nc.vector.memset(stat[:], 0.0)
                nc.vector.memset(zrow[:], 0.0)
                nc.vector.memset(nils[:], NIL)
                for n in range(3):
                    nc.vector.memset(wblk[n][0][:], 0.0)
                nc.vector.memset(w0[:], 0.0).then_inc(zeroed, 1)

            @block.gpsimd
            def _(pool):
                nc.gpsimd.memset(ident[:], 0.0).then_inc(made, 1)
                nc.gpsimd.memset(lower[:], 0.0).then_inc(made, 1)
                pool.wait_ge(made, 2)
                nc.gpsimd.affine_select(out=ident[:], in_=ident[:], compare_op=ALU.not_equal, fill=1.0, base=0,
                                        pattern=[[-1, 128]], channel_multiplier=1)
                nc.gpsimd.affine_select(out=lower[:], in_=lower[:], compare_op=ALU.is_ge, fill=1.0, base=0,
                                        pattern=[[1, P]], channel_multiplier=-1)
                nc.gpsimd.iota(trash[:], pattern=[[0, 1]], base=N, channel_multiplier=1,
                               allow_small_or_imprecise_dtypes=True)
                nc.gpsimd.iota(rid_i[:], pattern=[[1, T]], base=0, channel_multiplier=T)

            @block.sync
            def _(sp):
                def load(to, of):
                    sp.dma_start(to, of).then_inc(loaded, 16)
                    n_loads[0] += 1

                sp.wait_ge(zeroed, 1)
                load(w0[:], a["L0_gnn_weight"])
                load(w1e[0:2 * F, :], a["L1_gnn_W"])
                load(w1e[2 * F:2 * F + 1, :], a["L1_gnn_b"].rearrange("(o f) -> o f", o=1))
                load(w1d[0:F, :], a["L1_gnn_W"][0:F, :])
                load(w1d[F:F + 1, :], a["L1_gnn_b"].rearrange("(o f) -> o f", o=1))
                for n in range(3):
                    init, w, root, b = (a[f"L2_gnn_c{n + 1}_{s}"] for s in ("init", "w", "root", "b"))
                    h, f = hs[n], fins[n]
                    kb = wbias[n].shape[0] - 1
                    kv = lambda t: t.rearrange("f (k g) -> f k g", k=K)
                    load(kv(wbias[n][kb - f:kb, :]), init.rearrange("k f g -> f k g"))
                    load(kv(wbias[n][kb:kb + 1, :]), b[0].rearrange("k o g -> o k g"))
                    load(kv((wbias[n] if n == 0 else wroot0[n])[0:f, :]), root[0].rearrange("k f g -> f k g"))
                    load(kv(wroot1[n][0:f, :]), root[1].rearrange("k f g -> f k g"))
                    load(kv(wroot1[n][f:f + 1, :]), b[1].rearrange("k o g -> o k g"))
                    for k in range(K):
                        if h == H and k == 2:
                            load(wblk[n][1][:, :], w[0, k])
                        else:
                            load(wblk[n][0][k * h:(k + 1) * h, k * h:(k + 1) * h], w[0, k])
                load(wl1[:], a["L3_gnn_W1"])
                load(wl2[:], a["L3_gnn_W2"])
                load(gamma[:], a["L2_gnn_bn_gamma"].partition_broadcast(128))
                load(beta[:], a["L2_gnn_bn_beta"].partition_broadcast(128))
                inits = [(ytab[0:N, :].rearrange("(p n) f -> p (n f)", p=P), x.rearrange("(p n) f -> p (n f)", p=P)),
                         (ytab[N:N + P, :], zrow[0:P, 0:F]),
                         (slot_tab.rearrange("(p n) o -> p (n o)", p=P), nils[:]),
                         (mtab[NIL:NIL + 1, :], zrow[0:1, 0:SW])]
                inits += [(atab[n][NIL:NIL + 1, :], zrow[0:1, 0:fins[n]]) for n in range(3)]
                for to, of in inits:
                    sp.dma_start(to, of).then_inc(init_done, 16)
                sp.wait_ge(loaded, 16 * n_loads[0])
                sp.wait_ge(init_done, 16 * len(inits))

        with Phase(nc) as ph:
            folded = sem("folded", ph)
            block = ph.open()

            @block.scalar
            def _(act):
                for n in range(3):
                    for w in (wroot1[n], wblk[n][0], wblk[n][1]):
                        if w is not None:
                            nc.scalar.mul(w[:], w[:], 1.0 / K)
                nc.scalar.mul(wl1[:], wl1[:], 0.2 ** 0.5)

            @block.vector
            def _(dve):
                ps, pv = 0.17677669529663687 / MUL ** 0.5, 0.25 / MUL ** 0.5
                path = lambda i: wl2[:, i * MUL * MOUT:(i + 1) * MUL * MOUT].rearrange("j (u w) -> j w u", u=MUL)
                mix = wmix[:].rearrange("j (o w h u) -> j o w h u", o=3, w=MOUT, h=2)
                vec = wvec[:].rearrange("j (w u) -> j w u", w=MOUT)
                for o, h, i, c in ((0, 0, 0, ps), (0, 1, 1, ps), (1, 0, 2, ps), (1, 1, 3, ps), (2, 0, 4, pv), (2, 1, 6, pv * 1.5 ** 0.5)):
                    nc.vector.tensor_scalar(mix[:, o, :, h], path(i), c, None, ALU.mult)
                nc.vector.tensor_scalar(vec, path(5), pv * 0.5773502691896258, None, ALU.mult).then_inc(folded, 1)
                dve.wait_ge(folded, 1)
                nc.vector.scalar_tensor_tensor(vec, path(6), -pv * 1.5 ** 0.5 / 3, vec, ALU.mult, ALU.add).then_inc(folded, 1)

        with Phase(nc) as ph:
            loaded = sem("rows_loaded", ph)
            filled = sem("rows_filled", ph)
            stored = sem("same_stored", ph)
            bcast = sem("same_bcast", ph)
            dlink = sem("prep_link", ph)
            row_ready = sem("row_ready", ph)
            turned = sem("turned", ph)
            taken = sem("taken", ph)
            ri = sb("ri", [ROW, 2, 2, P], I32, ph)
            edge_i = sb("edge_i", [ROW, 2, 2], I32, ph)
            rf = sb("rf", [ROW, 2, P + 2], F32, ph)
            cols = sb("cols", [ROW, 7, 2, P], F32, ph)
            same_f = sb("same_f", [ROW, 2, P], U8, ph)
            nl = sb("nl", [ROW, 2, P], F32, ph)
            pt = pb("prep_t", [128, 2, 512], ph)
            same_s = sb("same_s", [ROW, 2, P], F32, ph)
            nlast = sb("nlast", [ROW, 2, P], F32, ph)
            deg_l, fprod, bprod, rid_r, rid_m, rid_l = (
                sb(n, [ROW, 2, P], F32, ph) for n in ("deg_l", "fprod", "bprod", "rid_r", "rid_m", "rid_l"))
            no = sb("no", [ROW, P], F32, ph)
            ends = sb("ends", [1, 4, T], F32, ph)
            carry = sb("carry", [1, 2, T + 1], F32, ph)
            cin = sb("cin", [ROW, 2, 2], F32, ph)
            dlink2, dlink3 = sem("prep_link2", ph), sem("prep_link3", ph)
            half = lambda v: v.rearrange("(h q p) -> q h p", h=2, p=P)

            block = nc.Block()
            block.__enter__()

            @block.sync
            def _(sp):
                sp.wait_ge(filled, 1)
                sp.dma_start(ri[:, 0], half(src)).then_inc(loaded, 16)
                sp.dma_start(ri[:, 1], half(dst)).then_inc(loaded, 16)
                sp.dma_start(cols[:, 4], half(weight)).then_inc(loaded, 16)
                flat = dst.rearrange("(t p) -> t p", p=P)
                sp.dma_start(edge_i[1:ROW, 0, 0:1], flat[0:ROW - 1, P - 1:P], allow_slow_non_contiguous=True).then_inc(loaded, 16)
                sp.dma_start(edge_i[0:ROW, 1, 0:1], flat[ROW - 1:T - 1, P - 1:P], allow_slow_non_contiguous=True).then_inc(loaded, 16)
                sp.dma_start(edge_i[0:ROW, 0, 1:2], flat[1:ROW + 1, 0:1], allow_slow_non_contiguous=True).then_inc(loaded, 16)
                sp.dma_start(edge_i[0:ROW - 1, 1, 1:2], flat[ROW + 1:T, 0:1], allow_slow_non_contiguous=True).then_inc(loaded, 16)
                sp.wait_ge(row_ready, 1)
                sp.dma_start(half(same_row), same_f[:]).then_inc(stored, 16)
                sp.wait_ge(stored, 16)
                sp.dma_start(same_b[:], same_row.partition_broadcast(128)).then_inc(bcast, 16)
                sp.wait_ge(bcast, 16)

            @block.vector
            def _(dve):
                link = Links(dve, dlink)
                nc.vector.memset(edge_i[:], -1).then_inc(filled, 1)
                dve.wait_ge(filled, 1)
                dve.wait_ge(loaded, 7 * 16)
                nc.vector.tensor_copy(cols[:, 0], ri[:, 0])
                nc.vector.tensor_copy(rf[:, :, 0:1], edge_i[:, :, 0:1])
                nc.vector.tensor_copy(rf[:, :, P + 1:P + 2], edge_i[:, :, 1:2])
                nc.vector.tensor_copy(cols[:, 1], ri[:, 1])
                link(nc.vector.tensor_copy(rf[:, :, 1:P + 1], ri[:, 1]))
                nc.vector.memset(no[:], 0.0)
                nc.vector.tensor_tensor(same_s[:], rf[:, :, 1:P + 1], rf[:, :, 0:P], ALU.is_equal)
                nc.vector.tensor_tensor(nlast[:], rf[:, :, 1:P + 1], rf[:, :, 2:P + 2], ALU.is_equal)
                nc.vector.tensor_tensor(same_f[:], rf[:, :, 1:P + 1], rf[:, :, 0:P], ALU.is_equal).then_inc(row_ready, 1)
                link(nc.vector.tensor_tensor(nl[:], rf[:, :, 1:P + 1], rf[:, :, 2:P + 2], ALU.is_equal))
                nc.vector.tensor_scalar(cols[:, 3], nl[:], -1.0, 1.0, ALU.mult, ALU.add)
                link(nc.vector.tensor_scalar(nl[:], nl[:], float(FAR), None, ALU.mult))
                nc.vector.tensor_tensor(cols[:, 2], rf[:, :, 1:P + 1], nl[:], ALU.add).then_inc(row_ready, 1)
            block.__exit__(None, None, None)


            def ends_to_row(name, cols_of):
                with Phase(nc) as b:
                    there = sem(name, b)
                    blk = b.open()

                    @blk.tensor
                    def _(pe):
                        for n, col in enumerate(cols_of):
                            for h in range(2):
                                last = nc.tensor.transpose(pt[0:1, n // 2, (n % 2 * 2 + h) * ROW:(n % 2 * 2 + h + 1) * ROW],
                                                           col[:, h], ident[0:ROW, 0:ROW])
                        last.then_inc(there, 1)

                    @blk.vector
                    def _(dve):
                        dve.wait_ge(there, 1)
                        for n in range(len(cols_of)):
                            nc.vector.tensor_copy(ends[0:1, n], pt[0:1, n // 2, n % 2 * T:(n % 2 + 1) * T])

            def row_to_ends(name, n_rows):
                with Phase(nc) as b:
                    there = sem(name, b)
                    blk = b.open()

                    @blk.tensor
                    def _(pe):
                        for n in range(n_rows):
                            for h in range(2):
                                last = nc.tensor.transpose(pt[0:ROW, 0, n * 2 + h:n * 2 + h + 1],
                                                           carry[0:1, n, 1 + h * ROW:1 + (h + 1) * ROW], ident[0:1, 0:1])
                        last.then_inc(there, 1)

                    @blk.vector
                    def _(dve):
                        dve.wait_ge(there, 1)
                        nc.vector.tensor_copy(cin[:, 0:n_rows], pt[0:ROW, 0, 0:2 * n_rows].rearrange("r (n h) -> r n h", h=2))

            scan = nc.vector.tensor_tensor_scan
            with nc.Block() as b1:
                @b1.gpsimd
                def _(pool):
                    nc.gpsimd.iota(rid_r[:], pattern=[[ROW, 2], [T, P]], base=0, channel_multiplier=1,
                                   allow_small_or_imprecise_dtypes=True)

                @b1.vector
                def _(dve):
                    nc.vector.memset(carry[:], 0.0)
                    for h in range(2):
                        scan(deg_l[:, h], same_s[:, h], cols[:, 4, h], 0.0, ALU.mult, ALU.add)
                        scan(fprod[:, h], same_s[:, h], no[:], 1.0, ALU.mult, ALU.add)
                        scan(bprod[:, h, ::-1], nlast[:, h, ::-1], no[:], 1.0, ALU.mult, ALU.add)
            with nc.Block() as b2:
                @b2.vector
                def _(dve):
                    nc.vector.tensor_tensor(rid_m[:], rid_r[:], cols[:, 3], ALU.mult).then_inc(dlink2, 1)
                    dve.wait_ge(dlink2, 1)
                    for h in range(2):
                        scan(rid_l[:, h, ::-1], nlast[:, h, ::-1], rid_m[:, h, ::-1], 0.0, ALU.mult, ALU.add)
            ends_to_row("e1", [deg_l[:, :, P - 1:P], fprod[:, :, P - 1:P], rid_l[:, :, 0:1], bprod[:, :, 0:1]])
            with nc.Block() as b3:
                @b3.vector
                def _(dve):
                    scan(carry[0:1, 0, 2:T + 1], ends[0:1, 1, 0:T - 1], ends[0:1, 0, 0:T - 1], 0.0, ALU.mult, ALU.add)
                    scan(carry[0:1, 1, 1:T][:, ::-1], ends[0:1, 3, 1:T][:, ::-1], ends[0:1, 2, 1:T][:, ::-1], 0.0, ALU.mult, ALU.add)
            row_to_ends("e2", 2)
            with nc.Block() as b4:
                @b4.vector
                def _(dve):
                    link = Links(dve, dlink3)
                    for h in range(2):
                        nc.vector.scalar_tensor_tensor(cols[:, 6, h], bprod[:, h], cin[:, 1, h:h + 1], rid_l[:, h], ALU.mult, ALU.add)
                        link(nc.vector.scalar_tensor_tensor(deg_l[:, h], fprod[:, h], cin[:, 0, h:h + 1], deg_l[:, h], ALU.mult, ALU.add))
                    link(nc.vector.tensor_tensor(deg_l[:], deg_l[:], cols[:, 3], ALU.mult))
                    for h in range(2):
                        scan(cols[:, 5, h, ::-1], nlast[:, h, ::-1], deg_l[:, h, ::-1], 0.0, ALU.mult, ALU.add)
            ends_to_row("e3", [cols[:, 5, :, 0:1], bprod[:, :, 0:1]])
            with nc.Block() as b5:
                @b5.vector
                def _(dve):
                    scan(carry[0:1, 0, 1:T][:, ::-1], ends[0:1, 1, 1:T][:, ::-1], ends[0:1, 0, 1:T][:, ::-1], 0.0, ALU.mult, ALU.add)
                    nc.vector.memset(carry[0:1, 0, T:T + 1], 0.0)
            row_to_ends("e4", 1)
            with nc.Block() as b6:
                @b6.vector
                def _(dve):
                    for h in range(2):
                        nc.vector.scalar_tensor_tensor(cols[:, 5, h], bprod[:, h], cin[:, 0, h:h + 1], cols[:, 5, h], ALU.mult, ALU.add)

            with nc.Block() as b7:
                @b7.vector
                def _(dve):
                    for q, to in enumerate((src_f, dst_i, last_i, ew, dinv_t, slot_t)):
                        for h in range(2):
                            n = 2 * q + h
                            dve.wait_ge(turned, n + 1)
                            last = nc.vector.tensor_copy(to[0:P, h * ROW:(h + 1) * ROW], pt[0:P, h, 0:ROW])
                            if q == 0:
                                last = nc.vector.tensor_copy(src_i[0:P, h * ROW:(h + 1) * ROW], pt[0:P, h, 0:ROW])
                            last.then_inc(taken, 1)

                @b7.tensor
                def _(pe):
                    for q, col in enumerate((0, 1, 2, 4, 5, 6)):
                        for h in range(2):
                            n = 2 * q + h
                            if n >= 2:
                                pe.wait_ge(taken, n - 1)
                            nc.tensor.transpose(pt[0:P, h, 0:ROW], cols[:, col, h], ident[0:ROW, 0:ROW]).then_inc(turned, 1)

        with Phase(nc) as ph:
            staged_d = [sem(f"l0_staged_d{s}", ph) for s in range(2)]
            staged = [sem(f"l0_staged{s}", ph) for s in range(2)]
            rep_made = sem("l0_rep_made", ph)
            rep_turned = sem("l0_rep_turned", ph)
            eq_made = sem("l0_eq_made", ph)
            idx_made = sem("l0_idx_made", ph)
            scaled = sem("l0_scaled", ph)
            summed = sem("l0_summed", ph)
            sum_taken = sem("l0_sum_taken", ph)
            mult = sem("l0_mult", ph)
            row_made = sem("l0_row_made", ph)
            used = sem("l0_used", ph)
            dlink = sem("l0_link", ph)
            stg_d = sb("l0_stg_d", [128, 2, C], I32, ph)
            stg = sb("l0_stg", [128, 2, 2, C], I32, ph)
            stg_a = sb("l0_stg_a", [128, 2, C], I32, ph)
            xt = sb("l0_xt", [128, 2, C, F], F32, ph)
            rep = sb("l0_rep", [128, 2, C, P], F32, ph)
            eq = sb("l0_eq", [128, 2, C, P], F32, ph)
            eql = sb("l0_eql", [128, C, P], F32, ph)
            dup = sb("l0_dup", [128, C], F32, ph)
            tmp = sb("l0_tmp", [128, C], F32, ph)
            xe = sb("l0_xe", [128, 2, C, F], F32, ph)
            zt = sb("l0_zt", [F, 2, PG], F32, ph)
            zrows = sb("l0_zrows", [128, 2, C, F], F32, ph)
            p_rep = pb("l0_p_rep", [128, 2, 512], ph)
            p_sum = pb("l0_p_sum", [128, 2, 512], ph)
            p_row = pb("l0_p_row", [128, 2, 512], ph)
            block = ph.open()

            @block.sync
            def _(sp):
                sp.dma_start(stg_d[0:P, 0], dst_i[0:P, 0:C]).then_inc(staged_d[0], 16)
                with sp.Fori(0, NG // 2) as i:
                    for s in range(2):
                        g = i * 2 + s
                        sp.wait_ge(scaled, free1(g))
                        sp.sem_inc(sp_tick, 1)
                        sp.dma_start(stg_d[0:P, 1 - s], dst_i[0:P, bass.ds(g * C + C, C)]).then_inc(staged_d[1 - s], 16)
                        sp.wait_ge(used, free(g))
                        sp.sem_inc(sp_tick, 1)
                        sp.dma_start(stg[0:P, s, 0], last_i[0:P, bass.ds(g * C, C)]).then_inc(staged[s], 16)
                        sp.dma_start(stg[0:P, s, 1], rid_i[0:P, bass.ds(g * C, C)]).then_inc(staged[s], 16)

            @block.gpsimd
            def _(pool):
                bound = pool.to_reg(N - 1)
                credit(pool, used)

                def gather(s, c):
                    pool.indirect_dma_start(out=xt[0:P, s, c], out_offset=None, in_=x, in_offset=bass.IndirectOffsetOnAxis(
                        ap=stg_d[0:P, s, c:c + 1], axis=0)).then_inc(gathered[s], 16)

                pool.wait_ge(staged_d[0], 16)
                pool.sem_inc(pool_tick, 1)
                for c in range(C):
                    gather(0, c)
                with pool.Fori(0, NG // 2) as i:
                    for s in range(2):
                        g = i * 2 + s
                        pool.wait_ge(staged_d[1 - s], (i + 1 + s) * 16)
                        pool.wait_ge(scaled, free1(g))
                        pool.sem_inc(pool_tick, 1)
                        for c in range(C):
                            gather(1 - s, c)
                        pool.wait_ge(row_made, done(g))
                        pool.wait_ge(idx_made, done(g))
                        pool.wait_ge(staged[s], (i + 1) * 32)
                        pool.sem_inc(pool_tick, 1)
                        for c in range(C):
                            pool.indirect_dma_start(out=ytab, out_offset=bass.IndirectOffsetOnAxis(ap=stg_a[0:P, s, c:c + 1], axis=0),
                                                    in_=zrows[0:P, s, c], in_offset=None, compute_op=ALU.add).then_inc(added, 16)
                            pool.indirect_dma_start(out=slot_tab, out_offset=bass.IndirectOffsetOnAxis(ap=stg[0:P, s, 0, c:c + 1], axis=0),
                                                    in_=stg[0:P, s, 1, c:c + 1], in_offset=None, bounds_check=bound,
                                                    oob_is_err=False).then_inc(slotted, 16)
                            pool.wait_ge(added, g * C * 16 + c * 16 + 16)
                            pool.sem_inc(pool_tick, 1)
                        pool.wait_ge(slotted, g * C * 16 + C * 16)
                        pool.sem_inc(pool_tick, 1)
                        pool.sem_inc(used, 1)
                pool.wait_ge(gathered[0], (NG // 2 + 1) * C * 16)

            @block.vector
            def _(dve):
                link = Links(dve, dlink)
                credit(dve, rep_made, eq_made, idx_made, scaled)
                with dve.Fori(0, NG // 2) as i:
                    link.turn(i, 10)
                    for s in range(2):
                        g = i * 2 + s
                        mine = src_f[0:P, bass.ds(g * C, C)]
                        dve.wait_ge(rep_turned, free(g))
                        dve.sem_inc(dve_tick, 1)
                        nc.vector.tensor_scalar(rep[0:P, s], over(mine, P), 1.0, None, ALU.mult).then_inc(rep_made, 1)
                        dve.wait_ge(rep_turned, done(g))
                        dve.wait_ge(summed, free(g))
                        dve.sem_inc(dve_tick, 1)
                        pr = p_rep[0:P, s, 0:PG].rearrange("p (c q) -> p c q", c=C)
                        link(nc.vector.tensor_tensor(eq[0:P, s], pr, over(mine, P), ALU.is_equal))
                        link(nc.vector.tensor_tensor(eql[0:P], eq[0:P, s], lower[0:P, :].unsqueeze(1).broadcast_to([P, C, P]), ALU.mult))
                        dve.sem_inc(eq_made, 1)
                        nc.vector.tensor_scalar(tmp[0:P], mine, -1.0, trash[0:P, 0:1], ALU.mult, ALU.add)
                        link(nc.vector.reduce_sum(dup[0:P], eql[0:P], AX))
                        link(nc.vector.scalar_tensor_tensor(tmp[0:P], dup[0:P], 1.0, tmp[0:P], ALU.min, ALU.mult))
                        dve.wait_ge(used, free(g))
                        dve.sem_inc(dve_tick, 1)
                        link(nc.vector.tensor_tensor(stg_a[0:P, s], tmp[0:P], mine, ALU.add))
                        dve.sem_inc(idx_made, 1)
                        dve.wait_ge(gathered[s], (i + 1) * C * 16)
                        dve.sem_inc(dve_tick, 1)
                        nc.vector.tensor_tensor(xe[0:P, s], xt[0:P, s], over(ew[0:P, bass.ds(g * C, C)], F), ALU.mult).then_inc(scaled, 1)
                link.end(NG // 2)

            @block.tensor
            def _(pe):
                credit(pe, rep_turned, summed, mult)
                with pe.Fori(0, NG // 2) as i:
                    for s in range(2):
                        g = i * 2 + s
                        pe.wait_ge(rep_made, done(g))
                        pe.wait_ge(eq_made, free(g))
                        pe.sem_inc(pe_tick, 1)
                        for c in range(C):
                            last = nc.tensor.transpose(p_rep[0:P, s, c * P:(c + 1) * P], rep[0:P, s, c], ident[0:P, 0:P])
                        last.then_inc(rep_turned, 1)
                        pe.wait_ge(eq_made, done(g))
                        pe.wait_ge(scaled, done(g))
                        pe.wait_ge(sum_taken, free(g))
                        pe.sem_inc(pe_tick, 1)
                        for c in range(C):
                            last = nc.tensor.matmul(p_sum[0:F, s, c * P:(c + 1) * P], xe[0:P, s, c], eq[0:P, s, c], start=True, stop=True)
                        last.then_inc(summed, 1)
                        pe.wait_ge(sum_taken, done(g))
                        pe.wait_ge(row_made, free(g))
                        pe.sem_inc(pe_tick, 1)
                        for c in range(C):
                            last = nc.tensor.matmul(p_row[0:P, s, c * F:(c + 1) * F], zt[:, s, c * P:(c + 1) * P], w0[:], start=True, stop=True)
                        last.then_inc(mult, 1)

            @block.scalar
            def _(act):
                credit(act, sum_taken, row_made)
                with act.Fori(0, NG // 2) as i:
                    for s in range(2):
                        g = i * 2 + s
                        act.wait_ge(summed, done(g))
                        act.wait_ge(mult, free(g))
                        act.sem_inc(act_tick, 1)
                        nc.scalar.copy(zt[:, s], p_sum[0:F, s, 0:PG]).then_inc(sum_taken, 1)
                        act.wait_ge(mult, done(g))
                        act.wait_ge(used, free(g))
                        act.sem_inc(act_tick, 1)
                        nc.scalar.copy(zrows[0:P, s], p_row[0:P, s, 0:C * F].rearrange("p (c f) -> p c f", c=C)).then_inc(row_made, 1)

        g_base[0] += (NG // 2 + 1) * C * 16
        g_base[1] += NG // 2 * C * 16


        with Phase(nc) as ph:
            staged = [sem(f"l1_staged{s}", ph) for s in range(2)]
            stored = [sem(f"l1_stored{s}", ph) for s in range(2)]
            var_made, dev_made, read, rs_made, scanned, sums_made, xt_made = (
                sem(f"l1_{n}", ph) for n in ("var_made", "dev_made", "read", "rs_made", "scanned", "sums_made", "xt_made"))
            turned, backed, fm_turned, mult = (sem(f"l1_{n}", ph) for n in ("turned", "backed", "fm_turned", "mult"))
            fm_taken, used = sem("l1_fm_taken", ph), sem("l1_used", ph)
            dlink = sem("l1_link", ph)
            stg = sb("l1_stg", [128, 2, 2, C], I32, ph)
            gy = sb("l1_gy", [128, 2, 2 * C, F], F32, ph)
            gs = sb("l1_gs", [128, 2, C], I32, ph)
            cb = sb("l1_cb", [128, 2 * C, F], F32, ph)
            sq = sb("l1_sq", [128, 2 * C, F], F32, ph)
            sm = sb("l1_sm", [128, 2 * C], F32, ph)
            va = sb("l1_va", [128, 2 * C], F32, ph)
            sd = sb("l1_sd", [128, 2 * C], F32, ph)
            rc = sb("l1_rc", [128, 2 * C], F32, ph)
            rs = sb("l1_rs", [128, 2, C, SW], F32, ph)
            sc = sb("l1_sc", [SW, 2, PG], F32, ph)
            mrow = sb("l1_mrow", [128, 2, C, SW], F32, ph)
            xt = sb("l1_xt", [128, 2, C, 2 * F + 1], F32, ph)
            xf = sb("l1_xf", [2 * F + 1, 2, PG], F32, ph)
            u = sb("l1_u", [128, C, F], F32, ph)
            p_t = pb("l1_p_t", [128, 2, 512], ph)
            p_b = pb("l1_p_b", [128, 2, 512], ph)
            p_f = pb("l1_p_f", [128, 2, 512], ph)
            p_m = pb("l1_p_m", [128, 2, 512], ph)
            block = ph.open()

            @block.sync
            def _(sp):
                with sp.Fori(0, NG // 2) as i:
                    for s in range(2):
                        g = i * 2 + s
                        sp.wait_ge(read, free(g))
                        sp.sem_inc(sp_tick, 1)
                        sp.dma_start(stg[0:P, s, 0], src_i[0:P, bass.ds(g * C, C)]).then_inc(staged[s], 16)
                        sp.dma_start(stg[0:P, s, 1], dst_i[0:P, bass.ds(g * C, C)]).then_inc(staged[s], 16)

            @block.gpsimd
            def _(pool):
                with pool.Fori(0, NG // 2) as i:
                    for s in range(2):
                        g = i * 2 + s
                        pool.wait_ge(staged[s], (i + 1) * 32)
                        pool.wait_ge(read, free(g))
                        pool.sem_inc(pool_tick, 1)
                        for tab, to, k in ((ytab, gy[0:P, s, 0:C], 0), (ytab, gy[0:P, s, C:2 * C], 1),
                                           (slot_tab, gs[0:P, s].unsqueeze(2), 0)):
                            for c in range(C):
                                pool.indirect_dma_start(out=to[:, c], out_offset=None, in_=tab, in_offset=bass.IndirectOffsetOnAxis(
                                    ap=stg[0:P, s, k, c:c + 1], axis=0)).then_inc(gathered[s], 16)

            @block.vector
            def _(dve):
                link = Links(dve, dlink)
                credit(dve, var_made, read, rs_made, scanned, sums_made, xt_made)
                for s in range(2):
                    nc.vector.memset(rs[:, s, :, F:F + 1], 1.0)
                    nc.vector.memset(xt[:, s, :, 2 * F:2 * F + 1], 1.0)
                link(nc.vector.memset(sc[:, 1, PG - 1:PG], 0.0))
                link.base = 1
                with dve.Fori(0, NG // 2) as i:
                    link.turn(i, 2 * 13)
                    for s in range(2):
                        g = i * 2 + s
                        cols = bass.ds(g * C, C)
                        dve.wait_ge(gathered[s], (i + 1) * 3 * C * 16 + g_base[s])
                        dve.wait_ge(turned, free(g))
                        dve.wait_ge(fm_turned, free(g))
                        dve.sem_inc(dve_tick, 1)
                        nc.vector.tensor_scalar(slot_i[0:P, cols], gs[0:P, s], 0, None, ALU.add)
                        center(link, cb[0:P], sm[0:P], sq[0:P], va[0:P], gy[0:P, s]).then_inc(var_made, 1)
                        dve.sem_inc(read, 1)
                        dve.wait_ge(dev_made, i * 4 + 2 * s + 1)
                        dve.sem_inc(dve_tick, 1)
                        link(nc.vector.reciprocal(rc[0:P], sd[0:P]))
                        nc.vector.tensor_tensor(rs[0:P, s, :, 0:F], cb[0:P, 0:C], over(rc[0:P, 0:C], F), ALU.mult)
                        nc.vector.tensor_tensor(x2s[0:P, cols, :], cb[0:P, 0:C], over(rc[0:P, 0:C], F), ALU.mult)
                        nc.vector.tensor_tensor(xt[0:P, s, :, 0:F], cb[0:P, C:2 * C], over(rc[0:P, C:2 * C], F), ALU.mult)
                        nc.vector.tensor_scalar(rs[0:P, s, :, F + 1], ew[0:P, cols], 1.0, None, ALU.mult).then_inc(rs_made, 1)
                        dve.wait_ge(turned, done(g))
                        dve.wait_ge(backed, free(g))
                        dve.sem_inc(dve_tick, 1)
                        link(nc.vector.tensor_tensor_scan(sc[:, s], same_b[0:SW, bass.ds(g * PG, PG)], p_t[0:SW, s, 0:PG],
                                                          sc[:, 1 - s, PG - 1:PG], ALU.mult, ALU.add))
                        dve.sem_inc(scanned, 1)
                        dve.wait_ge(backed, done(g))
                        dve.wait_ge(stored[s], (i + 1) * 16)
                        dve.sem_inc(dve_tick, 1)
                        sums = p_b[0:P, s, 0:C * SW].rearrange("p (c f) -> p c f", c=C)
                        nc.vector.tensor_copy(mrow[0:P, s], sums).then_inc(sums_made, 1)
                        link(nc.vector.tensor_scalar(sm[0:P, 0:C], sums[:, :, F], 1.0, None, ALU.max))
                        link(nc.vector.reciprocal(rc[0:P, 0:C], sm[0:P, 0:C]))
                        nc.vector.tensor_tensor(xt[0:P, s, :, F:2 * F], sums[:, :, 0:F], over(rc[0:P, 0:C], F), ALU.mult).then_inc(xt_made, 1)
                        dve.wait_ge(mult, done(g))
                        dve.sem_inc(dve_tick, 1)
                        link(nc.vector.scalar_tensor_tensor(u[0:P], p_m[0:P, s, 0:C * F].rearrange("p (c f) -> p c f", c=C), 0.0,
                                                            xt[0:P, s, :, 0:F], ALU.max, ALU.add))
                        center(link, cb[0:P, 0:C], sm[0:P, 0:C], sq[0:P, 0:C], va[0:P, 0:C], u[0:P]).then_inc(var_made, 1)
                        dve.sem_inc(used, 1)
                        dve.wait_ge(dev_made, i * 4 + 2 * s + 2)
                        dve.sem_inc(dve_tick, 1)
                        link(nc.vector.reciprocal(rc[0:P, 0:C], sd[0:P, 0:C]))
                        link(nc.vector.tensor_tensor(x2t[0:P, cols, :], cb[0:P, 0:C], over(rc[0:P, 0:C], F), ALU.mult))
                link.end(NG // 2)

            @block.tensor
            def _(pe):
                credit(pe, turned, backed, fm_turned, mult)
                with pe.Fori(0, NG // 2) as i:
                    for s in range(2):
                        g = i * 2 + s
                        pe.wait_ge(rs_made, done(g))
                        pe.wait_ge(scanned, free(g))
                        pe.sem_inc(pe_tick, 1)
                        for c in range(C):
                            last = nc.tensor.transpose(p_t[0:SW, s, c * P:(c + 1) * P], rs[0:P, s, c], ident[0:P, 0:P])
                        last.then_inc(turned, 1)
                        pe.wait_ge(scanned, done(g))
                        pe.wait_ge(xt_made, free(g))
                        pe.sem_inc(pe_tick, 1)
                        for c in range(C):
                            last = nc.tensor.transpose(p_b[0:P, s, c * SW:(c + 1) * SW], sc[:, s, c * P:(c + 1) * P], ident[0:SW, 0:SW])
                        last.then_inc(backed, 1)
                        pe.wait_ge(xt_made, done(g))
                        pe.wait_ge(fm_taken, free(g))
                        pe.sem_inc(pe_tick, 1)
                        for c in range(C):
                            last = nc.tensor.transpose(p_f[0:2 * F + 1, s, c * P:(c + 1) * P], xt[0:P, s, c], ident[0:P, 0:P])
                        last.then_inc(fm_turned, 1)
                        pe.wait_ge(fm_taken, done(g))
                        pe.wait_ge(used, g + 1)
                        pe.sem_inc(pe_tick, 1)
                        for c in range(C):
                            last = nc.tensor.matmul(p_m[0:P, s, c * F:(c + 1) * F], xf[:, s, c * P:(c + 1) * P], w1e[:], start=True, stop=True)
                        last.then_inc(mult, 1)

            @block.scalar
            def _(act):
                credit(act, fm_taken)
                act.sem_inc(stored[0], 16)
                act.sem_inc(stored[1], 16)
                act.sem_inc(used, LEAD)
                with act.Fori(0, NG // 2) as i:
                    for s in range(2):
                        g = i * 2 + s
                        act.wait_ge(var_made, i * 4 + 2 * s + 1 + LEAD)
                        act.sem_inc(act_tick, 1)
                        deviation(sd[0:P], va[0:P]).then_inc(dev_made, 1)
                        act.wait_ge(sums_made, done(g))
                        act.sem_inc(act_tick, 1)
                        act.dma_start(rows(mtab, g), mrow[0:P, s]).then_inc(stored[s], 16)
                        act.wait_ge(fm_turned, done(g))
                        act.wait_ge(mult, free(g))
                        act.sem_inc(act_tick, 1)
                        nc.scalar.copy(xf[:, s], p_f[0:2 * F + 1, s, 0:PG]).then_inc(fm_taken, 1)
                        act.wait_ge(var_made, i * 4 + 2 * s + 2 + LEAD)
                        act.sem_inc(act_tick, 1)
                        deviation(sd[0:P, 0:C], va[0:P, 0:C]).then_inc(dev_made, 1)
                for s in range(2):
                    act.wait_ge(stored[s], (NG // 2 + 1) * 16)

        for s in range(2):
            g_base[s] += NG // 2 * 3 * C * 16
        with Phase(nc) as ph:
            staged = [sem(f"c_staged{s}", ph) for s in range(2)]
            var_made, dev_made, xt_made, fm_turned, fm_taken, mult, used = (
                sem(f"c_{n}", ph) for n in ("var_made", "dev_made", "xt_made", "fm_turned", "fm_taken", "mult", "used"))
            dlink = sem("c_link", ph)
            stg = sb("c_stg", [128, 2, C], I32, ph)
            gm = sb("c_gm", [128, 2, C, SW], F32, ph)
            cb = sb("c_cb", [128, C, F], F32, ph)
            sq = sb("c_sq", [128, C, F], F32, ph)
            sm, va, sd, rc = (sb(f"c_{n}", [128, C], F32, ph) for n in ("sm", "va", "sd", "rc"))
            xt = sb("c_xt", [128, 2, C, 2 * F + 1], F32, ph)
            xf = sb("c_xf", [2 * F + 1, 2, PG], F32, ph)
            u = sb("c_u", [128, C, F], F32, ph)
            p_f = pb("c_p_f", [128, 2, 512], ph)
            p_m = pb("c_p_m", [128, 2, 512], ph)
            block = ph.open()

            @block.sync
            def _(sp):
                with sp.Fori(0, NG // 2) as i:
                    for s in range(2):
                        g = i * 2 + s
                        sp.wait_ge(xt_made, free(g))
                        sp.sem_inc(sp_tick, 1)
                        sp.dma_start(stg[0:P, s], slot_i[0:P, bass.ds(g * C, C)]).then_inc(staged[s], 16)

            @block.gpsimd
            def _(pool):
                with pool.Fori(0, NG // 2) as i:
                    for s in range(2):
                        g = i * 2 + s
                        pool.wait_ge(staged[s], (i + 1) * 16)
                        pool.wait_ge(xt_made, free(g))
                        pool.sem_inc(pool_tick, 1)
                        for c in range(C):
                            pool.indirect_dma_start(out=gm[0:P, s, c], out_offset=None, in_=mtab, in_offset=bass.IndirectOffsetOnAxis(
                                ap=stg[0:P, s, c:c + 1], axis=0)).then_inc(gathered[s], 16)

            @block.vector
            def _(dve):
                link = Links(dve, dlink)
                credit(dve, var_made, xt_made, used)
                for s in range(2):
                    nc.vector.memset(xt[:, s, :, 2 * F:2 * F + 1], 1.0)
                with dve.Fori(0, NG // 2) as i:
                    link.turn(i, 2 * 8)
                    for s in range(2):
                        g = i * 2 + s
                        cols = bass.ds(g * C, C)
                        dve.wait_ge(gathered[s], (i + 1) * C * 16 + g_base[s])
                        dve.wait_ge(fm_turned, free(g))
                        dve.sem_inc(dve_tick, 1)
                        nc.vector.tensor_scalar(norm[0:P, cols], gm[0:P, s, :, F + 1], 1.0, None, ALU.mult)
                        nc.vector.tensor_scalar(xt[0:P, s, :, 0:F], x2s[0:P, cols, :], 1.0, None, ALU.mult)
                        link(nc.vector.tensor_scalar(sm[0:P], gm[0:P, s, :, F], 1.0, None, ALU.max))
                        link(nc.vector.reciprocal(rc[0:P], sm[0:P]))
                        nc.vector.tensor_tensor(xt[0:P, s, :, F:2 * F], gm[0:P, s, :, 0:F], over(rc[0:P], F), ALU.mult).then_inc(xt_made, 1)
                        dve.wait_ge(mult, done(g))
                        dve.sem_inc(dve_tick, 1)
                        link(nc.vector.scalar_tensor_tensor(u[0:P], p_m[0:P, s, 0:C * F].rearrange("p (c f) -> p c f", c=C), 0.0,
                                                            xt[0:P, s, :, 0:F], ALU.max, ALU.add))
                        center(link, cb[0:P], sm[0:P], sq[0:P], va[0:P], u[0:P]).then_inc(var_made, 1)
                        dve.sem_inc(used, 1)
                        dve.wait_ge(dev_made, g + 1)
                        dve.sem_inc(dve_tick, 1)
                        link(nc.vector.reciprocal(rc[0:P], sd[0:P]))
                        link(nc.vector.tensor_tensor(x2s[0:P, cols, :], cb[0:P], over(rc[0:P], F), ALU.mult))
                link.end(NG // 2)

            @block.tensor
            def _(pe):
                credit(pe, fm_turned, mult)
                with pe.Fori(0, NG // 2) as i:
                    for s in range(2):
                        g = i * 2 + s
                        pe.wait_ge(xt_made, done(g))
                        pe.wait_ge(fm_taken, free(g))
                        pe.sem_inc(pe_tick, 1)
                        for c in range(C):
                            last = nc.tensor.transpose(p_f[0:2 * F + 1, s, c * P:(c + 1) * P], xt[0:P, s, c], ident[0:P, 0:P])
                        last.then_inc(fm_turned, 1)
                        pe.wait_ge(fm_taken, done(g))
                        pe.wait_ge(used, free(g))
                        pe.sem_inc(pe_tick, 1)
                        for c in range(C):
                            last = nc.tensor.matmul(p_m[0:P, s, c * F:(c + 1) * F], xf[:, s, c * P:(c + 1) * P], w1e[:], start=True, stop=True)
                        last.then_inc(mult, 1)

            @block.scalar
            def _(act):
                credit(act, fm_taken)
                with act.Fori(0, NG // 2) as i:
                    for s in range(2):
                        g = i * 2 + s
                        act.wait_ge(fm_turned, done(g))
                        act.wait_ge(mult, free(g))
                        act.sem_inc(act_tick, 1)
                        nc.scalar.copy(xf[:, s], p_f[0:2 * F + 1, s, 0:PG]).then_inc(fm_taken, 1)
                        act.wait_ge(var_made, done(g))
                        act.sem_inc(act_tick, 1)
                        deviation(sd[0:P], va[0:P]).then_inc(dev_made, 1)

        for s in range(2):
            g_base[s] += NG // 2 * C * 16
        with Phase(nc) as ph:
            made, rooted = sem("n_made", ph), sem("n_rooted", ph)
            x2_stored = sem("x2_stored", ph)
            dlink = sem("n_link", ph)
            dg = sb("n_dg", [128, 2, T], F32, ph)
            some = sb("n_some", [128, 2, T], F32, ph)
            block = ph.open()

            @block.vector
            def _(dve):
                link = Links(dve, dlink)
                for k, d in enumerate((norm, dinv_t)):
                    nc.vector.tensor_scalar(some[0:P, k], d[0:P], 0.0, None, ALU.is_gt)
                    last = nc.vector.tensor_scalar(dg[0:P, k], d[0:P], TINY, None, ALU.max)
                last.then_inc(made, 1)
                dve.wait_ge(rooted, 1)
                link(nc.vector.reciprocal(dg[0:P], dg[0:P]))
                link(nc.vector.tensor_tensor(dg[0:P], dg[0:P], some[0:P], ALU.mult))
                link(nc.vector.tensor_tensor(norm[0:P], dg[0:P, 0], ew[0:P], ALU.mult))
                link(nc.vector.tensor_tensor(norm[0:P], norm[0:P], dg[0:P, 1], ALU.mult))

            @block.sync
            def _(sp):
                for tab, v in ((htab[2], x2t), (btab[2], x2s)):
                    sp.dma_start(tab.rearrange("(p t) f -> p t f", p=P)[:, :, F:2 * F], v[0:P]).then_inc(x2_stored, 16)
                sp.wait_ge(x2_stored, 32)

            @block.scalar
            def _(act):
                act.wait_ge(made, 1)
                nc.scalar.activation(dg[0:P], dg[0:P], ACT.Sqrt).then_inc(rooted, 1)

        hsp = sb("hsp", [128, T, H])
        for n in range(3):
            f, h, hp = fins[n], hs[n], hs[n - 1]
            W = K * h
            wide = F if n == 2 else 0
            with Phase(nc) as ph:
                nm = f"p{n}_"
                staged = [sem(f"{nm}staged{s}", ph) for s in range(2)]
                filled = [sem(f"{nm}filled{s}", ph) for s in range(2)]
                a_stored = [sem(f"{nm}a_stored{s}", ph) for s in range(2)]
                b_stored = [sem(f"{nm}b_stored{s}", ph) for s in range(2)]
                xs_made, turned, scanned, backed, a_taken, x_turned, x_taken, mult, relued, b_made = (
                    sem(nm + v, ph) for v in ("xs_made", "turned", "scanned", "backed", "a_taken", "x_turned",
                                              "x_taken", "mult", "relued", "b_made"))
                dlink = sem(nm + "link", ph)
                stg = sb(nm + "stg", [128, 2, C], I32, ph)
                gx = sb(nm + "gx", [128, 2, C, f], F32, ph)
                xs = sb(nm + "xs", [128, 2, C, f], F32, ph)
                xb = sb(nm + "xb", [128, 2, C, f + 1], F32, ph)
                sc = sb(nm + "sc", [f, 2, PG], F32, ph)
                arow = sb(nm + "arow", [128, 2, C, f], F32, ph)
                xf = sb(nm + "xf", [f + 1, 2, PG], F32, ph)
                hk = sb(nm + "hk", [128, 2, C, W], F32, ph)
                brow = sb(nm + "brow", [128, 2, C, h], F32, ph)
                p_t = pb(nm + "p_t", [128, 2, 512], ph)
                p_b = pb(nm + "p_b", [128, 512], ph)
                p_f = pb(nm + "p_f", [128, 512], ph)
                p_h = pb(nm + "p_h", [128, 2, 2, 512], ph)
                block = ph.open()

                @block.sync
                def _(sp):
                    if n == 0:
                        return
                    with sp.Fori(0, NG // 2) as i:
                        for s in range(2):
                            g = i * 2 + s
                            sp.wait_ge(xs_made, free(g))
                            sp.sem_inc(sp_tick, 1)
                            sp.dma_start(stg[0:P, s], slot_i[0:P, bass.ds(g * C, C)]).then_inc(staged[s], 16)
                            sp.dma_start(gx[0:P, s], rows(btab[n - 1], g)).then_inc(filled[s], 16)

                @block.gpsimd
                def _(pool):
                    if n == 0:
                        return
                    bound = pool.to_reg(E - 1)
                    with pool.Fori(0, NG // 2) as i:
                        for s in range(2):
                            pool.wait_ge(staged[s], (i + 1) * 16)
                            pool.wait_ge(filled[s], (i + 1) * 16)
                            pool.sem_inc(pool_tick, 1)
                            for c in range(C):
                                pool.indirect_dma_start(out=gx[0:P, s, c], out_offset=None, in_=htab[n - 1],
                                                        in_offset=bass.IndirectOffsetOnAxis(ap=stg[0:P, s, c:c + 1], axis=0),
                                                        bounds_check=bound, oob_is_err=False).then_inc(gathered[s], 16)

                @block.vector
                def _(dve):
                    link = Links(dve, dlink)
                    credit(dve, xs_made, scanned, b_made)
                    for s in range(2):
                        nc.vector.memset(xb[:, s, :, f:f + 1], 1.0)
                    link(nc.vector.memset(sc[:, 1, PG - 1:PG], 0.0))
                    link.base = 1

                    def inputs(g, s, k):
                        cols = bass.ds(g * C, C)
                        dve.wait_ge(turned, free(g))
                        dve.wait_ge(x_turned, free(g))
                        dve.sem_inc(dve_tick, 1)
                        if n:
                            dve.wait_ge(gathered[s], (k + 1) * C * 16 + g_base[s])
                            dve.sem_inc(dve_tick, 1)
                        x_in = gx[0:P, s] if n else x2s[0:P, cols, :]
                        nm_b = over(norm[0:P, cols], f)
                        nc.vector.tensor_scalar(xb[0:P, s, :, 0:f], x_in, 1.0, None, ALU.mult)
                        if n:
                            nc.vector.tensor_tensor(hsp[0:P, cols, :], x_in, nm_b, ALU.mult)
                        nc.vector.tensor_tensor(xs[0:P, s], x_in, nm_b, ALU.mult).then_inc(xs_made, 1)

                    def body(g, s, k, new, old, more):
                        if not old:
                            inputs(g, s, k)
                        if more:
                            inputs(g + 1, 1 - s, k + s)
                        if new:
                            dve.wait_ge(turned, done(g))
                            dve.wait_ge(backed, free(g))
                            dve.sem_inc(dve_tick, 1)
                            link(nc.vector.tensor_tensor_scan(sc[:, s], same_b[0:f, bass.ds(g * PG, PG)], p_t[0:f, s, 0:PG],
                                                              sc[:, 1 - s, PG - 1:PG], ALU.mult, ALU.add))
                            dve.sem_inc(scanned, 1)
                        if old:
                            o = 1 - s
                            dve.wait_ge(relued, done(g - 1))
                            dve.wait_ge(b_stored[o], (k + s) * 16)
                            dve.sem_inc(dve_tick, 1)
                            link(nc.vector.tensor_tensor(brow[0:P, o], hk[0:P, o, :, 0:h], hk[0:P, o, :, h:2 * h], ALU.add))
                            nc.vector.tensor_tensor(brow[0:P, o], brow[0:P, o], hk[0:P, o, :, 2 * h:3 * h], ALU.add).then_inc(b_made, 1)

                    skewed(dve, NG, body, link, lambda new, old, more: new + old)

                @block.tensor
                def _(pe):
                    credit(pe, turned, backed, x_turned, mult)

                    def body(g, s, k, new, old, more):
                        if new:
                            pe.wait_ge(xs_made, done(g))
                            pe.wait_ge(scanned, free(g))
                            pe.wait_ge(x_taken, free1(g))
                            pe.sem_inc(pe_tick, 1)
                            for c in range(C):
                                last = nc.tensor.transpose(p_f[0:f + 1, c * P:(c + 1) * P], xb[0:P, s, c], ident[0:P, 0:P])
                            last.then_inc(x_turned, 1)
                            for c in range(C):
                                last = nc.tensor.transpose(p_t[0:f, s, c * P:(c + 1) * P], xs[0:P, s, c], ident[0:P, 0:P])
                            last.then_inc(turned, 1)
                        if old:
                            pe.wait_ge(scanned, done(g - 1))
                            if not (isinstance(g, int) and g == 1):
                                pe.wait_ge(a_taken, free1(g - 1))
                            pe.sem_inc(pe_tick, 1)
                            for c in range(C):
                                last = nc.tensor.transpose(p_b[0:P, c * f:(c + 1) * f], sc[:, 1 - s, c * P:(c + 1) * P], ident[0:f, 0:f])
                            last.then_inc(backed, 1)
                        if new:
                            pe.wait_ge(x_taken, done(g))
                            pe.wait_ge(relued, free(g))
                            pe.sem_inc(pe_tick, 1)
                            for c in range(C):
                                last = nc.tensor.matmul(p_h[0:P, s, c // 2, c % 2 * W:(c % 2 + 1) * W], xf[:, s, c * P:(c + 1) * P],
                                                        wroot1[n][:], start=True, stop=True)
                            last.then_inc(mult, 1)

                    skewed(pe, NG, body)

                @block.scalar
                def _(act):
                    credit(act, a_taken, x_taken, relued)
                    for s in range(2):
                        act.sem_inc(a_stored[s], 16)
                        act.sem_inc(b_stored[s], 16)

                    def store_b(q, s):
                        act.wait_ge(b_made, done(q))
                        act.sem_inc(act_tick, 1)
                        act.dma_start(rows(btab[n], q)[:, :, 0:h], brow[0:P, s]).then_inc(b_stored[s], 16)

                    def body(g, s, k, new, old, more):
                        o = 1 - s
                        if new:
                            act.wait_ge(x_turned, done(g))
                            act.wait_ge(mult, free(g))
                            act.sem_inc(act_tick, 1)
                            nc.scalar.copy(xf[:, s], p_f[0:f + 1, 0:PG]).then_inc(x_taken, 1)
                        if old:
                            act.wait_ge(backed, done(g - 1))
                            act.wait_ge(a_stored[o], (k + s) * 16)
                            act.sem_inc(act_tick, 1)
                            nc.scalar.copy(arow[0:P, o], p_b[0:P, 0:C * f].rearrange("p (c f) -> p c f", c=C)).then_inc(a_taken, 1)
                        if new:
                            act.wait_ge(mult, done(g))
                            act.wait_ge(b_made, free(g))
                            act.sem_inc(act_tick, 1)
                            nc.scalar.activation(hk[0:P, s].rearrange("p (b c) w -> p b (c w)", b=2), p_h[0:P, s, :, 0:2 * W],
                                                 ACT.Relu).then_inc(relued, 1)
                        if old:
                            act.wait_ge(a_taken, done(g - 1))
                            act.sem_inc(act_tick, 1)
                            act.dma_start(rows(atab[n], g - 1), arow[0:P, o]).then_inc(a_stored[o], 16)
                            store_b(g - 1, o)

                    skewed(act, NG, body)
                    for s in range(2):
                        act.wait_ge(a_stored[s], (NG // 2 + 1) * 16)
                        act.wait_ge(b_stored[s], (NG // 2 + 1) * 16)

            if n:
                for s in range(2):
                    g_base[s] += NG // 2 * C * 16
            with Phase(nc) as ph:
                nm = f"e{n}_"
                M1 = 2 * h if h == H else W
                parts = [(0, M1)] + ([(M1, h)] if h == H else [])
                fx = (2 * F + 1) if n == 0 else f + 1
                staged = [sem(f"{nm}staged{s}", ph) for s in range(2)]
                t_loaded = [sem(f"{nm}t_loaded{s}", ph) for s in range(2)]
                h_stored = [sem(f"{nm}h_stored{s}", ph) for s in range(2)]
                xa_made, a_turned, t_turned, a_taken, t_taken, msg, relu0, scanned, mult, relued, h_made = (
                    sem(nm + v, ph) for v in ("xa_made", "a_turned", "t_turned", "a_taken", "t_taken", "msg", "relu0",
                                              "scanned", "mult", "relued", "h_made"))
                s_turned, s_taken = sem(nm + "s_turned", ph), sem(nm + "s_taken", ph)
                dlink = sem(nm + "link", ph)
                stg = sb(nm + "stg", [128, 2, C], I32, ph)
                ga = sb(nm + "ga", [128, 2, C, f], F32, ph)
                xa = sb(nm + "xa", [128, 2, C, fx], F32, ph)
                xh = sb(nm + "xh", [128, 2, C, f], F32, ph) if n else None
                xt = sb(nm + "xt", [128, 2, C, f + 1], F32, ph)
                fa = sb(nm + "fa", [fx, 2, PG], F32, ph)
                fh = sb(nm + "fh", [f, 2, PG], F32, ph) if n else None
                ft = sb(nm + "ft", [f + 1, 2, PG], F32, ph)
                m = [sb(f"{nm}m{k}", [w, PG], F32, ph) for k, (_, w) in enumerate(parts)]
                sc = [sb(f"{nm}sc{k}", [w, 2, PG], F32, ph) for k, (_, w) in enumerate(parts)]
                hk = sb(nm + "hk", [128, 2, C, W], F32, ph)
                hrow = sb(nm + "hrow", [128, 2, C, h], F32, ph)
                p_x = pb(nm + "p_x", [128, 2, 512], ph)
                p_o = [pb(f"{nm}p_o{k}", [128, 512], ph) for k in range(2)]
                p_h = pb(nm + "p_h", [128, 2, 2, 512], ph)
                block = ph.open()

                @block.sync
                def _(sp):
                    with sp.Fori(0, NG // 2) as i:
                        for s in range(2):
                            g = i * 2 + s
                            sp.wait_ge(xa_made, free(g))
                            sp.sem_inc(sp_tick, 1)
                            sp.dma_start(stg[0:P, s], slot_i[0:P, bass.ds(g * C, C)]).then_inc(staged[s], 16)
                            if n:
                                sp.wait_ge(t_turned, free(g))
                                sp.sem_inc(sp_tick, 1)
                                sp.dma_start(xt[0:P, s, :, 0:f], rows(htab[n - 1], g)).then_inc(t_loaded[s], 16)

                @block.gpsimd
                def _(pool):
                    with pool.Fori(0, NG // 2) as i:
                        for s in range(2):
                            g = i * 2 + s
                            pool.wait_ge(staged[s], (i + 1) * 16)
                            pool.wait_ge(xa_made, free(g))
                            pool.sem_inc(pool_tick, 1)
                            for c in range(C):
                                pool.indirect_dma_start(out=ga[0:P, s, c], out_offset=None, in_=atab[n],
                                                        in_offset=bass.IndirectOffsetOnAxis(ap=stg[0:P, s, c:c + 1], axis=0)
                                                        ).then_inc(gathered[s], 16)

                @block.vector
                def _(dve):
                    link = Links(dve, dlink)
                    credit(dve, xa_made, scanned, h_made)
                    for s in range(2):
                        nc.vector.memset(xt[:, s, :, f:f + 1], 1.0)
                    for k in range(len(parts)):
                        link(nc.vector.memset(sc[k][:, 1, PG - 1:PG], 0.0))
                    link.base = len(parts)

                    def inputs(g, s, k):
                        cols = bass.ds(g * C, C)
                        dve.wait_ge(gathered[s], (k + 1) * C * 16 + g_base[s])
                        dve.wait_ge(a_turned, free(g))
                        dve.wait_ge(s_turned if n else t_turned, free(g))
                        dve.sem_inc(dve_tick, 1)
                        nm_b = norm[0:P, cols]
                        if n == 0:
                            nc.vector.tensor_tensor(xa[0:P, s, :, 0:F], x2s[0:P, cols, :], over(nm_b, F), ALU.mult)
                            nc.vector.tensor_scalar(xt[0:P, s, :, 0:F], x2t[0:P, cols, :], 1.0, None, ALU.mult)
                        else:
                            nc.vector.tensor_scalar(xh[0:P, s], hsp[0:P, cols, :], 1.0, None, ALU.mult)
                        nc.vector.tensor_scalar(xa[0:P, s, :, fx - 1], nm_b, 1.0, None, ALU.mult)
                        nc.vector.tensor_tensor(xa[0:P, s, :, fx - 1 - f:fx - 1], ga[0:P, s], over(nm_b, f), ALU.mult).then_inc(xa_made, 1)

                    def body(g, s, k, new, old, more):
                        if not old:
                            inputs(g, s, k)
                        if more:
                            inputs(g + 1, 1 - s, k + s)
                        if old:
                            o = 1 - s
                            dve.wait_ge(relued, done(g - 1))
                            dve.wait_ge(h_stored[o], (k + s) * 16)
                            dve.sem_inc(dve_tick, 1)
                            link(nc.vector.tensor_tensor(hrow[0:P, o], hk[0:P, o, :, 0:h], hk[0:P, o, :, h:2 * h], ALU.add))
                            nc.vector.tensor_tensor(hrow[0:P, o], hrow[0:P, o], hk[0:P, o, :, 2 * h:3 * h], ALU.add).then_inc(h_made, 1)
                        if new:
                            dve.wait_ge(relu0, done(g))
                            dve.wait_ge(mult, free(g))
                            dve.sem_inc(dve_tick, 1)
                            for q, (_, w) in enumerate(parts):
                                link(nc.vector.tensor_tensor_scan(sc[q][:, s], same_b[0:w, bass.ds(g * PG, PG)], m[q][:],
                                                                  sc[q][:, 1 - s, PG - 1:PG], ALU.mult, ALU.add))
                            dve.sem_inc(scanned, 1)

                    skewed(dve, NG, body, link, lambda new, old, more: new * len(parts) + old)

                @block.tensor
                def _(pe):
                    credit(pe, a_turned, t_turned, s_turned, msg, mult)

                    def body(g, s, k, new, old, more):
                        if new:
                            pe.wait_ge(xa_made, done(g))
                            pe.wait_ge(s_taken if n else a_taken, free1(g))
                            pe.sem_inc(pe_tick, 1)
                            for c in range(C):
                                last = nc.tensor.transpose(p_x[0:fx, 0, c * P:(c + 1) * P], xa[0:P, s, c], ident[0:P, 0:P])
                            last.then_inc(a_turned, 1)
                            pe.wait_ge(t_taken, free1(g))
                            if n:
                                pe.wait_ge(t_loaded[s], (k + 1) * 16)
                            pe.sem_inc(pe_tick, 1)
                            for c in range(C):
                                last = nc.tensor.transpose(p_x[0:f + 1, 1, c * P:(c + 1) * P], xt[0:P, s, c], ident[0:P, 0:P])
                            last.then_inc(t_turned, 1)
                            if n:
                                pe.wait_ge(a_taken, done(g))
                                pe.sem_inc(pe_tick, 1)
                                for c in range(C):
                                    last = nc.tensor.transpose(p_x[0:f, 0, c * P:(c + 1) * P], xh[0:P, s, c], ident[0:P, 0:P])
                                last.then_inc(s_turned, 1)
                        if old:
                            o = 1 - s
                            pe.wait_ge(t_taken, done(g - 1))
                            pe.wait_ge(scanned, done(g - 1))
                            if not (isinstance(g, int) and g == 1):
                                pe.wait_ge(relued, free(g - 1))
                            pe.sem_inc(pe_tick, 1)
                            for c in range(C):
                                for q, (b, w) in enumerate(parts):
                                    to = p_h[0:P, o, c // 2, c % 2 * W + b:c % 2 * W + b + w]
                                    nc.tensor.matmul(to, ft[:, o, c * P:(c + 1) * P], wroot1[n][:, b:b + w], start=True, stop=False)
                                    last = nc.tensor.matmul(to, sc[q][:, o, c * P:(c + 1) * P], wblk[n][q][:], start=False, stop=True)
                            last.then_inc(mult, 1)
                        if new:
                            pe.wait_ge(s_taken if n else a_taken, done(g))
                            pe.wait_ge(relu0, free1(g))
                            pe.sem_inc(pe_tick, 1)
                            for q, (b, w) in enumerate(parts):
                                if n:
                                    nc.tensor.matmul(p_o[q][0:w, 0:PG], wroot0[n][:, b:b + w], fh[:, s], start=True, stop=False)
                                last = nc.tensor.matmul(p_o[q][0:w, 0:PG], wbias[n][:, b:b + w], fa[:, s], start=(n == 0), stop=True)
                            last.then_inc(msg, 1)

                    skewed(pe, NG, body)

                @block.scalar
                def _(act):
                    credit(act, a_taken, t_taken, s_taken, relu0, relued)
                    for s in range(2):
                        act.sem_inc(h_stored[s], 16)

                    def store(q, s):
                        act.wait_ge(h_made, done(q))
                        act.sem_inc(act_tick, 1)
                        act.dma_start(rows(htab[n], q)[:, :, 0:h], hrow[0:P, s]).then_inc(h_stored[s], 16)

                    def body(g, s, k, new, old, more):
                        o = 1 - s
                        if new:
                            act.wait_ge(a_turned, done(g))
                            act.wait_ge(msg, free(g))
                            act.sem_inc(act_tick, 1)
                            nc.scalar.copy(fa[:, s], p_x[0:fx, 0, 0:PG]).then_inc(a_taken, 1)
                            act.wait_ge(t_turned, done(g))
                            act.wait_ge(mult, free(g))
                            act.sem_inc(act_tick, 1)
                            nc.scalar.copy(ft[:, s], p_x[0:f + 1, 1, 0:PG]).then_inc(t_taken, 1)
                            if n:
                                act.wait_ge(s_turned, done(g))
                                act.sem_inc(act_tick, 1)
                                nc.scalar.copy(fh[:, s], p_x[0:f, 0, 0:PG]).then_inc(s_taken, 1)
                        if old:
                            act.wait_ge(mult, done(g - 1))
                            if not (isinstance(g, int) and g == 1):
                                act.wait_ge(h_made, free(g - 1))
                            act.sem_inc(act_tick, 1)
                            nc.scalar.activation(hk[0:P, o].rearrange("p (b c) w -> p b (c w)", b=2), p_h[0:P, o, :, 0:2 * W],
                                                 ACT.Relu).then_inc(relued, 1)
                        if new:
                            act.wait_ge(msg, done(g))
                            act.wait_ge(scanned, free1(g))
                            act.sem_inc(act_tick, 1)
                            for q, (_, w) in enumerate(parts):
                                last = nc.scalar.activation(m[q][:], p_o[q][0:w, 0:PG], ACT.Relu)
                            last.then_inc(relu0, 1)
                        if old:
                            store(g - 1, o)

                    skewed(act, NG, body)
                    for s in range(2):
                        act.wait_ge(h_stored[s], (NG // 2 + 1) * 16)

            for s in range(2):
                g_base[s] += NG // 2 * C * 16
        with Phase(nc) as ph:
            loaded = [sem(f"d_loaded{s}", ph) for s in range(2)]
            stored = [sem(f"d_stored{s}", ph) for s in range(2)]
            new_made, old_made, turned, taken, mult, relued, summed, var_made, dev_made, read, out_made = (
                sem("d_" + v, ph) for v in ("new_made", "old_made", "turned", "taken", "mult", "relued", "summed", "var_made",
                                            "dev_made", "read", "out_made"))
            dlink = sem("d_link", ph)
            R = SUB * C
            yt = sb("d_yt", [128, 2, R, F], F32, ph)
            sl = sb("d_sl", [128, 2, R], I32, ph)
            cb = sb("d_cb", [128, R, F], F32, ph)
            sq = sb("d_sq", [128, R, F], F32, ph)
            sm, va, sd, rc = (sb(f"d_{v}", [128, R], F32, ph) for v in ("sm", "va", "sd", "rc"))
            no_edge = sb("d_no_edge", [128, 2, R], F32, ph)
            u = sb("d_u", [128, R, F], F32, ph)
            x1 = sb("d_x1", [128, R, F], F32, ph)
            x2 = sb("d_x2", [128, 2, R, F], F32, ph)
            h12 = [sb(f"d_h{k}", [128, R, H], F32, ph) for k in (1, 2)]
            h3 = sb("d_h3", [128, 2, R, F], F32, ph)
            hm, hm2 = (sb(f"d_{v}", [128, R, F], F32, ph) for v in ("hm", "hm2"))
            acc = sb("d_acc", [128, 2, R, F], F32, ph)
            xf = [sb("d_xf0", [F + 1, SUB, PG], F32, ph), sb("d_xf1", [H + 1, SUB, PG], F32, ph)]
            hk = sb("d_hk", [128, 2, C, K * H], F32, ph)
            p_t = pb("d_p_t", [128, 2, 512], ph)
            p_m = pb("d_p_m", [128, 2, 2, 512], ph)
            block = ph.open()
            Q = 4 * SUB
            ems = (x1, x2, h12[0], h12[1])
            wts = (w1d, wroot1[0], wroot1[1], wroot1[2])

            @block.sync
            def _(sp):
                with sp.Fori(0, ND // 2) as i:
                    for s in range(2):
                        g = i * 2 + s
                        sp.wait_ge(read, free(g))
                        sp.sem_inc(sp_tick, 1)
                        sp.dma_start(yt[0:P, s], nodes(ytab, g)).then_inc(loaded[s], 16)
                        sp.dma_start(sl[0:P, s].unsqueeze(2), nodes(slot_tab, g)).then_inc(loaded[s], 16)

            L1, CONV1, CONV2, CONV3 = range(4)

            def items(new, old):
                seq = [it for j in range(SUB) for it in (((L1, j),) if new else ()) + (((CONV2, j),) if old else ())]
                return seq + [(CONV3, j) for j in range(SUB) if old] + [(CONV1, j) for j in range(SUB) if new]

            def bodies(eng, body):
                at = lambda g: g * Q - Q // 2
                body(0, 0, 0, 0, True, False, True)
                with eng.Fori(0, ND // 2 - 1) as i:
                    body(i * 2 + 1, 1, i, at(i * 2 + 1), True, True, True)
                    body(i * 2 + 2, 0, i + 1, at(i * 2 + 2), True, True, True)
                body(ND - 1, 1, ND // 2 - 1, at(ND - 1), True, True, False)
                body(ND, 0, ND // 2, at(ND), False, True, False)

            @block.vector
            def _(dve):
                link = Links(dve, dlink)
                credit(dve, read, summed, out_made)
                nc.vector.memset(xf[0][F:F + 1], 1.0)
                nc.vector.memset(xf[1][H:H + 1], 1.0)
                link(nc.vector.memset(acc[:], 0.0))
                link.base = 1

                def first_norm(g, s, k):
                    dve.wait_ge(loaded[s], (k + 1) * 32)
                    dve.sem_inc(dve_tick, 1)
                    nc.vector.tensor_scalar(no_edge[0:P, s], sl[0:P, s], float(NIL), None, ALU.is_equal)
                    center(link, cb[0:P], sm[0:P], sq[0:P], va[0:P], yt[0:P, s]).then_inc(var_made, 1)
                    dve.sem_inc(read, 1)
                    dve.wait_ge(dev_made, g * 2 + 1)
                    dve.sem_inc(dve_tick, 1)
                    link(nc.vector.reciprocal(rc[0:P], sd[0:P]))
                    nc.vector.tensor_tensor(x1[0:P], cb[0:P], over(rc[0:P], F), ALU.mult).then_inc(new_made, SUB)

                def second_norm(g, s, k, items_done):
                    dve.wait_ge(summed, items_done + LEAD)
                    dve.wait_ge(stored[s], (k + 1) * 32)
                    dve.sem_inc(dve_tick, 1)
                    center(link, cb[0:P], sm[0:P], sq[0:P], va[0:P], u[0:P]).then_inc(var_made, 1)
                    dve.wait_ge(dev_made, g * 2 + 2)
                    dve.sem_inc(dve_tick, 1)
                    link(nc.vector.reciprocal(rc[0:P], sd[0:P]))
                    nc.vector.tensor_tensor(x2[0:P, s], cb[0:P], over(rc[0:P], F), ALU.mult).then_inc(new_made, SUB)

                def batch_sums(s, items_done):
                    dve.wait_ge(summed, items_done + LEAD)
                    dve.sem_inc(dve_tick, 1)
                    dve.sem_inc(out_made, 1)
                    link(nc.vector.tensor_tensor(hm[0:P], h3[0:P, s], over(no_edge[0:P, s], F), ALU.mult))
                    nc.vector.tensor_tensor(acc[0:P, 0], acc[0:P, 0], hm[0:P], ALU.add)
                    link(nc.vector.tensor_tensor(hm2[0:P], hm[0:P], h3[0:P, s], ALU.mult))
                    link(nc.vector.tensor_tensor(acc[0:P, 1], acc[0:P, 1], hm2[0:P], ALU.add))

                def body(g, s, k, before, new, old, more):
                    seq = items(new, old)
                    if isinstance(g, int):
                        link.turn(0, 8 * new + SUB * (new + 2 * old) + 3 * old - 4 * (new and not more) + 4 * (not old))
                    if not old:
                        first_norm(g, s, k)
                    for m, (step, j) in enumerate(seq):
                        if new and m == (2 * SUB if old else SUB):
                            second_norm(g, s, k, before + m)
                        if new and m == len(seq) - SUB:
                            if old:
                                batch_sums(1 - s, before + m)
                            if more:
                                first_norm(g + 1, 1 - s, k + s)
                        cs = slice(j * C, (j + 1) * C)
                        dve.wait_ge(relued, before + m + 1 + LEAD)
                        dve.sem_inc(dve_tick, 1)
                        if step == L1:
                            nc.vector.tensor_tensor(u[0:P, cs], hk[0:P, m % 2, :, 0:F], x1[0:P, cs], ALU.add).then_inc(summed, 1)
                            continue
                        h = hs[step - 1]
                        to = h3[:, 1 - s] if step == CONV3 else h12[step - 1]
                        a3 = [hk[0:P, m % 2, :, b * h:(b + 1) * h] for b in range(3)]
                        link(nc.vector.tensor_tensor(to[0:P, cs], a3[0], a3[1], ALU.add))
                        nc.vector.tensor_tensor(to[0:P, cs], to[0:P, cs], a3[2], ALU.add).then_inc(summed, 1)
                        if step != CONV3:
                            dve.wait_ge(summed, before + m + 1 + LEAD)
                            dve.sem_inc(old_made, 1)
                    if not new:
                        batch_sums(1 - s, before + len(seq))
                    if isinstance(g, int):
                        link.end(1)

                def looped(g, s, k, before, new, old, more):
                    if not isinstance(g, int) and s == 1:
                        link.turn(k, 2 * 23)
                    body(g, s, k, before, new, old, more)
                    if not isinstance(g, int) and s == 0:
                        link.end(ND // 2 - 1)

                bodies(dve, looped)
                for k in range(2):
                    last = nc.vector.reduce_sum(stat[0:P, k], acc[0:P, k].rearrange("p n f -> p f n"), AX)

            @block.tensor
            def _(pe):
                credit(pe, turned, mult)

                def turn(g, s, before, m, step, j):
                    f = F if step < CONV2 else H
                    em = x2[:, s] if step == CONV1 else ems[step]
                    if step < CONV2:
                        pe.wait_ge(new_made, g * 2 * SUB + step * SUB + j + 1)
                    else:
                        pe.wait_ge(old_made, (g - 1) * 2 * SUB + (step - CONV2) * SUB + j + 1)
                    pe.wait_ge(taken, before + m - 1 + LEAD)
                    pe.sem_inc(pe_tick, 1)
                    for c in range(C):
                        last = nc.tensor.transpose(p_t[0:f, m % 2, c * P:(c + 1) * P], em[0:P, j * C + c], ident[0:P, 0:P])
                    last.then_inc(turned, 1)

                def product(before, m, step, j):
                    W = F if step == L1 else K * hs[step - 1]
                    pe.wait_ge(taken, before + m + 1 + LEAD)
                    pe.wait_ge(relued, before + m - 1 + LEAD)
                    pe.sem_inc(pe_tick, 1)
                    for c in range(C):
                        last = nc.tensor.matmul(p_m[0:P, m % 2, c // 2, c % 2 * W:(c % 2 + 1) * W],
                                                xf[step // 2][:, j, c * P:(c + 1) * P], wts[step][:], start=True, stop=True)
                    last.then_inc(mult, 1)

                def body(g, s, k, before, new, old, more):
                    seq = items(new, old)
                    for m, (step, j) in enumerate(seq):
                        if m == SUB and not old:
                            product(before, m - 1, *seq[m - 1])
                        turn(g, s, before, m, step, j)
                        if m and not (m == SUB and not old):
                            product(before, m - 1, *seq[m - 1])
                    product(before, len(seq) - 1, *seq[-1])

                bodies(pe, body)

            @block.scalar
            def _(act):
                credit(act, taken, relued)
                for s in range(2):
                    act.sem_inc(stored[s], 32)

                def take(before, m, step, j):
                    f = F if step < CONV2 else H
                    act.wait_ge(turned, before + m + 1 + LEAD)
                    act.sem_inc(act_tick, 1)
                    nc.scalar.copy(xf[step // 2][0:f, j], p_t[0:f, m % 2, 0:PG]).then_inc(taken, 1)

                def relu(before, m, step, j):
                    W = F if step == L1 else K * hs[step - 1]
                    act.wait_ge(mult, before + m + 1 + LEAD)
                    act.wait_ge(summed, before + m - 1 + LEAD)
                    act.sem_inc(act_tick, 1)
                    nc.scalar.activation(hk[0:P, m % 2].rearrange("p (b c) w -> p b c w", b=2)[:, :, :, 0:W],
                                         p_m[0:P, m % 2, :, 0:2 * W].rearrange("p b (c w) -> p b c w", c=2), ACT.Relu).then_inc(relued, 1)

                def norm_deviation(n):
                    act.wait_ge(var_made, n)
                    act.sem_inc(act_tick, 1)
                    deviation(sd[0:P], va[0:P]).then_inc(dev_made, 1)

                def store(g, s):
                    act.wait_ge(out_made, g + LEAD)
                    act.sem_inc(act_tick, 1)
                    act.dma_start(nodes(x2d, g - 1), x2[0:P, 1 - s]).then_inc(stored[1 - s], 16)
                    act.dma_start(nodes(h3d, g - 1), h3[0:P, 1 - s]).then_inc(stored[1 - s], 16)

                def body(g, s, k, before, new, old, more):
                    seq = items(new, old)
                    if not old:
                        norm_deviation(1)
                    for m, it in enumerate(seq):
                        if m == SUB and not old:
                            relu(before, m - 1, *seq[m - 1])
                            norm_deviation(2)
                            norm_deviation(3)
                        take(before, m, *it)
                        if m and not (m == SUB and not old):
                            relu(before, m - 1, *seq[m - 1])
                        if new and old and m == 2 * SUB + 1:
                            norm_deviation(g * 2 + 2)
                        if new and old and m == 3 * SUB + 1:
                            store(g, s)
                            if more:
                                norm_deviation(g * 2 + 3)
                    relu(before, len(seq) - 1, *seq[-1])
                    if not new:
                        store(g, s)

                bodies(act, body)
                for s in range(2):
                    act.wait_ge(stored[s], (ND // 2 + 1) * 32)

        with Phase(nc) as ph:
            loaded, summed, dev, multd, dlink = (sem("b_" + v, ph) for v in ("loaded", "summed", "dev", "mult", "link"))
            h3t = sb("b_h3t", [128, T, F], F32, ph)
            last_m = sb("b_last_m", [128, T], F32, ph)
            part = sb("b_part", [128, 2, F], F32, ph)
            tot = sb("b_tot", [128, 2, F], F32, ph)
            p_s = pb("b_p_s", [128, 512], ph)
            block = ph.open()

            @block.sync
            def _(sp):
                sp.dma_start(h3t[0:P], htab[2].rearrange("(p t) f -> p t f", p=P)[:, :, 0:F]).then_inc(loaded, 16)

            @block.vector
            def _(dve):
                link = Links(dve, dlink)
                flat = lambda v: v.rearrange("p k f -> p (k f)")
                link(nc.vector.tensor_scalar(last_m[0:P], last_i[0:P], float(N), None, ALU.is_lt))
                dve.wait_ge(loaded, 16)
                link(nc.vector.tensor_tensor(hsp[0:P, :, 0:F], h3t[0:P], over(last_m[0:P], F), ALU.mult))
                link(nc.vector.tensor_tensor(hsp[0:P, :, F:2 * F], hsp[0:P, :, 0:F], h3t[0:P], ALU.mult))
                for k in range(2):
                    last = nc.vector.reduce_sum(part[0:P, k], hsp[0:P, :, k * F:(k + 1) * F].rearrange("p t f -> p f t"), AX)
                link(last)
                nc.vector.tensor_tensor(flat(part[0:P]), flat(part[0:P]), flat(stat[0:P]), ALU.add).then_inc(summed, 1)
                dve.wait_ge(multd, 1)
                link(nc.vector.tensor_scalar(flat(tot[:]), p_s[:, 0:2 * F], 1.0 / N, None, ALU.mult))
                link(nc.vector.tensor_tensor(part[:, 0], tot[:, 0], tot[:, 0], ALU.mult))
                link(nc.vector.tensor_tensor(tot[:, 1], tot[:, 1], part[:, 0], ALU.subtract))
                nc.vector.tensor_scalar(tot[:, 1], tot[:, 1], 0.0, None, ALU.max).then_inc(summed, 1)
                dve.wait_ge(dev, 1)
                link(nc.vector.reciprocal(part[:, 1], part[:, 1]))
                link(nc.vector.tensor_tensor(stat[:, 0], part[:, 1], gamma[:], ALU.mult))
                link(nc.vector.tensor_tensor(part[:, 0], stat[:, 0], tot[:, 0], ALU.mult))
                link(nc.vector.tensor_tensor(stat[:, 1], beta[:], part[:, 0], ALU.subtract))

            @block.tensor
            def _(pe):
                pe.wait_ge(summed, 1)
                nc.tensor.matmul(p_s[:, 0:2 * F], ones[0:P, :], part[0:P].rearrange("p k f -> p (k f)"), start=True, stop=True).then_inc(multd, 1)

            @block.scalar
            def _(act):
                act.wait_ge(summed, 2)
                nc.scalar.activation(part[:, 1], tot[:, 1], ACT.Sqrt, bias=epsc[:, 0:1]).then_inc(dev, 1)

        def bn(link, t, h, n):
            row = lambda k: stat[0:P, k].unsqueeze(1).broadcast_to([P, n, F])
            link(nc.vector.tensor_tensor(t, h, row(0), ALU.mult))
            link(nc.vector.tensor_tensor(t, t, row(1), ALU.add))

        with Phase(nc) as ph:
            loaded = [sem(f"f_loaded{s}", ph) for s in range(2)]
            stored = [sem(f"f_stored{s}", ph) for s in range(2)]
            var_made, dev_made, read, out_made, dlink = (sem("f_" + v, ph) for v in ("var_made", "dev_made", "read", "out_made", "link"))
            R = SUB * C
            xin = sb("f_xin", [128, 2, R, F], F32, ph)
            hin = sb("f_hin", [128, 2, R, F], F32, ph)
            cb = sb("f_cb", [128, R, F], F32, ph)
            sq = sb("f_sq", [128, R, F], F32, ph)
            sm, va, sd, rc = (sb(f"f_{v}", [128, R], F32, ph) for v in ("sm", "va", "sd", "rc"))
            u = sb("f_u", [128, R, F], F32, ph)
            xo = sb("f_xo", [128, 2, R, F], F32, ph)
            block = ph.open()

            @block.sync
            def _(sp):
                with sp.Fori(0, ND // 2) as i:
                    for s in range(2):
                        g = i * 2 + s
                        sp.wait_ge(read, free(g))
                        sp.sem_inc(sp_tick, 1)
                        sp.dma_start(xin[0:P, s], nodes(x2d, g)).then_inc(loaded[s], 16)
                        sp.dma_start(hin[0:P, s], nodes(h3d, g)).then_inc(loaded[s], 16)

            @block.vector
            def _(dve):
                link = Links(dve, dlink)
                credit(dve, read)
                with dve.Fori(0, ND // 2) as i:
                    link.turn(i, 2 * 12)
                    for s in range(2):
                        g = i * 2 + s
                        dve.wait_ge(loaded[s], (i + 1) * 32)
                        dve.sem_inc(dve_tick, 1)
                        bn(link, u[0:P], hin[0:P, s], R)
                        link(nc.vector.scalar_tensor_tensor(u[0:P], u[0:P], 0.0, xin[0:P, s], ALU.max, ALU.add))
                        dve.sem_inc(read, 1)
                        center(link, cb[0:P], sm[0:P], sq[0:P], va[0:P], u[0:P]).then_inc(var_made, 1)
                        dve.wait_ge(dev_made, g * 2 + 1)
                        dve.wait_ge(stored[s], (i + 1) * 16)
                        dve.sem_inc(dve_tick, 1)
                        link(nc.vector.reciprocal(rc[0:P], sd[0:P]))
                        link(nc.vector.tensor_tensor(u[0:P], cb[0:P], over(rc[0:P], F), ALU.mult))
                        center(link, cb[0:P], sm[0:P], sq[0:P], va[0:P], u[0:P]).then_inc(var_made, 1)
                        dve.wait_ge(dev_made, g * 2 + 2)
                        dve.sem_inc(dve_tick, 1)
                        link(nc.vector.reciprocal(rc[0:P], sd[0:P]))
                        nc.vector.tensor_tensor(xo[0:P, s], cb[0:P], over(rc[0:P], F), ALU.mult).then_inc(out_made, 1)
                link.end(ND // 2)

            @block.scalar
            def _(act):
                for s in range(2):
                    act.sem_inc(stored[s], 16)
                with act.Fori(0, ND // 2) as i:
                    for s in range(2):
                        g = i * 2 + s
                        for k in range(2):
                            act.wait_ge(var_made, g * 2 + k + 1)
                            act.sem_inc(act_tick, 1)
                            deviation(sd[0:P], va[0:P]).then_inc(dev_made, 1)
                        act.wait_ge(out_made, g + 1)
                        act.sem_inc(act_tick, 1)
                        act.dma_start(nodes(out, g), xo[0:P, s]).then_inc(stored[s], 16)
                for s in range(2):
                    act.wait_ge(stored[s], (ND // 2 + 1) * 16)

        s_base = T * 16
        with Phase(nc) as ph:
            staged = [sem(f"j_staged{s}", ph) for s in range(2)]
            filled = [sem(f"j_filled{s}", ph) for s in range(2)]
            attrs = [sem(f"j_attrs{s}", ph) for s in range(2)]
            (var_made, dev_made, x3_made, e_turned, e_taken, hid, h_taken, w_mult, w_used, out_sum, tanhed, f_made,
             f_turned, scanned, backed, u_made, x4_made, placed, read) = (
                sem("j_" + v, ph) for v in ("var_made", "dev_made", "x3_made", "e_turned", "e_taken", "hid", "h_taken",
                                            "w_mult", "w_used", "out_sum", "tanhed", "f_made", "f_turned", "scanned",
                                            "backed", "u_made", "x4_made", "placed", "read"))
            dlink = sem("j_link", ph)
            M2 = 2 * MUL
            gx = sb("j_gx", [128, 2, 2 * C, 2 * F], F32, ph)
            stg = sb("j_stg", [128, 2, 3, C], I32, ph)
            e3 = sb("j_e3", [128, 2, C, 3], F32, ph)
            e10 = sb("j_e10", [128, 2, C, 10], F32, ph)
            cb = sb("j_cb", [128, 2 * C, F], F32, ph)
            sq = sb("j_sq", [128, 2 * C, F], F32, ph)
            u = sb("j_u", [128, 2 * C, F], F32, ph)
            sm = sb("j_sm", [128, 2 * C], F32, ph)
            va = sb("j_va", [128, 2 * C], F32, ph)
            sd = sb("j_sd", [128, 2 * C], F32, ph)
            rc = sb("j_rc", [128, 2 * C], F32, ph)
            n2 = sb("j_n2", [128, C], F32, ph)
            nd = sb("j_nd", [128, C], F32, ph)
            nr = sb("j_nr", [128, C], F32, ph)
            e3q = sb("j_e3q", [128, C, 3], F32, ph)
            nv = sb("j_nv", [128, C, 3], F32, ph)
            x3 = sb("j_x3", [128, 2 * C, F], F32, ph)
            ad = sb("j_ad", [128, C, M2], F32, ph)
            xv = sb("j_xv", [128, C, 3, MUL], F32, ph)
            xn = sb("j_xn", [128, C, 3, MUL], F32, ph)
            ef = sb("j_ef", [10, 2, PG], F32, ph)
            hf = sb("j_hf", [MUL, 2, PG], F32, ph)
            pr1 = sb("j_pr1", [128, 2, 2, 12, M2], F32, ph)
            pr2 = sb("j_pr2", [128, 2, 3, MOUT, MUL], F32, ph)
            o1 = sb("j_o1", [128, C, 24], F32, ph)
            o3 = sb("j_o3", [128, C, 3, MOUT], F32, ph)
            th = sb("j_th", [128, C, MUL], F32, ph)
            ew2 = sb("j_ew2", [128, C], F32, ph)
            vv = sb("j_vv", [128, C, MOUT, 3], F32, ph)
            fr = sb("j_fr", [128, 2, C, F], F32, ph)
            sc = sb("j_sc", [F, 2, PG], F32, ph)
            x4 = sb("j_x4", [128, 2, C, F], F32, ph)
            p_e = pb("j_p_e", [128, 512], ph)
            p_h = pb("j_p_h", [128, 512], ph)
            p_w = pb("j_p_w", [128, 2, 2, 512], ph)
            p_f = pb("j_p_f", [128, 512], ph)
            p_b = pb("j_p_b", [128, 512], ph)
            block = ph.open()
            GAIN = 1.593
            WC = 2 * C

            @block.sync
            def _(sp):
                edges = lambda v, g: v.rearrange("(t p) f -> p t f", p=P)[:, bass.ds(g * C, C), :]
                with sp.Fori(0, NG // 2) as i:
                    for s in range(2):
                        g = i * 2 + s
                        sp.wait_ge(read, free(g))
                        sp.wait_ge(placed, g + 1)
                        sp.sem_inc(sp_tick, 1)
                        sp.dma_start(stg[0:P, s, 0], slot_i[0:P, bass.ds(g * C, C)]).then_inc(staged[s], 16)
                        sp.dma_start(stg[0:P, s, 1], slot_t[0:P, bass.ds(g * C, C)]).then_inc(staged[s], 16)
                        sp.dma_start(stg[0:P, s, 2], last_i[0:P, bass.ds(g * C, C)]).then_inc(staged[s], 16)
                        sp.dma_start(gx[0:P, s, 0:C], rows(btab[2], g)).then_inc(filled[s], 16)
                        sp.dma_start(e3[0:P, s], edges(attr3, g)).then_inc(attrs[s], 16)
                        sp.dma_start(e10[0:P, s], edges(attr10, g)).then_inc(attrs[s], 16)

            @block.gpsimd
            def _(pool):
                pool.sem_inc(placed, 1)

                def place(s):
                    for c in range(C):
                        pool.indirect_dma_start(out=out, out_offset=bass.IndirectOffsetOnAxis(ap=stg[0:P, s, 2, c:c + 1], axis=0),
                                                in_=x4[0:P, s, c], in_offset=None, bounds_check=b_n,
                                                oob_is_err=False).then_inc(slotted, 16)

                b_e, b_n = pool.to_reg(E - 1), pool.to_reg(N - 1)

                def gather(s):
                    for k in range(2):
                        for c in range(C):
                            pool.indirect_dma_start(out=gx[0:P, s, k * C + c], out_offset=None, in_=htab[2],
                                                    in_offset=bass.IndirectOffsetOnAxis(ap=stg[0:P, s, k, c:c + 1], axis=0),
                                                    bounds_check=b_e, oob_is_err=False).then_inc(gathered[s], 16)

                with pool.Fori(0, NG // 2) as i:
                    for s in range(2):
                        g = i * 2 + s
                        pool.wait_ge(staged[s], (i + 1) * 48)
                        pool.wait_ge(filled[s], (i + 1) * 16)
                        pool.sem_inc(pool_tick, 1)
                        gather(s)
                        pool.wait_ge(x4_made, g + LEAD)
                        pool.sem_inc(pool_tick, 1)
                        place(1 - s)
                        pool.wait_ge(slotted, g * C * 16 + C * 16 + s_base)
                        pool.sem_inc(pool_tick, 1)
                        pool.sem_inc(placed, 1)
                pool.wait_ge(x4_made, NG + LEAD)
                pool.sem_inc(pool_tick, 1)
                place(1)
                pool.wait_ge(slotted, (NG + 1) * C * 16 + s_base)

            @block.vector
            def _(dve):
                link = Links(dve, dlink)
                nc.vector.memset(stg[:, 1, 2], FAR)
                nc.vector.memset(x4[:, 1], 0.0)
                link(nc.vector.memset(sc[:, 1, PG - 1:PG], 0.0))
                link.base = 1
                credit(dve, read, w_used, scanned, x4_made, f_made, u_made)
                with dve.Fori(0, NG // 2) as i:
                    link.turn(i, 2 * 30)
                    for s in range(2):
                        g = i * 2 + s
                        cols = bass.ds(g * C, C)
                        dve.wait_ge(gathered[s], (i + 1) * 2 * C * 16 + g_base[s])
                        dve.wait_ge(attrs[s], (i + 1) * 32)
                        dve.sem_inc(dve_tick, 1)
                        bn(link, u[0:P], gx[0:P, s, :, 0:F], 2 * C)
                        link(nc.vector.scalar_tensor_tensor(u[0:P], u[0:P], 0.0, gx[0:P, s, :, F:2 * F], ALU.max, ALU.add))
                        link(nc.vector.tensor_tensor(e3q[0:P], e3[0:P, s], e3[0:P, s], ALU.mult))
                        nc.vector.reduce_sum(n2[0:P], e3q[0:P], AX)
                        center(link, cb[0:P], sm[0:P], sq[0:P], va[0:P], u[0:P]).then_inc(var_made, 1)
                        dve.wait_ge(dev_made, g * 2 + 1)
                        dve.sem_inc(dve_tick, 1)
                        nc.vector.reciprocal(nr[0:P], nd[0:P])
                        link(nc.vector.reciprocal(rc[0:P], sd[0:P]))
                        nc.vector.tensor_tensor(nv[0:P], e3[0:P, s], over(nr[0:P], 3), ALU.mult)
                        link(nc.vector.tensor_tensor(x3[0:P], cb[0:P], over(rc[0:P], F), ALU.mult))
                        dve.sem_inc(read, 1)
                        for k in range(2):
                            half = slice(k * 8, k * 8 + 8)
                            nc.vector.tensor_copy(ad[0:P, :, half], x3[0:P, k * C:(k + 1) * C, 0:8])
                            last = nc.vector.tensor_copy(xv[0:P, :, :, half], x3[0:P, k * C:(k + 1) * C, 8:F].rearrange("p c (u k) -> p c k u", k=3))
                        link(last)
                        link(nc.vector.tensor_tensor(xn[0:P], xv[0:P], over(nv[0:P], MUL), ALU.mult))
                        link(nc.vector.reduce_sum(ad[0:P, :, MUL:M2], xn[0:P].rearrange("p c k u -> p c u k"), AX))
                        for c in range(C):
                            b = c % 2
                            dve.wait_ge(w_mult, g * C + c + 1 + WC)
                            dve.sem_inc(dve_tick, 1)
                            nc.vector.tensor_tensor(pr1[0:P, b], p_w[0:P, b, :, 0:384].rearrange("p b (o u) -> p b o u", u=M2),
                                                    ad[0:P, c].unsqueeze(1).unsqueeze(1).broadcast_to([P, 2, 12, M2]), ALU.mult)
                            link(nc.vector.tensor_tensor(pr2[0:P, b],
                                                         p_w[0:P, b, 1, 384:512].rearrange("p (w u) -> p w u", u=MUL).unsqueeze(1).broadcast_to([P, 3, MOUT, MUL]),
                                                         xv[0:P, c].unsqueeze(2).broadcast_to([P, 3, MOUT, MUL]), ALU.mult))
                            dve.sem_inc(w_used, 1)
                            nc.vector.reduce_sum(o1[0:P, c], pr1[0:P, b].rearrange("p b o u -> p (b o) u"), AX)
                            link(nc.vector.reduce_sum(o3[0:P, c], pr2[0:P, b], AX))
                        dve.sem_inc(out_sum, 1)
                        link(nc.vector.tensor_tensor(vv[0:P], over(o1[0:P, :, MUL:24], 3), nv[0:P].unsqueeze(2).broadcast_to([P, C, MOUT, 3]), ALU.mult))
                        nc.vector.tensor_scalar(ew2[0:P], ew[0:P, cols], GAIN, None, ALU.mult)
                        link(nc.vector.tensor_tensor(vv[0:P], vv[0:P], o3[0:P].rearrange("p c k w -> p c w k"), ALU.add))
                        dve.wait_ge(tanhed, g + 1)
                        dve.wait_ge(f_turned, free(g))
                        dve.sem_inc(dve_tick, 1)
                        link(nc.vector.tensor_tensor(th[0:P], th[0:P], over(ew2[0:P], MUL), ALU.mult))
                        nc.vector.tensor_copy(fr[0:P, s, :, 0:MOUT], th[0:P, :, 0:MOUT])
                        nc.vector.tensor_tensor(fr[0:P, s, :, MOUT:F].rearrange("p c (w k) -> p c w k", k=3), vv[0:P],
                                                over(th[0:P, :, MOUT:MUL], 3), ALU.mult).then_inc(f_made, 1)
                        dve.wait_ge(f_turned, done(g))
                        dve.wait_ge(backed, free(g))
                        dve.sem_inc(dve_tick, 1)
                        link(nc.vector.tensor_tensor_scan(sc[:, s], same_b[0:F, bass.ds(g * PG, PG)], p_f[0:F, 0:PG],
                                                          sc[:, 1 - s, PG - 1:PG], ALU.mult, ALU.add))
                        dve.sem_inc(scanned, 1)
                        dve.wait_ge(backed, done(g))
                        dve.wait_ge(placed, g + 1)
                        dve.sem_inc(dve_tick, 1)
                        link(nc.vector.tensor_tensor(u[0:P, 0:C], p_b[0:P, 0:C * F].rearrange("p (c f) -> p c f", c=C), x3[0:P, C:2 * C], ALU.add))
                        dve.sem_inc(u_made, 1)
                        center(link, cb[0:P, 0:C], sm[0:P, 0:C], sq[0:P, 0:C], va[0:P, 0:C], u[0:P, 0:C]).then_inc(var_made, 1)
                        dve.wait_ge(dev_made, g * 2 + 2)
                        dve.sem_inc(dve_tick, 1)
                        link(nc.vector.reciprocal(rc[0:P, 0:C], sd[0:P, 0:C]))
                        link(nc.vector.tensor_tensor(x4[0:P, s], cb[0:P, 0:C], over(rc[0:P, 0:C], F), ALU.mult))
                        dve.sem_inc(x4_made, 1)
                link.end(NG // 2)

            @block.tensor
            def _(pe):
                credit(pe, e_turned, hid, f_turned, backed)
                pe.sem_inc(w_mult, WC)
                with pe.Fori(0, NG // 2) as i:
                    for s in range(2):
                        g = i * 2 + s
                        pe.wait_ge(attrs[s], (i + 1) * 32)
                        pe.wait_ge(e_taken, free1(g))
                        pe.sem_inc(pe_tick, 1)
                        for c in range(C):
                            last = nc.tensor.transpose(p_e[0:10, c * P:(c + 1) * P], e10[0:P, s, c], ident[0:P, 0:P])
                        last.then_inc(e_turned, 1)
                        pe.wait_ge(e_taken, done(g))
                        pe.wait_ge(h_taken, free1(g))
                        pe.sem_inc(pe_tick, 1)
                        nc.tensor.matmul(p_h[0:MUL, 0:PG], wl1[:], ef[:, s], start=True, stop=True).then_inc(hid, 1)
                        pe.wait_ge(h_taken, done(g))
                        pe.sem_inc(pe_tick, 1)
                        for c in range(C):
                            pe.wait_ge(w_used, g * C + c - 1 + LEAD)
                            pe.sem_inc(pe_tick, 1)
                            hc = hf[:, s, c * P:(c + 1) * P]
                            nc.tensor.matmul(p_w[0:P, c % 2, 0, 0:384], hc, wmix[:, 0:384], start=True, stop=True)
                            nc.tensor.matmul(p_w[0:P, c % 2, 1, 0:384], hc, wmix[:, 384:768], start=True, stop=True)
                            nc.tensor.matmul(p_w[0:P, c % 2, 1, 384:512], hc, wvec[:], start=True, stop=True).then_inc(w_mult, 1)
                        pe.wait_ge(f_made, done(g))
                        pe.wait_ge(scanned, free1(g))
                        pe.sem_inc(pe_tick, 1)
                        for c in range(C):
                            last = nc.tensor.transpose(p_f[0:F, c * P:(c + 1) * P], fr[0:P, s, c], ident[0:P, 0:P])
                        last.then_inc(f_turned, 1)
                        pe.wait_ge(scanned, done(g))
                        pe.wait_ge(u_made, free1(g))
                        pe.sem_inc(pe_tick, 1)
                        for c in range(C):
                            last = nc.tensor.transpose(p_b[0:P, c * F:(c + 1) * F], sc[:, s, c * P:(c + 1) * P], ident[0:F, 0:F])
                        last.then_inc(backed, 1)

            @block.scalar
            def _(act):
                credit(act, e_taken, h_taken)
                with act.Fori(0, NG // 2) as i:
                    for s in range(2):
                        g = i * 2 + s
                        act.wait_ge(e_turned, done(g))
                        act.wait_ge(hid, free(g))
                        act.sem_inc(act_tick, 1)
                        nc.scalar.copy(ef[:, s], p_e[0:10, 0:PG]).then_inc(e_taken, 1)
                        act.wait_ge(hid, done(g))
                        act.wait_ge(w_mult, g * C - C + WC)
                        act.sem_inc(act_tick, 1)
                        nc.scalar.activation(hf[:, s], p_h[0:MUL, 0:PG], ACT.Relu).then_inc(h_taken, 1)
                        act.wait_ge(var_made, g * 2 + 1)
                        act.sem_inc(act_tick, 1)
                        nc.scalar.activation(nd[0:P], n2[0:P], ACT.Sqrt)
                        deviation(sd[0:P], va[0:P]).then_inc(dev_made, 1)
                        act.wait_ge(out_sum, g + 1)
                        act.sem_inc(act_tick, 1)
                        nc.scalar.activation(th[0:P], o1[0:P, :, 0:MUL], ACT.Tanh).then_inc(tanhed, 1)
                        act.wait_ge(var_made, g * 2 + 2)
                        act.sem_inc(act_tick, 1)
                        deviation(sd[0:P, 0:C], va[0:P, 0:C]).then_inc(dev_made, 1)


def kernel(**inputs):
    import numpy as np
    import concourse.bacc as bacc
    from concourse.bass_utils import run_bass_kernel_spmd

    nc = bacc.Bacc("TRN2", target_bir_lowering=False, num_devices=1)
    arrays, args = {}, {}
    for name, value in inputs.items():
        value = np.ascontiguousarray(value)
        arrays["in_" + name] = value
        args[name] = nc.dram_tensor("in_" + name, value.shape, mybir.dt.from_np(value.dtype), kind="ExternalInput").ap()
    shape = inputs["x"].shape
    out = nc.dram_tensor("out_0", shape, F32, kind="ExternalOutput").ap()
    gnn_kernel(nc, args, out)
    return run_bass_kernel_spmd(nc, [arrays], core_ids=[0]).results[0]["out_0"]
```

```python
import concourse.bass as bass
from concourse import mybir
from contextlib import ExitStack

F32 = mybir.dt.float32
I32 = mybir.dt.int32
U8 = mybir.dt.uint8
ALU = mybir.AluOpType
ACT = mybir.ActivationFunctionType
AX = mybir.AxisListType.X

P = 125
C = 4
PG = P * C
LEAD = 2
FAR = 1 << 20
EPS = 1e-5


def over(ap, n):
    return ap.unsqueeze(ap.ndim).broadcast_to(list(ap.shape) + [n])


class Phase(ExitStack):

    def __init__(self, nc):
        super().__init__()
        self.nc, self.sems, self.blk = nc, [], None

    def open(self):
        self.blk = self.nc.Block()
        return self.blk.__enter__()

    def close_sems(self):
        with self.nc.Block() as block:
            @block.sync
            def _(sp):
                for s in self.sems:
                    sp.sem_clear(s)

    def __exit__(self, *error):
        if self.blk is not None:
            self.blk.__exit__(*error)
        if error[0] is None:
            self.close_sems()
        return super().__exit__(*error)


class Links:

    def __init__(self, eng, sem):
        self.eng, self.sem, self.base, self.n, self.i, self.per = eng, sem, 0, 0, 0, 0

    def turn(self, i, per):
        self.i, self.per, self.n = i, per, 0

    def __call__(self, ins):
        ins.then_inc(self.sem, 1)
        self.n += 1
        self.eng.wait_ge(self.sem, self.i * self.per + self.base + self.n)

    def end(self, turns):
        assert self.n == self.per, (self.n, self.per)
        self.base += turns * self.per
        self.i = self.per = self.n = 0


def skewed(eng, groups, body, link=None, links=None):
    def alone(g, new, old, more):
        if link is not None:
            link.turn(0, links(new, old, more))
        body(g, g % 2, g // 2, new, old, more)
        if link is not None:
            link.end(1)

    turns = groups // 2 - 1
    alone(0, True, False, True)
    with eng.Fori(0, turns) as i:
        if link is not None:
            link.turn(i, 2 * links(True, True, True))
        body(i * 2 + 1, 1, i, True, True, True)
        body(i * 2 + 2, 0, i + 1, True, True, True)
        if link is not None:
            link.end(turns)
    alone(groups - 1, True, True, False)
    alone(groups, False, True, False)


def gnn_kernel(nc, a, out):
    x = a["x"]
    N, F = x.shape
    E = a["src"].shape[0]
    T = E // P
    NG = T // C
    H = a["L2_gnn_c1_init"].shape[2]
    K = a["L2_gnn_c1_init"].shape[0]
    NIL = E
    SW = F + 2
    ROW = T // 2
    SUB = 4
    ND = N // (PG * SUB)
    TINY = 1e-30
    MUL, MOUT, PATHS = 16, 8, 7

    ctx = ExitStack()

    with ctx:
        def sb(name, shape, dt=F32, c=ctx):
            return c.enter_context(nc.sbuf_tensor(name, shape, dt))

        def pb(name, shape, c):
            return c.enter_context(nc.psum_tensor(name, shape, F32))

        def sem(name, c=ctx):
            s = c.enter_context(nc.semaphore(name))
            if c is not ctx:
                c.sems.append(s)
            return s

        def dram(name, shape, dt=F32):
            return nc.dram_tensor(name, shape, dt, kind="Internal").ap()

        ytab = dram("ytab", [N + P, F])
        slot_tab = dram("slot_tab", [N, 1], I32)
        same_row = dram("same_row", [E], U8)
        mtab = dram("mtab", [E + 1, SW])
        atab = [dram("a1tab", [E + 1, F]), dram("a2tab", [E + 1, H]), dram("a3tab", [E + 1, H])]
        htab = [dram("h1tab", [E, H]), dram("h2tab", [E, H]), dram("xhtab", [E, 2 * F])]
        btab = [dram("b1tab", [E, H]), dram("b2tab", [E, H]), dram("xbtab", [E, 2 * F])]
        x2d = dram("x2d", [N, F])
        h3d = dram("h3d", [N, F])

        def rows(tab, g, n=C):
            return tab[0:E, :].rearrange("(p t) f -> p t f", p=P)[:, bass.ds(g * C, n), :]

        def nodes(tab, g):
            return tab[0:N, :].rearrange("(g p n) f -> g p n f", g=ND, p=P)[bass.ds(g, 1)].rearrange("g p n f -> p (g n) f")

        fields = ("src", "dst", "edge_weight", "edge_attr_10", "edge_attr_3")
        wide = [1, 1, 1, 10, 3]
        by_dst = [dram("by_dst_" + n, [E, w], a[n].dtype) for n, w in zip(fields, wide)]
        given = [a[n].rearrange("(e o) -> e o", o=1) if w == 1 else a[n] for n, w in zip(fields, wide)]
        src, dst, weight, attr10, attr3 = (v.rearrange("e o -> (e o)") if w == 1 else v for v, w in zip(by_dst, wide))

        pool_tick, act_tick, dve_tick, pe_tick, sp_tick = (sem(f"{e}_tick") for e in ("pool", "act", "dve", "pe", "sp"))

        gathered = [sem(f"gathered{s}") for s in range(2)]
        added, slotted = sem("added"), sem("slotted")
        g_base = [0, 0]

        def done(g):
            return g + 1 + LEAD

        def free(g):
            return g - 1 + LEAD

        def free1(g):
            return g + LEAD

        def credit(eng, *sems):
            for s in sems:
                eng.sem_inc(s, LEAD)

        unsorted = sb("unsorted", [1, 1], I32)
        with Phase(nc) as ph:
            copied, loaded, cleared, checked, joined = (sem("o_" + v, ph) for v in ("copied", "loaded", "cleared", "checked", "joined"))
            dlink = sem("o_link", ph)
            now = sb("o_now", [ROW, 2, P], I32, ph)
            near = sb("o_near", [ROW, 2, P], F32, ph)
            edge = sb("o_edge", [ROW, 2], I32, ph)
            some = sb("o_some", [ROW, 2], F32, ph)
            one = sb("o_one", [ROW, 1], F32, ph)
            p_c = pb("o_p_c", [128, 512], ph)
            block = ph.open()
            came = a["dst"]

            @block.sync
            def _(sp):
                for to, of, w in zip(by_dst, given, wide):
                    sp.dma_start(to.rearrange("(p t) w -> p (t w)", p=P), of.rearrange("(p t) w -> p (t w)", p=P)).then_inc(copied, 16)
                sp.wait_ge(cleared, 1)
                flat = came.rearrange("(t p) -> t p", p=P)
                sp.dma_start(now[:], came.rearrange("(h q p) -> q h p", h=2, p=P)).then_inc(loaded, 16)
                sp.dma_start(edge[1:ROW, 0:1], flat[0:ROW - 1, P - 1:P], allow_slow_non_contiguous=True).then_inc(loaded, 16)
                sp.dma_start(edge[0:ROW, 1:2], flat[ROW - 1:T - 1, P - 1:P], allow_slow_non_contiguous=True).then_inc(loaded, 16)
                sp.wait_ge(copied, 16 * len(by_dst))

            @block.vector
            def _(dve):
                link = Links(dve, dlink)
                nc.vector.memset(one[:], 1.0)
                nc.vector.memset(edge[:], -1).then_inc(cleared, 1)
                dve.wait_ge(loaded, 48)
                nc.vector.tensor_tensor(near[:, :, 0], now[:, :, 0], edge[:], ALU.is_lt)
                link(nc.vector.tensor_tensor(near[:, :, 1:P], now[:, :, 1:P], now[:, :, 0:P - 1], ALU.is_lt))
                link(nc.vector.reduce_sum(some[:], near[:], AX))
                nc.vector.tensor_tensor(some[:, 0:1], some[:, 0:1], some[:, 1:2], ALU.add).then_inc(checked, 1)
                dve.wait_ge(joined, 1)
                nc.vector.tensor_scalar(unsorted[:], p_c[0:1, 0:1], 0.0, None, ALU.is_gt)

            @block.tensor
            def _(pe):
                pe.wait_ge(checked, 1)
                nc.tensor.matmul(p_c[0:1, 0:1], some[:, 0:1], one[:], start=True, stop=True).then_inc(joined, 1)

        placed_rows = sem("placed_rows")
        with Phase(nc) as ph:
            loaded, made, ranked, staged, moved = (sem("r_" + v, ph) for v in ("loaded", "made", "ranked", "staged", "moved"))
            dlink = sem("r_link", ph)
            PART = E // 10
            all_dst = sb("r_all_dst", [128, E], I32, ph)
            cols = [sb(f"r_col{k}", [128, T, w], a[n].dtype, ph) for k, (n, w) in enumerate(zip(fields, wide))]
            at = sb("r_at", [128, PART], F32, ph)
            tile0 = sb("r_tile0", [128, T], F32, ph)
            part0 = sb("r_part0", [128, 10], F32, ph)
            mine = sb("r_mine", [128, 10], F32, ph)
            dcol = sb("r_dcol", [128, T], F32, ph)
            lower_at = sb("r_lower_at", [128, PART], F32, ph)
            sums = sb("r_sums", [128, 10], F32, ph)
            rank_i = sb("r_rank_i", [128, T], I32, ph)
            s_rank = sb("r_s_rank", [128, 1], I32, ph)
            s_row = [sb(f"r_s_row{k}", [128, w], a[n].dtype, ph) for k, (n, w) in enumerate(zip(fields, wide))]
            block = ph.open()

            @block.sync
            def _(sp):
                with sp.If(sp.value_load(unsorted[0:1, 0:1]) > 0):
                    sp.dma_start(all_dst[:], a["dst"].partition_broadcast(128)).then_inc(loaded, 16)
                    for to, of in zip(cols, given):
                        sp.dma_start(to[0:P], of.rearrange("(t p) w -> p t w", p=P), allow_slow_non_contiguous=True).then_inc(loaded, 16)
                    with sp.Fori(0, T) as t:
                        sp.wait_ge(ranked, t + 1)
                        sp.wait_ge(moved, t + 1)
                        sp.sem_inc(sp_tick, 1)
                        sp.dma_start(s_rank[0:P], rank_i[0:P, bass.ds(t, 1)]).then_inc(staged, 16)
                        for to, of in zip(s_row, cols):
                            sp.dma_start(to[0:P].unsqueeze(1), of[0:P, bass.ds(t, 1)]).then_inc(staged, 16)

            @block.gpsimd
            def _(pool):
                with pool.If(pool.value_load(unsorted[0:1, 0:1]) > 0):
                    nc.gpsimd.iota(at[:], pattern=[[1, PART]], base=0, channel_multiplier=0, allow_small_or_imprecise_dtypes=True)
                    nc.gpsimd.iota(tile0[:], pattern=[[P, T]], base=0, channel_multiplier=0, allow_small_or_imprecise_dtypes=True)
                    nc.gpsimd.iota(part0[:], pattern=[[-PART, 10]], base=0, channel_multiplier=1,
                                   allow_small_or_imprecise_dtypes=True).then_inc(made, 1)
                    pool.sem_inc(moved, 1)
                    with pool.Fori(0, T) as t:
                        pool.wait_ge(staged, (t + 1) * 16 * 6)
                        pool.sem_inc(pool_tick, 1)
                        for to, of in zip(by_dst, s_row):
                            pool.indirect_dma_start(out=to, out_offset=bass.IndirectOffsetOnAxis(ap=s_rank[0:P, 0:1], axis=0),
                                                    in_=of[0:P], in_offset=None).then_inc(placed_rows, 16)
                        pool.wait_ge(placed_rows, (t + 1) * 16 * 5)
                        pool.sem_inc(moved, 1)

            @block.vector
            def _(dve):
                with dve.If(dve.value_load(unsorted[0:1, 0:1]) > 0):
                    link = Links(dve, dlink)
                    dve.wait_ge(loaded, 16 * 6)
                    dve.wait_ge(made, 1)
                    link(nc.vector.tensor_copy(dcol[0:P], cols[1][0:P, :, 0]))
                    link.base = 1
                    with dve.Fori(0, T) as t:
                        link.turn(t, 4 * 10 + 3)
                        link(nc.vector.tensor_scalar(mine[0:P], part0[0:P], tile0[0:P, bass.ds(t, 1)], None, ALU.add))
                        own = dcol[0:P, bass.ds(t, 1)]
                        for q in range(10):
                            part = all_dst[0:P, q * PART:(q + 1) * PART]
                            link(nc.vector.tensor_scalar(lower_at[0:P], at[0:P], mine[0:P, q:q + 1], None, ALU.is_lt))
                            link(nc.vector.scalar_tensor_tensor(lower_at[0:P], part, own, lower_at[0:P], ALU.is_equal, ALU.mult))
                            link(nc.vector.scalar_tensor_tensor(lower_at[0:P], part, own, lower_at[0:P], ALU.is_lt, ALU.add))
                            link(nc.vector.reduce_sum(sums[0:P, q:q + 1], lower_at[0:P], AX))
                        link(nc.vector.reduce_sum(mine[0:P, 0:1], sums[0:P], AX))
                        link(nc.vector.tensor_scalar(rank_i[0:P, bass.ds(t, 1)], mine[0:P, 0:1], 0.0, None, ALU.add))
                        dve.sem_inc(ranked, 1)
                    link.end(T)

        ident = sb("ident", [128, 128])
        ones = sb("ones", [128, 128])
        lower = sb("lower", [128, P])
        trash = sb("trash", [128, 1])
        epsc = sb("epsc", [128, 1])
        src_i = sb("src_i", [128, T], I32)
        dst_i = sb("dst_i", [128, T + 2 * C], I32)
        last_i = sb("last_i", [128, T], I32)
        rid_i = sb("rid_i", [128, T], I32)
        slot_i = sb("slot_i", [128, T], I32)
        slot_t = sb("slot_t", [128, T], I32)
        src_f = sb("src_f", [128, T])
        ew = sb("ew", [128, T])
        norm = sb("norm", [128, T])
        dinv_t = sb("dinv_t", [128, T])
        same_b = sb("same_b", [128, E], U8)
        stat = sb("stat", [128, 2, F])
        w0 = sb("w0", [F, F])
        w1e = sb("w1e", [2 * F + 1, F])
        w1d = sb("w1d", [C * F, C * F])
        b1d = sb("b1d", [1, C * F])
        fins, hs = [F, H, H], [H, H, F]
        wbias = []
        wroot0 = []
        wroot1 = []
        wblk = []
        for n in range(3):
            k0 = 2 * F + 1 if n == 0 else H + 1
            wbias.append(sb(f"wbias{n}", [k0, K * hs[n]]))
            wroot0.append(None if n == 0 else sb(f"wroot0_{n}", [H, K * hs[n]]))
            wroot1.append(sb(f"wroot1_{n}", [fins[n] + 1, K * hs[n]]))
            wblk.append([sb(f"wblka{n}", [128 if hs[n] == H else K * F, 2 * H if hs[n] == H else K * F]),
                         sb(f"wblkb{n}", [H, H]) if hs[n] == H else None])
        wl1 = sb("wl1", [10, MUL])
        wl2 = sb("wl2", [MUL, PATHS * MUL * MOUT])
        wmix = sb("wmix", [MUL, 3 * MOUT * 2 * MUL])
        wvec = sb("wvec", [MUL, MOUT * MUL])
        gamma = sb("gamma", [128, F])
        beta = sb("beta", [128, F])
        x2s = sb("x2s", [128, T, F])
        x2t = sb("x2t", [128, T, F])

        def center(link, c, sm, sq, v, x):
            link(nc.vector.reduce_sum(sm, x, AX))
            link(nc.vector.scalar_tensor_tensor(c, over(sm, F), -1.0 / F, x, ALU.mult, ALU.add))
            link(nc.vector.tensor_tensor(sq, c, c, ALU.mult))
            return nc.vector.reduce_sum(v, sq, AX)

        def deviation(sd, v):
            return nc.scalar.activation(sd, v, ACT.Sqrt, bias=epsc[0:P, 0:1], scale=1.0 / F)

        with Phase(nc) as ph:
            loaded = sem("loaded", ph)
            made = sem("made", ph)
            zeroed = sem("zeroed", ph)
            init_done = sem("init_done", ph)
            nils = sb("nils", [P, N // P], I32, ph)
            zrow = sb("zrow", [128, H], F32, ph)
            block = ph.open()
            n_loads = [0]

            @block.vector
            def _(dve):
                nc.vector.memset(ones[:], 1.0)
                nc.vector.memset(epsc[:], EPS)
                nc.vector.memset(dst_i[:], 0)
                nc.vector.memset(stat[:], 0.0)
                nc.vector.memset(zrow[:], 0.0)
                nc.vector.memset(nils[:], NIL)
                for n in range(3):
                    nc.vector.memset(wblk[n][0][:], 0.0)
                nc.vector.memset(w1d[:], 0.0)
                nc.vector.memset(w0[:], 0.0).then_inc(zeroed, 1)

            @block.gpsimd
            def _(pool):
                nc.gpsimd.memset(ident[:], 0.0).then_inc(made, 1)
                nc.gpsimd.memset(lower[:], 0.0).then_inc(made, 1)
                pool.wait_ge(made, 2)
                nc.gpsimd.affine_select(out=ident[:], in_=ident[:], compare_op=ALU.not_equal, fill=1.0, base=0,
                                        pattern=[[-1, 128]], channel_multiplier=1)
                nc.gpsimd.affine_select(out=lower[:], in_=lower[:], compare_op=ALU.is_ge, fill=1.0, base=0,
                                        pattern=[[1, P]], channel_multiplier=-1)
                nc.gpsimd.iota(trash[:], pattern=[[0, 1]], base=N, channel_multiplier=1,
                               allow_small_or_imprecise_dtypes=True)
                nc.gpsimd.iota(rid_i[:], pattern=[[1, T]], base=0, channel_multiplier=T)

            @block.sync
            def _(sp):
                def load(to, of):
                    sp.dma_start(to, of).then_inc(loaded, 16)
                    n_loads[0] += 1

                sp.wait_ge(zeroed, 1)
                load(w0[:], a["L0_gnn_weight"])
                load(w1e[0:2 * F, :], a["L1_gnn_W"])
                load(w1e[2 * F:2 * F + 1, :], a["L1_gnn_b"].rearrange("(o f) -> o f", o=1))
                for c in range(C):
                    cf = slice(c * F, (c + 1) * F)
                    load(w1d[cf, cf], a["L1_gnn_W"][0:F, :])
                    load(b1d[:, cf], a["L1_gnn_b"].rearrange("(o f) -> o f", o=1))
                for n in range(3):
                    init, w, root, b = (a[f"L2_gnn_c{n + 1}_{s}"] for s in ("init", "w", "root", "b"))
                    h, f = hs[n], fins[n]
                    kb = wbias[n].shape[0] - 1
                    kv = lambda t: t.rearrange("f (k g) -> f k g", k=K)
                    load(kv(wbias[n][kb - f:kb, :]), init.rearrange("k f g -> f k g"))
                    load(kv(wbias[n][kb:kb + 1, :]), b[0].rearrange("k o g -> o k g"))
                    load(kv((wbias[n] if n == 0 else wroot0[n])[0:f, :]), root[0].rearrange("k f g -> f k g"))
                    load(kv(wroot1[n][0:f, :]), root[1].rearrange("k f g -> f k g"))
                    load(kv(wroot1[n][f:f + 1, :]), b[1].rearrange("k o g -> o k g"))
                    for k in range(K):
                        if h == H and k == 2:
                            load(wblk[n][1][:, :], w[0, k])
                        else:
                            load(wblk[n][0][k * h:(k + 1) * h, k * h:(k + 1) * h], w[0, k])
                load(wl1[:], a["L3_gnn_W1"])
                load(wl2[:], a["L3_gnn_W2"])
                load(gamma[:], a["L2_gnn_bn_gamma"].partition_broadcast(128))
                load(beta[:], a["L2_gnn_bn_beta"].partition_broadcast(128))
                inits = [(ytab[0:N, :].rearrange("(p n) f -> p (n f)", p=P), x.rearrange("(p n) f -> p (n f)", p=P)),
                         (ytab[N:N + P, :], zrow[0:P, 0:F]),
                         (slot_tab.rearrange("(p n) o -> p (n o)", p=P), nils[:]),
                         (mtab[NIL:NIL + 1, :], zrow[0:1, 0:SW])]
                inits += [(atab[n][NIL:NIL + 1, :], zrow[0:1, 0:fins[n]]) for n in range(3)]
                for to, of in inits:
                    sp.dma_start(to, of).then_inc(init_done, 16)
                sp.wait_ge(loaded, 16 * n_loads[0])
                sp.wait_ge(init_done, 16 * len(inits))

        with Phase(nc) as ph:
            folded = sem("folded", ph)
            block = ph.open()

            @block.scalar
            def _(act):
                for n in range(3):
                    for w in (wroot1[n], wblk[n][0], wblk[n][1]):
                        if w is not None:
                            nc.scalar.mul(w[:], w[:], 1.0 / K)
                nc.scalar.mul(wl1[:], wl1[:], 0.2 ** 0.5)

            @block.vector
            def _(dve):
                ps, pv = 0.17677669529663687 / MUL ** 0.5, 0.25 / MUL ** 0.5
                path = lambda i: wl2[:, i * MUL * MOUT:(i + 1) * MUL * MOUT].rearrange("j (u w) -> j w u", u=MUL)
                mix = wmix[:].rearrange("j (o w h u) -> j o w h u", o=3, w=MOUT, h=2)
                vec = wvec[:].rearrange("j (w u) -> j w u", w=MOUT)
                for o, h, i, c in ((0, 0, 0, ps), (0, 1, 1, ps), (1, 0, 2, ps), (1, 1, 3, ps), (2, 0, 4, pv), (2, 1, 6, pv * 1.5 ** 0.5)):
                    nc.vector.tensor_scalar(mix[:, o, :, h], path(i), c, None, ALU.mult)
                nc.vector.tensor_scalar(vec, path(5), pv * 0.5773502691896258, None, ALU.mult).then_inc(folded, 1)
                dve.wait_ge(folded, 1)
                nc.vector.scalar_tensor_tensor(vec, path(6), -pv * 1.5 ** 0.5 / 3, vec, ALU.mult, ALU.add).then_inc(folded, 1)

        with Phase(nc) as ph:
            loaded = sem("rows_loaded", ph)
            filled = sem("rows_filled", ph)
            stored = sem("same_stored", ph)
            bcast = sem("same_bcast", ph)
            dlink = sem("prep_link", ph)
            row_ready = sem("row_ready", ph)
            turned = sem("turned", ph)
            taken = sem("taken", ph)
            ri = sb("ri", [ROW, 2, 2, P], I32, ph)
            edge_i = sb("edge_i", [ROW, 2, 2], I32, ph)
            rf = sb("rf", [ROW, 2, P + 2], F32, ph)
            cols = sb("cols", [ROW, 7, 2, P], F32, ph)
            same_f = sb("same_f", [ROW, 2, P], U8, ph)
            nl = sb("nl", [ROW, 2, P], F32, ph)
            pt = pb("prep_t", [128, 2, 512], ph)
            same_s = sb("same_s", [ROW, 2, P], F32, ph)
            nlast = sb("nlast", [ROW, 2, P], F32, ph)
            deg_l, fprod, bprod, rid_r, rid_m, rid_l = (
                sb(n, [ROW, 2, P], F32, ph) for n in ("deg_l", "fprod", "bprod", "rid_r", "rid_m", "rid_l"))
            no = sb("no", [ROW, P], F32, ph)
            ends = sb("ends", [1, 4, T], F32, ph)
            carry = sb("carry", [1, 2, T + 1], F32, ph)
            cin = sb("cin", [ROW, 2, 2], F32, ph)
            dlink2, dlink3 = sem("prep_link2", ph), sem("prep_link3", ph)
            half = lambda v: v.rearrange("(h q p) -> q h p", h=2, p=P)

            block = nc.Block()
            block.__enter__()

            @block.sync
            def _(sp):
                sp.wait_ge(filled, 1)
                sp.dma_start(ri[:, 0], half(src)).then_inc(loaded, 16)
                sp.dma_start(ri[:, 1], half(dst)).then_inc(loaded, 16)
                sp.dma_start(cols[:, 4], half(weight)).then_inc(loaded, 16)
                flat = dst.rearrange("(t p) -> t p", p=P)
                sp.dma_start(edge_i[1:ROW, 0, 0:1], flat[0:ROW - 1, P - 1:P], allow_slow_non_contiguous=True).then_inc(loaded, 16)
                sp.dma_start(edge_i[0:ROW, 1, 0:1], flat[ROW - 1:T - 1, P - 1:P], allow_slow_non_contiguous=True).then_inc(loaded, 16)
                sp.dma_start(edge_i[0:ROW, 0, 1:2], flat[1:ROW + 1, 0:1], allow_slow_non_contiguous=True).then_inc(loaded, 16)
                sp.dma_start(edge_i[0:ROW - 1, 1, 1:2], flat[ROW + 1:T, 0:1], allow_slow_non_contiguous=True).then_inc(loaded, 16)
                sp.wait_ge(row_ready, 1)
                sp.dma_start(half(same_row), same_f[:]).then_inc(stored, 16)
                sp.wait_ge(stored, 16)
                sp.dma_start(same_b[:], same_row.partition_broadcast(128)).then_inc(bcast, 16)
                sp.wait_ge(bcast, 16)

            @block.vector
            def _(dve):
                link = Links(dve, dlink)
                nc.vector.memset(edge_i[:], -1).then_inc(filled, 1)
                dve.wait_ge(filled, 1)
                dve.wait_ge(loaded, 7 * 16)
                nc.vector.tensor_copy(cols[:, 0], ri[:, 0])
                nc.vector.tensor_copy(rf[:, :, 0:1], edge_i[:, :, 0:1])
                nc.vector.tensor_copy(rf[:, :, P + 1:P + 2], edge_i[:, :, 1:2])
                nc.vector.tensor_copy(cols[:, 1], ri[:, 1])
                link(nc.vector.tensor_copy(rf[:, :, 1:P + 1], ri[:, 1]))
                nc.vector.memset(no[:], 0.0)
                nc.vector.tensor_tensor(same_s[:], rf[:, :, 1:P + 1], rf[:, :, 0:P], ALU.is_equal)
                nc.vector.tensor_tensor(nlast[:], rf[:, :, 1:P + 1], rf[:, :, 2:P + 2], ALU.is_equal)
                nc.vector.tensor_tensor(same_f[:], rf[:, :, 1:P + 1], rf[:, :, 0:P], ALU.is_equal).then_inc(row_ready, 1)
                link(nc.vector.tensor_tensor(nl[:], rf[:, :, 1:P + 1], rf[:, :, 2:P + 2], ALU.is_equal))
                nc.vector.tensor_scalar(cols[:, 3], nl[:], -1.0, 1.0, ALU.mult, ALU.add)
                link(nc.vector.tensor_scalar(nl[:], nl[:], float(FAR), None, ALU.mult))
                nc.vector.tensor_tensor(cols[:, 2], rf[:, :, 1:P + 1], nl[:], ALU.add).then_inc(row_ready, 1)
            block.__exit__(None, None, None)


            def ends_to_row(name, cols_of):
                with Phase(nc) as b:
                    there = sem(name, b)
                    blk = b.open()

                    @blk.tensor
                    def _(pe):
                        for n, col in enumerate(cols_of):
                            for h in range(2):
                                last = nc.tensor.transpose(pt[0:1, n // 2, (n % 2 * 2 + h) * ROW:(n % 2 * 2 + h + 1) * ROW],
                                                           col[:, h], ident[0:ROW, 0:ROW])
                        last.then_inc(there, 1)

                    @blk.vector
                    def _(dve):
                        dve.wait_ge(there, 1)
                        for n in range(len(cols_of)):
                            nc.vector.tensor_copy(ends[0:1, n], pt[0:1, n // 2, n % 2 * T:(n % 2 + 1) * T])

            def row_to_ends(name, n_rows):
                with Phase(nc) as b:
                    there = sem(name, b)
                    blk = b.open()

                    @blk.tensor
                    def _(pe):
                        for n in range(n_rows):
                            for h in range(2):
                                last = nc.tensor.transpose(pt[0:ROW, 0, n * 2 + h:n * 2 + h + 1],
                                                           carry[0:1, n, 1 + h * ROW:1 + (h + 1) * ROW], ident[0:1, 0:1])
                        last.then_inc(there, 1)

                    @blk.vector
                    def _(dve):
                        dve.wait_ge(there, 1)
                        nc.vector.tensor_copy(cin[:, 0:n_rows], pt[0:ROW, 0, 0:2 * n_rows].rearrange("r (n h) -> r n h", h=2))

            scan = nc.vector.tensor_tensor_scan
            with nc.Block() as b1:
                @b1.gpsimd
                def _(pool):
                    nc.gpsimd.iota(rid_r[:], pattern=[[ROW, 2], [T, P]], base=0, channel_multiplier=1,
                                   allow_small_or_imprecise_dtypes=True)

                @b1.vector
                def _(dve):
                    nc.vector.memset(carry[:], 0.0)
                    for h in range(2):
                        scan(deg_l[:, h], same_s[:, h], cols[:, 4, h], 0.0, ALU.mult, ALU.add)
                        scan(fprod[:, h], same_s[:, h], no[:], 1.0, ALU.mult, ALU.add)
                        scan(bprod[:, h, ::-1], nlast[:, h, ::-1], no[:], 1.0, ALU.mult, ALU.add)
            with nc.Block() as b2:
                @b2.vector
                def _(dve):
                    nc.vector.tensor_tensor(rid_m[:], rid_r[:], cols[:, 3], ALU.mult).then_inc(dlink2, 1)
                    dve.wait_ge(dlink2, 1)
                    for h in range(2):
                        scan(rid_l[:, h, ::-1], nlast[:, h, ::-1], rid_m[:, h, ::-1], 0.0, ALU.mult, ALU.add)
            ends_to_row("e1", [deg_l[:, :, P - 1:P], fprod[:, :, P - 1:P], rid_l[:, :, 0:1], bprod[:, :, 0:1]])
            with nc.Block() as b3:
                @b3.vector
                def _(dve):
                    scan(carry[0:1, 0, 2:T + 1], ends[0:1, 1, 0:T - 1], ends[0:1, 0, 0:T - 1], 0.0, ALU.mult, ALU.add)
                    scan(carry[0:1, 1, 1:T][:, ::-1], ends[0:1, 3, 1:T][:, ::-1], ends[0:1, 2, 1:T][:, ::-1], 0.0, ALU.mult, ALU.add)
            row_to_ends("e2", 2)
            with nc.Block() as b4:
                @b4.vector
                def _(dve):
                    link = Links(dve, dlink3)
                    for h in range(2):
                        nc.vector.scalar_tensor_tensor(cols[:, 6, h], bprod[:, h], cin[:, 1, h:h + 1], rid_l[:, h], ALU.mult, ALU.add)
                        link(nc.vector.scalar_tensor_tensor(deg_l[:, h], fprod[:, h], cin[:, 0, h:h + 1], deg_l[:, h], ALU.mult, ALU.add))
                    link(nc.vector.tensor_tensor(deg_l[:], deg_l[:], cols[:, 3], ALU.mult))
                    for h in range(2):
                        scan(cols[:, 5, h, ::-1], nlast[:, h, ::-1], deg_l[:, h, ::-1], 0.0, ALU.mult, ALU.add)
            ends_to_row("e3", [cols[:, 5, :, 0:1], bprod[:, :, 0:1]])
            with nc.Block() as b5:
                @b5.vector
                def _(dve):
                    scan(carry[0:1, 0, 1:T][:, ::-1], ends[0:1, 1, 1:T][:, ::-1], ends[0:1, 0, 1:T][:, ::-1], 0.0, ALU.mult, ALU.add)
                    nc.vector.memset(carry[0:1, 0, T:T + 1], 0.0)
            row_to_ends("e4", 1)
            with nc.Block() as b6:
                @b6.vector
                def _(dve):
                    for h in range(2):
                        nc.vector.scalar_tensor_tensor(cols[:, 5, h], bprod[:, h], cin[:, 0, h:h + 1], cols[:, 5, h], ALU.mult, ALU.add)

            with nc.Block() as b7:
                @b7.vector
                def _(dve):
                    for q, to in enumerate((src_f, dst_i, last_i, ew, dinv_t, slot_t)):
                        for h in range(2):
                            n = 2 * q + h
                            dve.wait_ge(turned, n + 1)
                            last = nc.vector.tensor_copy(to[0:P, h * ROW:(h + 1) * ROW], pt[0:P, h, 0:ROW])
                            if q == 0:
                                last = nc.vector.tensor_copy(src_i[0:P, h * ROW:(h + 1) * ROW], pt[0:P, h, 0:ROW])
                            last.then_inc(taken, 1)

                @b7.tensor
                def _(pe):
                    for q, col in enumerate((0, 1, 2, 4, 5, 6)):
                        for h in range(2):
                            n = 2 * q + h
                            if n >= 2:
                                pe.wait_ge(taken, n - 1)
                            nc.tensor.transpose(pt[0:P, h, 0:ROW], cols[:, col, h], ident[0:ROW, 0:ROW]).then_inc(turned, 1)

        with Phase(nc) as ph:
            staged_d = [sem(f"l0_staged_d{s}", ph) for s in range(2)]
            staged = [sem(f"l0_staged{s}", ph) for s in range(2)]
            rep_made = sem("l0_rep_made", ph)
            rep_turned = sem("l0_rep_turned", ph)
            eq_made = sem("l0_eq_made", ph)
            idx_made = sem("l0_idx_made", ph)
            scaled = sem("l0_scaled", ph)
            summed = sem("l0_summed", ph)
            sum_taken = sem("l0_sum_taken", ph)
            mult = sem("l0_mult", ph)
            row_made = sem("l0_row_made", ph)
            used = sem("l0_used", ph)
            dlink = sem("l0_link", ph)
            stg_d = sb("l0_stg_d", [128, 2, C], I32, ph)
            stg = sb("l0_stg", [128, 2, 2, C], I32, ph)
            stg_a = sb("l0_stg_a", [128, 2, C], I32, ph)
            xt = sb("l0_xt", [128, 2, C, F], F32, ph)
            rep = sb("l0_rep", [128, 2, C, P], F32, ph)
            eq = sb("l0_eq", [128, 2, C, P], F32, ph)
            eql = sb("l0_eql", [128, C, P], F32, ph)
            dup = sb("l0_dup", [128, C], F32, ph)
            tmp = sb("l0_tmp", [128, C], F32, ph)
            xe = sb("l0_xe", [128, 2, C, F], F32, ph)
            zt = sb("l0_zt", [F, 2, PG], F32, ph)
            zrows = sb("l0_zrows", [128, 2, C, F], F32, ph)
            p_rep = pb("l0_p_rep", [128, 2, 512], ph)
            p_sum = pb("l0_p_sum", [128, 2, 512], ph)
            p_row = pb("l0_p_row", [128, 2, 512], ph)
            block = ph.open()

            @block.sync
            def _(sp):
                for s in range(2):
                    sp.dma_start(stg_d[0:P, s], dst_i[0:P, s * C:(s + 1) * C]).then_inc(staged_d[s], 16)
                with sp.Fori(0, NG // 2) as i:
                    for s in range(2):
                        g = i * 2 + s
                        sp.wait_ge(used, free(g))
                        sp.sem_inc(sp_tick, 1)
                        sp.dma_start(stg[0:P, s, 0], last_i[0:P, bass.ds(g * C, C)]).then_inc(staged[s], 16)
                        sp.dma_start(stg[0:P, s, 1], rid_i[0:P, bass.ds(g * C, C)]).then_inc(staged[s], 16)
                        sp.wait_ge(scaled, done(g))
                        sp.sem_inc(sp_tick, 1)
                        sp.dma_start(stg_d[0:P, s], dst_i[0:P, bass.ds(g * C + 2 * C, C)]).then_inc(staged_d[s], 16)

            @block.gpsimd
            def _(pool):
                bound = pool.to_reg(N - 1)
                credit(pool, used)

                def gather(s, c):
                    pool.indirect_dma_start(out=xt[0:P, s, c], out_offset=None, in_=x, in_offset=bass.IndirectOffsetOnAxis(
                        ap=stg_d[0:P, s, c:c + 1], axis=0)).then_inc(gathered[s], 16)

                for s in range(2):
                    pool.wait_ge(staged_d[s], 16)
                    pool.sem_inc(pool_tick, 1)
                    for c in range(C):
                        gather(s, c)
                with pool.Fori(0, NG // 2) as i:
                    for s in range(2):
                        g = i * 2 + s
                        pool.wait_ge(row_made, done(g))
                        pool.wait_ge(idx_made, done(g))
                        pool.wait_ge(staged[s], (i + 1) * 32)
                        pool.wait_ge(scaled, done(g))
                        pool.wait_ge(staged_d[s], (i + 2) * 16)
                        pool.sem_inc(pool_tick, 1)
                        for c in range(C):
                            pool.indirect_dma_start(out=ytab, out_offset=bass.IndirectOffsetOnAxis(ap=stg_a[0:P, s, c:c + 1], axis=0),
                                                    in_=zrows[0:P, s, c], in_offset=None, compute_op=ALU.add).then_inc(added, 16)
                            gather(s, c)
                            pool.indirect_dma_start(out=slot_tab, out_offset=bass.IndirectOffsetOnAxis(ap=stg[0:P, s, 0, c:c + 1], axis=0),
                                                    in_=stg[0:P, s, 1, c:c + 1], in_offset=None, bounds_check=bound,
                                                    oob_is_err=False).then_inc(slotted, 16)
                            pool.wait_ge(added, g * C * 16 + c * 16 + 16)
                            pool.sem_inc(pool_tick, 1)
                        pool.wait_ge(slotted, g * C * 16 + C * 16)
                        pool.sem_inc(pool_tick, 1)
                        pool.sem_inc(used, 1)
                for s in range(2):
                    pool.wait_ge(gathered[s], (NG // 2 + 1) * C * 16)

            @block.vector
            def _(dve):
                link = Links(dve, dlink)
                credit(dve, rep_made, eq_made, idx_made, scaled)
                with dve.Fori(0, NG // 2) as i:
                    link.turn(i, 10)
                    for s in range(2):
                        g = i * 2 + s
                        mine = src_f[0:P, bass.ds(g * C, C)]
                        dve.wait_ge(rep_turned, free(g))
                        dve.sem_inc(dve_tick, 1)
                        nc.vector.tensor_scalar(rep[0:P, s], over(mine, P), 1.0, None, ALU.mult).then_inc(rep_made, 1)
                        dve.wait_ge(rep_turned, done(g))
                        dve.wait_ge(summed, free(g))
                        dve.sem_inc(dve_tick, 1)
                        pr = p_rep[0:P, s, 0:PG].rearrange("p (c q) -> p c q", c=C)
                        link(nc.vector.tensor_tensor(eq[0:P, s], pr, over(mine, P), ALU.is_equal))
                        link(nc.vector.tensor_tensor(eql[0:P], eq[0:P, s], lower[0:P, :].unsqueeze(1).broadcast_to([P, C, P]), ALU.mult))
                        dve.sem_inc(eq_made, 1)
                        nc.vector.tensor_scalar(tmp[0:P], mine, -1.0, trash[0:P, 0:1], ALU.mult, ALU.add)
                        link(nc.vector.reduce_sum(dup[0:P], eql[0:P], AX))
                        link(nc.vector.scalar_tensor_tensor(tmp[0:P], dup[0:P], 1.0, tmp[0:P], ALU.min, ALU.mult))
                        dve.wait_ge(used, free(g))
                        dve.sem_inc(dve_tick, 1)
                        link(nc.vector.tensor_tensor(stg_a[0:P, s], tmp[0:P], mine, ALU.add))
                        dve.sem_inc(idx_made, 1)
                        dve.wait_ge(gathered[s], (i + 1) * C * 16)
                        dve.sem_inc(dve_tick, 1)
                        nc.vector.tensor_tensor(xe[0:P, s], xt[0:P, s], over(ew[0:P, bass.ds(g * C, C)], F), ALU.mult).then_inc(scaled, 1)
                link.end(NG // 2)

            @block.tensor
            def _(pe):
                credit(pe, rep_turned, summed, mult)
                with pe.Fori(0, NG // 2) as i:
                    for s in range(2):
                        g = i * 2 + s
                        pe.wait_ge(rep_made, done(g))
                        pe.wait_ge(eq_made, free(g))
                        pe.sem_inc(pe_tick, 1)
                        for c in range(C):
                            last = nc.tensor.transpose(p_rep[0:P, s, c * P:(c + 1) * P], rep[0:P, s, c], ident[0:P, 0:P])
                        last.then_inc(rep_turned, 1)
                        pe.wait_ge(eq_made, done(g))
                        pe.wait_ge(scaled, done(g))
                        pe.wait_ge(sum_taken, free(g))
                        pe.sem_inc(pe_tick, 1)
                        for c in range(C):
                            last = nc.tensor.matmul(p_sum[0:F, s, c * P:(c + 1) * P], xe[0:P, s, c], eq[0:P, s, c], start=True, stop=True)
                        last.then_inc(summed, 1)
                        pe.wait_ge(sum_taken, done(g))
                        pe.wait_ge(row_made, free(g))
                        pe.sem_inc(pe_tick, 1)
                        for c in range(C):
                            last = nc.tensor.matmul(p_row[0:P, s, c * F:(c + 1) * F], zt[:, s, c * P:(c + 1) * P], w0[:], start=True, stop=True)
                        last.then_inc(mult, 1)

            @block.scalar
            def _(act):
                credit(act, sum_taken, row_made)
                with act.Fori(0, NG // 2) as i:
                    for s in range(2):
                        g = i * 2 + s
                        act.wait_ge(summed, done(g))
                        act.wait_ge(mult, free(g))
                        act.sem_inc(act_tick, 1)
                        nc.scalar.copy(zt[:, s], p_sum[0:F, s, 0:PG]).then_inc(sum_taken, 1)
                        act.wait_ge(mult, done(g))
                        act.wait_ge(used, free(g))
                        act.sem_inc(act_tick, 1)
                        nc.scalar.copy(zrows[0:P, s], p_row[0:P, s, 0:C * F].rearrange("p (c f) -> p c f", c=C)).then_inc(row_made, 1)

        for s in range(2):
            g_base[s] += (NG // 2 + 1) * C * 16


        assert ND == NG
        with Phase(nc) as ph:
            loaded = [sem(f"d_loaded{s}", ph) for s in range(2)]
            stored = [sem(f"d_stored{s}", ph) for s in range(2)]
            new_made, old_made, turned, taken, mult, relued, summed, var_made, dev_made, read, out_made = (
                sem("d_" + v, ph) for v in ("new_made", "old_made", "turned", "taken", "mult", "relued", "summed", "var_made",
                                            "dev_made", "read", "out_made"))
            dlink = sem("d_link", ph)
            R = SUB * C
            yt = sb("d_yt", [128, 2, R, F], F32, ph)
            sl = sb("d_sl", [128, 2, R], I32, ph)
            cb = sb("d_cb", [128, R, F], F32, ph)
            sq = sb("d_sq", [128, R, F], F32, ph)
            sm, va, sd, rc = (sb(f"d_{v}", [128, R], F32, ph) for v in ("sm", "va", "sd", "rc"))
            no_edge = sb("d_no_edge", [128, 2, R], F32, ph)
            u = sb("d_u", [128, R, F], F32, ph)
            x1 = sb("d_x1", [128, R, F], F32, ph)
            x2 = sb("d_x2", [128, 2, R, F], F32, ph)
            h12 = [sb(f"d_h{k}", [128, R, H], F32, ph) for k in (1, 2)]
            h3 = sb("d_h3", [128, 2, R, F], F32, ph)
            hm, hm2 = (sb(f"d_{v}", [128, R, F], F32, ph) for v in ("hm", "hm2"))
            acc = sb("d_acc", [128, 2, R, F], F32, ph)
            xg = sb("d_xg", [C * F, SUB, P], F32, ph)
            xf = [sb("d_xf0", [F + 1, SUB, PG], F32, ph), sb("d_xf1", [H + 1, SUB, PG], F32, ph)]
            hk = sb("d_hk", [128, 2, C, K * H], F32, ph)
            p_t = pb("d_p_t", [128, 2, 512], ph)
            p_m = pb("d_p_m", [128, 2, 2, 512], ph)
            e_staged = [sem(f"l1_staged{s}", ph) for s in range(2)]
            e_stored = [sem(f"l1_stored{s}", ph) for s in range(2)]
            e_var_made, e_dev_made, e_read, e_rs_made, e_scanned, e_sums_made, e_xt_made = (
                sem(f"l1_{n}", ph) for n in ("var_made", "dev_made", "read", "rs_made", "scanned", "sums_made", "xt_made"))
            e_turned, e_backed, e_fm_turned, e_mult = (sem(f"l1_{n}", ph) for n in ("turned", "backed", "fm_turned", "mult"))
            e_fm_taken, e_used = sem("l1_fm_taken", ph), sem("l1_used", ph)
            e_stg = sb("l1_stg", [128, 2, 2, C], I32, ph)
            e_gy = sb("l1_gy", [128, 2, 2 * C, F], F32, ph)
            e_gs = sb("l1_gs", [128, 2, C], I32, ph)
            e_cb = sb("l1_cb", [128, 2 * C, F], F32, ph)
            e_sq = sb("l1_sq", [128, 2 * C, F], F32, ph)
            e_sm = sb("l1_sm", [128, 2 * C], F32, ph)
            e_va = sb("l1_va", [128, 2 * C], F32, ph)
            e_sd = sb("l1_sd", [128, 2 * C], F32, ph)
            e_rc = sb("l1_rc", [128, 2 * C], F32, ph)
            e_rs = sb("l1_rs", [128, 2, C, SW], F32, ph)
            e_sc = sb("l1_sc", [SW, 2, PG], F32, ph)
            e_mrow = sb("l1_mrow", [128, 2, C, SW], F32, ph)
            e_xt = sb("l1_xt", [128, 2, C, 2 * F + 1], F32, ph)
            e_xf = sb("l1_xf", [2 * F + 1, 2, PG], F32, ph)
            e_u = sb("l1_u", [128, C, F], F32, ph)
            e_p_f = pb("l1_p_f", [128, 512], ph)
            e_p_b = pb("l1_p_b", [128, 512], ph)
            E_M = 256
            block = ph.open()
            EDGE = 13
            Q = 4 * SUB
            ems = (x1, x2, h12[0], h12[1])
            wts = (None, wroot1[0], wroot1[1], wroot1[2])

            @block.sync
            def _(sp):
                with sp.Fori(0, ND // 2) as i:
                    for s in range(2):
                        g = i * 2 + s
                        sp.wait_ge(read, free(g))
                        sp.sem_inc(sp_tick, 1)
                        sp.dma_start(yt[0:P, s], nodes(ytab, g)).then_inc(loaded[s], 16)
                        sp.dma_start(sl[0:P, s].unsqueeze(2), nodes(slot_tab, g)).then_inc(loaded[s], 16)
                        sp.wait_ge(e_read, free(g))
                        sp.sem_inc(sp_tick, 1)
                        sp.dma_start(e_stg[0:P, s, 0], src_i[0:P, bass.ds(g * C, C)]).then_inc(e_staged[s], 16)
                        sp.dma_start(e_stg[0:P, s, 1], dst_i[0:P, bass.ds(g * C, C)]).then_inc(e_staged[s], 16)

            @block.gpsimd
            def _(pool):
                with pool.Fori(0, NG // 2) as i:
                    for s in range(2):
                        g = i * 2 + s
                        pool.wait_ge(e_staged[s], (i + 1) * 32)
                        pool.wait_ge(e_read, free(g))
                        pool.sem_inc(pool_tick, 1)
                        for tab, to, k in ((ytab, e_gy[0:P, s, 0:C], 0), (ytab, e_gy[0:P, s, C:2 * C], 1),
                                           (slot_tab, e_gs[0:P, s].unsqueeze(2), 0)):
                            for c in range(C):
                                pool.indirect_dma_start(out=to[:, c], out_offset=None, in_=tab, in_offset=bass.IndirectOffsetOnAxis(
                                    ap=e_stg[0:P, s, k, c:c + 1], axis=0)).then_inc(gathered[s], 16)

            L1, CONV1, CONV2, CONV3 = range(4)

            def items(new, old):
                seq = [it for j in range(SUB) for it in (((L1, j),) if new else ()) + (((CONV2, j),) if old else ())]
                return seq + [(CONV3, j) for j in range(SUB) if old] + [(CONV1, j) for j in range(SUB) if new]

            def bodies(eng, body):
                at = lambda g: g * Q - Q // 2
                body(0, 0, 0, 0, True, False, True)
                with eng.Fori(0, ND // 2 - 1) as i:
                    body(i * 2 + 1, 1, i, at(i * 2 + 1), True, True, True)
                    body(i * 2 + 2, 0, i + 1, at(i * 2 + 2), True, True, True)
                body(ND - 1, 1, ND // 2 - 1, at(ND - 1), True, True, False)
                body(ND, 0, ND // 2, at(ND), False, True, False)

            @block.vector
            def _(dve):
                link = Links(dve, dlink)
                credit(dve, read, summed, out_made)
                credit(dve, e_var_made, e_read, e_rs_made, e_scanned, e_sums_made, e_xt_made)
                for s in range(2):
                    nc.vector.memset(e_rs[:, s, :, F:F + 1], 1.0)
                    nc.vector.memset(e_xt[:, s, :, 2 * F:2 * F + 1], 1.0)
                link(nc.vector.memset(e_sc[:, 1, PG - 1:PG], 0.0))
                nc.vector.memset(xf[0][F:F + 1], 1.0)
                nc.vector.memset(xf[1][H:H + 1], 1.0)
                link(nc.vector.memset(acc[:], 0.0))
                link.base = 2

                def edge_stage(m, g, s, k):
                    cols = bass.ds(g * C, C)
                    if m == 0:
                        dve.wait_ge(gathered[s], (k + 1) * 3 * C * 16 + g_base[s])
                        dve.sem_inc(dve_tick, 1)
                        nc.vector.tensor_scalar(slot_i[0:P, cols], e_gs[0:P, s], 0, None, ALU.add)
                        center(link, e_cb[0:P], e_sm[0:P], e_sq[0:P], e_va[0:P], e_gy[0:P, s]).then_inc(e_var_made, 1)
                        dve.sem_inc(e_read, 1)
                    if m == 3:
                        dve.wait_ge(e_dev_made, g * 2 + 1)
                        dve.wait_ge(e_turned, free(g))
                        dve.wait_ge(e_fm_turned, free(g))
                        dve.sem_inc(dve_tick, 1)
                        link(nc.vector.reciprocal(e_rc[0:P], e_sd[0:P]))
                        nc.vector.tensor_tensor(e_rs[0:P, s, :, 0:F], e_cb[0:P, 0:C], over(e_rc[0:P, 0:C], F), ALU.mult)
                        nc.vector.tensor_tensor(x2s[0:P, cols, :], e_cb[0:P, 0:C], over(e_rc[0:P, 0:C], F), ALU.mult)
                        nc.vector.tensor_tensor(e_xt[0:P, s, :, 0:F], e_cb[0:P, C:2 * C], over(e_rc[0:P, C:2 * C], F), ALU.mult)
                        nc.vector.tensor_scalar(e_rs[0:P, s, :, F + 1], ew[0:P, cols], 1.0, None, ALU.mult).then_inc(e_rs_made, 1)
                    if m == 5:
                        dve.wait_ge(e_turned, done(g))
                        dve.wait_ge(e_backed, free(g))
                        dve.sem_inc(dve_tick, 1)
                        link(nc.vector.tensor_tensor_scan(e_sc[:, s], same_b[0:SW, bass.ds(g * PG, PG)], e_p_f[0:SW, 0:PG],
                                                          e_sc[:, 1 - s, PG - 1:PG], ALU.mult, ALU.add))
                        dve.sem_inc(e_scanned, 1)
                    if m == 7:
                        dve.wait_ge(e_backed, done(g))
                        dve.wait_ge(e_stored[s], (k + 1) * 16)
                        dve.sem_inc(dve_tick, 1)
                        sums = e_p_b[0:P, 0:C * SW].rearrange("p (c f) -> p c f", c=C)
                        nc.vector.tensor_copy(e_mrow[0:P, s], sums).then_inc(e_sums_made, 1)
                        link(nc.vector.tensor_scalar(e_sm[0:P, 0:C], sums[:, :, F], 1.0, None, ALU.max))
                        link(nc.vector.reciprocal(e_rc[0:P, 0:C], e_sm[0:P, 0:C]))
                        nc.vector.tensor_tensor(e_xt[0:P, s, :, F:2 * F], sums[:, :, 0:F], over(e_rc[0:P, 0:C], F), ALU.mult).then_inc(e_xt_made, 1)
                    if m == 11:
                        dve.wait_ge(e_mult, done(g))
                        dve.sem_inc(dve_tick, 1)
                        link(nc.vector.scalar_tensor_tensor(e_u[0:P], e_p_b[0:P, E_M:E_M + C * F].rearrange("p (c f) -> p c f", c=C), 0.0,
                                                            e_xt[0:P, s, :, 0:F], ALU.max, ALU.add))
                        center(link, e_cb[0:P, 0:C], e_sm[0:P, 0:C], e_sq[0:P, 0:C], e_va[0:P, 0:C], e_u[0:P]).then_inc(e_var_made, 1)
                        dve.sem_inc(e_used, 1)
                    if m == 14:
                        dve.wait_ge(e_dev_made, g * 2 + 2)
                        dve.sem_inc(dve_tick, 1)
                        link(nc.vector.reciprocal(e_rc[0:P, 0:C], e_sd[0:P, 0:C]))
                        link(nc.vector.tensor_tensor(x2t[0:P, cols, :], e_cb[0:P, 0:C], over(e_rc[0:P, 0:C], F), ALU.mult))


                def first_norm(g, s, k):
                    dve.wait_ge(loaded[s], (k + 1) * 32)
                    dve.sem_inc(dve_tick, 1)
                    nc.vector.tensor_scalar(no_edge[0:P, s], sl[0:P, s], float(NIL), None, ALU.is_equal)
                    center(link, cb[0:P], sm[0:P], sq[0:P], va[0:P], yt[0:P, s]).then_inc(var_made, 1)
                    dve.sem_inc(read, 1)
                    dve.wait_ge(dev_made, g * 2 + 1)
                    dve.sem_inc(dve_tick, 1)
                    link(nc.vector.reciprocal(rc[0:P], sd[0:P]))
                    nc.vector.tensor_tensor(x1[0:P], cb[0:P], over(rc[0:P], F), ALU.mult).then_inc(new_made, SUB)

                def second_norm(g, s, k, items_done):
                    dve.wait_ge(summed, items_done + LEAD)
                    dve.wait_ge(stored[s], (k + 1) * 32)
                    dve.sem_inc(dve_tick, 1)
                    center(link, cb[0:P], sm[0:P], sq[0:P], va[0:P], u[0:P]).then_inc(var_made, 1)
                    dve.wait_ge(dev_made, g * 2 + 2)
                    dve.sem_inc(dve_tick, 1)
                    link(nc.vector.reciprocal(rc[0:P], sd[0:P]))
                    nc.vector.tensor_tensor(x2[0:P, s], cb[0:P], over(rc[0:P], F), ALU.mult).then_inc(new_made, SUB)

                def batch_sums(s, items_done):
                    dve.wait_ge(summed, items_done + LEAD)
                    dve.sem_inc(dve_tick, 1)
                    dve.sem_inc(out_made, 1)
                    link(nc.vector.tensor_tensor(hm[0:P], h3[0:P, s], over(no_edge[0:P, s], F), ALU.mult))
                    nc.vector.tensor_tensor(acc[0:P, 0], acc[0:P, 0], hm[0:P], ALU.add)
                    link(nc.vector.tensor_tensor(hm2[0:P], hm[0:P], h3[0:P, s], ALU.mult))
                    link(nc.vector.tensor_tensor(acc[0:P, 1], acc[0:P, 1], hm2[0:P], ALU.add))

                def body(g, s, k, before, new, old, more):
                    seq = items(new, old)
                    if isinstance(g, int):
                        link.turn(0, EDGE * new + 8 * new + SUB * (new + 2 * old) + 3 * old - 4 * (new and not more) + 4 * (not old))
                    if not old:
                        for m in range(Q):
                            edge_stage(m, g, s, k)
                        first_norm(g, s, k)
                    for m, (step, j) in enumerate(seq):
                        if new and old:
                            edge_stage(m, g, s, k)
                        if new and m == (2 * SUB if old else SUB):
                            second_norm(g, s, k, before + m)
                        if new and m == len(seq) - SUB:
                            if old:
                                batch_sums(1 - s, before + m)
                            if more:
                                first_norm(g + 1, 1 - s, k + s)
                        cs = slice(j * C, (j + 1) * C)
                        dve.wait_ge(relued, before + m + 1 + LEAD)
                        dve.sem_inc(dve_tick, 1)
                        if step == L1:
                            nc.vector.tensor_tensor(u[0:P, cs], hk[0:P, m % 2, :, 0:F], x1[0:P, cs], ALU.add).then_inc(summed, 1)
                            continue
                        h = hs[step - 1]
                        to = h3[:, 1 - s] if step == CONV3 else h12[step - 1]
                        a3 = [hk[0:P, m % 2, :, b * h:(b + 1) * h] for b in range(3)]
                        link(nc.vector.tensor_tensor(to[0:P, cs], a3[0], a3[1], ALU.add))
                        nc.vector.tensor_tensor(to[0:P, cs], to[0:P, cs], a3[2], ALU.add).then_inc(summed, 1)
                        if step != CONV3:
                            dve.wait_ge(summed, before + m + 1 + LEAD)
                            dve.sem_inc(old_made, 1)
                    if not new:
                        batch_sums(1 - s, before + len(seq))
                    if isinstance(g, int):
                        link.end(1)

                def looped(g, s, k, before, new, old, more):
                    if not isinstance(g, int) and s == 1:
                        link.turn(k, 2 * (EDGE + 23))
                    body(g, s, k, before, new, old, more)
                    if not isinstance(g, int) and s == 0:
                        link.end(ND // 2 - 1)

                bodies(dve, looped)
                for k in range(2):
                    last = nc.vector.reduce_sum(stat[0:P, k], acc[0:P, k].rearrange("p n f -> p f n"), AX)

            @block.tensor
            def _(pe):
                credit(pe, turned, mult)
                credit(pe, e_turned, e_backed, e_fm_turned, e_mult)

                def edge_stage(m, g, s, k):
                    if m == 5:
                        pe.wait_ge(e_rs_made, done(g))
                        pe.wait_ge(e_fm_taken, free1(g))
                        pe.sem_inc(pe_tick, 1)
                        for c in range(C):
                            last = nc.tensor.transpose(e_p_f[0:SW, c * P:(c + 1) * P], e_rs[0:P, s, c], ident[0:P, 0:P])
                        last.then_inc(e_turned, 1)
                    if m == 7:
                        pe.wait_ge(e_scanned, done(g))
                        pe.wait_ge(e_xt_made, free1(g))
                        pe.sem_inc(pe_tick, 1)
                        for c in range(C):
                            last = nc.tensor.transpose(e_p_b[0:P, c * SW:(c + 1) * SW], e_sc[:, s, c * P:(c + 1) * P], ident[0:SW, 0:SW])
                        last.then_inc(e_backed, 1)
                    if m == 9:
                        pe.wait_ge(e_xt_made, done(g))
                        pe.wait_ge(e_scanned, done(g))
                        pe.sem_inc(pe_tick, 1)
                        for c in range(C):
                            last = nc.tensor.transpose(e_p_f[0:2 * F + 1, c * P:(c + 1) * P], e_xt[0:P, s, c], ident[0:P, 0:P])
                        last.then_inc(e_fm_turned, 1)
                    if m == 11:
                        pe.wait_ge(e_fm_taken, done(g))
                        pe.wait_ge(e_used, free1(g))
                        pe.sem_inc(pe_tick, 1)
                        for c in range(C):
                            last = nc.tensor.matmul(e_p_b[0:P, E_M + c * F:E_M + (c + 1) * F], e_xf[:, s, c * P:(c + 1) * P], w1e[:], start=True, stop=True)
                        last.then_inc(e_mult, 1)

                def turn(g, s, before, m, step, j):
                    f = F if step < CONV2 else H
                    em = x2[:, s] if step == CONV1 else ems[step]
                    if step < CONV2:
                        pe.wait_ge(new_made, g * 2 * SUB + step * SUB + j + 1)
                    else:
                        pe.wait_ge(old_made, (g - 1) * 2 * SUB + (step - CONV2) * SUB + j + 1)
                    pe.wait_ge(taken, before + m - 1 + LEAD)
                    pe.sem_inc(pe_tick, 1)
                    if step == L1:
                        nc.tensor.transpose(p_t[0:C * F, m % 2, 0:P], em[0:P, j * C:(j + 1) * C].rearrange("p c f -> p (c f)"),
                                            ident[0:P, 0:P]).then_inc(turned, 1)
                        return
                    for c in range(C):
                        last = nc.tensor.transpose(p_t[0:f, m % 2, c * P:(c + 1) * P], em[0:P, j * C + c], ident[0:P, 0:P])
                    last.then_inc(turned, 1)

                def product(before, m, step, j):
                    pe.wait_ge(taken, before + m + 1 + LEAD)
                    pe.wait_ge(relued, before + m - 1 + LEAD)
                    pe.sem_inc(pe_tick, 1)
                    if step == L1:
                        nc.tensor.matmul(p_m[0:P, m % 2, 0, 0:C * F], ones[0:1, 0:P], b1d[:], start=True, stop=False)
                        nc.tensor.matmul(p_m[0:P, m % 2, 0, 0:C * F], xg[:, j], w1d[:], start=False, stop=True).then_inc(mult, 1)
                        return
                    W = K * hs[step - 1]
                    for c in range(C):
                        last = nc.tensor.matmul(p_m[0:P, m % 2, c // 2, c % 2 * W:(c % 2 + 1) * W],
                                                xf[step // 2][:, j, c * P:(c + 1) * P], wts[step][:], start=True, stop=True)
                    last.then_inc(mult, 1)

                def body(g, s, k, before, new, old, more):
                    seq = items(new, old)
                    if not old:
                        for m in range(Q):
                            edge_stage(m, g, s, k)
                    for m, (step, j) in enumerate(seq):
                        if new and old:
                            edge_stage(m, g, s, k)
                        if m == SUB and not old:
                            product(before, m - 1, *seq[m - 1])
                        turn(g, s, before, m, step, j)
                        if m and not (m == SUB and not old):
                            product(before, m - 1, *seq[m - 1])
                    product(before, len(seq) - 1, *seq[-1])

                bodies(pe, body)

            @block.scalar
            def _(act):
                credit(act, taken, relued, e_fm_taken, e_used)
                for s in range(2):
                    act.sem_inc(stored[s], 32)
                    act.sem_inc(e_stored[s], 16)

                def edge_stage(m, g, s, k):
                    if m == 2:
                        act.wait_ge(e_var_made, g * 2 + 1 + LEAD)
                        act.sem_inc(act_tick, 1)
                        deviation(e_sd[0:P], e_va[0:P]).then_inc(e_dev_made, 1)
                    if m == 9:
                        act.wait_ge(e_sums_made, done(g))
                        act.sem_inc(act_tick, 1)
                        act.dma_start(rows(mtab, g), e_mrow[0:P, s]).then_inc(e_stored[s], 16)
                    if m == 10:
                        act.wait_ge(e_fm_turned, done(g))
                        act.wait_ge(e_mult, free(g))
                        act.sem_inc(act_tick, 1)
                        nc.scalar.copy(e_xf[:, s], e_p_f[0:2 * F + 1, 0:PG]).then_inc(e_fm_taken, 1)
                    if m == 13:
                        act.wait_ge(e_var_made, g * 2 + 2 + LEAD)
                        act.sem_inc(act_tick, 1)
                        deviation(e_sd[0:P, 0:C], e_va[0:P, 0:C]).then_inc(e_dev_made, 1)

                def take(before, m, step, j):
                    act.wait_ge(turned, before + m + 1 + LEAD)
                    act.sem_inc(act_tick, 1)
                    if step == L1:
                        nc.scalar.copy(xg[:, j], p_t[0:C * F, m % 2, 0:P]).then_inc(taken, 1)
                        return
                    f = F if step == CONV1 else H
                    nc.scalar.copy(xf[step // 2][0:f, j], p_t[0:f, m % 2, 0:PG]).then_inc(taken, 1)

                def relu(before, m, step, j):
                    act.wait_ge(mult, before + m + 1 + LEAD)
                    act.wait_ge(summed, before + m - 1 + LEAD)
                    act.sem_inc(act_tick, 1)
                    if step == L1:
                        nc.scalar.activation(hk[0:P, m % 2, :, 0:F], p_m[0:P, m % 2, 0, 0:C * F].rearrange("p (c w) -> p c w", c=C),
                                             ACT.Relu).then_inc(relued, 1)
                        return
                    W = K * hs[step - 1]
                    nc.scalar.activation(hk[0:P, m % 2].rearrange("p (b c) w -> p b c w", b=2)[:, :, :, 0:W],
                                         p_m[0:P, m % 2, :, 0:2 * W].rearrange("p b (c w) -> p b c w", c=2), ACT.Relu).then_inc(relued, 1)

                def norm_deviation(n):
                    act.wait_ge(var_made, n)
                    act.sem_inc(act_tick, 1)
                    deviation(sd[0:P], va[0:P]).then_inc(dev_made, 1)

                def store(g, s):
                    act.wait_ge(out_made, g + LEAD)
                    act.sem_inc(act_tick, 1)
                    act.dma_start(nodes(x2d, g - 1), x2[0:P, 1 - s]).then_inc(stored[1 - s], 16)
                    act.dma_start(nodes(h3d, g - 1), h3[0:P, 1 - s]).then_inc(stored[1 - s], 16)

                def body(g, s, k, before, new, old, more):
                    seq = items(new, old)
                    if not old:
                        for m in range(Q):
                            edge_stage(m, g, s, k)
                        norm_deviation(1)
                    for m, it in enumerate(seq):
                        if new and old:
                            edge_stage(m, g, s, k)
                        if m == SUB and not old:
                            relu(before, m - 1, *seq[m - 1])
                            norm_deviation(2)
                            norm_deviation(3)
                        take(before, m, *it)
                        if m and not (m == SUB and not old):
                            relu(before, m - 1, *seq[m - 1])
                        if new and old and m == 2 * SUB + 1:
                            norm_deviation(g * 2 + 2)
                        if new and old and m == 3 * SUB + 1:
                            store(g, s)
                            if more:
                                norm_deviation(g * 2 + 3)
                    relu(before, len(seq) - 1, *seq[-1])
                    if not new:
                        store(g, s)

                bodies(act, body)
                for s in range(2):
                    act.wait_ge(stored[s], (ND // 2 + 1) * 32)
                    act.wait_ge(e_stored[s], (NG // 2 + 1) * 16)

        for s in range(2):
            g_base[s] += NG // 2 * 3 * C * 16
        with Phase(nc) as ph:
            staged = [sem(f"c_staged{s}", ph) for s in range(2)]
            var_made, dev_made, xt_made, fm_turned, fm_taken, mult, used = (
                sem(f"c_{n}", ph) for n in ("var_made", "dev_made", "xt_made", "fm_turned", "fm_taken", "mult", "used"))
            dlink = sem("c_link", ph)
            stg = sb("c_stg", [128, 2, C], I32, ph)
            gm = sb("c_gm", [128, 2, C, SW], F32, ph)
            cb = sb("c_cb", [128, 2, C, F], F32, ph)
            sq = sb("c_sq", [128, C, F], F32, ph)
            sm, sd, rc, nm = (sb(f"c_{n}", [128, C], F32, ph) for n in ("sm", "sd", "rc", "nm"))
            va = sb("c_va", [128, 2, C], F32, ph)
            xt = sb("c_xt", [128, 2, C, 2 * F + 1], F32, ph)
            xf = sb("c_xf", [2 * F + 1, 2, PG], F32, ph)
            u = sb("c_u", [128, C, F], F32, ph)
            p_f = pb("c_p_f", [128, 2, 512], ph)
            p_m = pb("c_p_m", [128, 2, 512], ph)
            block = ph.open()

            @block.sync
            def _(sp):
                with sp.Fori(0, NG // 2) as i:
                    for s in range(2):
                        g = i * 2 + s
                        sp.wait_ge(xt_made, free(g))
                        sp.sem_inc(sp_tick, 1)
                        sp.dma_start(stg[0:P, s], slot_i[0:P, bass.ds(g * C, C)]).then_inc(staged[s], 16)

            @block.gpsimd
            def _(pool):
                with pool.Fori(0, NG // 2) as i:
                    for s in range(2):
                        g = i * 2 + s
                        pool.wait_ge(staged[s], (i + 1) * 16)
                        pool.wait_ge(xt_made, free(g))
                        pool.sem_inc(pool_tick, 1)
                        for c in range(C):
                            pool.indirect_dma_start(out=gm[0:P, s, c], out_offset=None, in_=mtab, in_offset=bass.IndirectOffsetOnAxis(
                                ap=stg[0:P, s, c:c + 1], axis=0)).then_inc(gathered[s], 16)

            @block.vector
            def _(dve):
                link = Links(dve, dlink)
                credit(dve, var_made, xt_made, used)
                for s in range(2):
                    nc.vector.memset(xt[:, s, :, 2 * F:2 * F + 1], 1.0)

                def inputs(g, s, k):
                    cols = bass.ds(g * C, C)
                    dve.wait_ge(gathered[s], (k + 1) * C * 16 + g_base[s])
                    dve.wait_ge(fm_turned, free(g))
                    dve.sem_inc(dve_tick, 1)
                    nc.vector.tensor_scalar(norm[0:P, cols], gm[0:P, s, :, F + 1], 1.0, None, ALU.mult)
                    nc.vector.tensor_scalar(xt[0:P, s, :, 0:F], x2s[0:P, cols, :], 1.0, None, ALU.mult)
                    link(nc.vector.tensor_scalar(nm[0:P], gm[0:P, s, :, F], 1.0, None, ALU.max))
                    link(nc.vector.reciprocal(nm[0:P], nm[0:P]))
                    nc.vector.tensor_tensor(xt[0:P, s, :, F:2 * F], gm[0:P, s, :, 0:F], over(nm[0:P], F), ALU.mult).then_inc(xt_made, 1)

                def body(g, s, k, new, old, more):
                    if not old:
                        inputs(g, s, k)
                    if new:
                        dve.wait_ge(mult, done(g))
                        dve.sem_inc(dve_tick, 1)
                        link(nc.vector.scalar_tensor_tensor(u[0:P], p_m[0:P, s, 0:C * F].rearrange("p (c f) -> p c f", c=C), 0.0,
                                                            xt[0:P, s, :, 0:F], ALU.max, ALU.add))
                        center(link, cb[0:P, s], sm[0:P], sq[0:P], va[0:P, s], u[0:P]).then_inc(var_made, 1)
                        dve.sem_inc(used, 1)
                    if more:
                        inputs(g + 1, 1 - s, k + s)
                    if new:
                        dve.wait_ge(dev_made, g + 1)
                        dve.sem_inc(dve_tick, 1)
                        link(nc.vector.reciprocal(rc[0:P], sd[0:P]))
                        link(nc.vector.tensor_tensor(x2s[0:P, bass.ds(g * C, C), :], cb[0:P, s], over(rc[0:P], F), ALU.mult))

                skewed(dve, NG, body, link, lambda new, old, more: 6 * new + 2 * more + 2 * (not old))

            @block.tensor
            def _(pe):
                credit(pe, fm_turned, mult)
                with pe.Fori(0, NG // 2) as i:
                    for s in range(2):
                        g = i * 2 + s
                        pe.wait_ge(xt_made, done(g))
                        pe.wait_ge(fm_taken, free(g))
                        pe.sem_inc(pe_tick, 1)
                        for c in range(C):
                            last = nc.tensor.transpose(p_f[0:2 * F + 1, s, c * P:(c + 1) * P], xt[0:P, s, c], ident[0:P, 0:P])
                        last.then_inc(fm_turned, 1)
                        pe.wait_ge(fm_taken, done(g))
                        pe.wait_ge(used, free(g))
                        pe.sem_inc(pe_tick, 1)
                        for c in range(C):
                            last = nc.tensor.matmul(p_m[0:P, s, c * F:(c + 1) * F], xf[:, s, c * P:(c + 1) * P], w1e[:], start=True, stop=True)
                        last.then_inc(mult, 1)

            @block.scalar
            def _(act):
                credit(act, fm_taken)

                def take(g, s):
                    act.wait_ge(fm_turned, done(g))
                    act.wait_ge(mult, free(g))
                    act.sem_inc(act_tick, 1)
                    nc.scalar.copy(xf[:, s], p_f[0:2 * F + 1, s, 0:PG]).then_inc(fm_taken, 1)

                def body(g, s, k, new, old, more):
                    if not old:
                        take(g, s)
                    if new:
                        act.wait_ge(var_made, done(g))
                        act.sem_inc(act_tick, 1)
                        deviation(sd[0:P], va[0:P, s]).then_inc(dev_made, 1)
                    if more:
                        take(g + 1, 1 - s)

                skewed(act, NG, body)

        for s in range(2):
            g_base[s] += NG // 2 * C * 16
        with Phase(nc) as ph:
            made, rooted = sem("n_made", ph), sem("n_rooted", ph)
            x2_stored = sem("x2_stored", ph)
            dlink = sem("n_link", ph)
            dg = sb("n_dg", [128, 2, T], F32, ph)
            some = sb("n_some", [128, 2, T], F32, ph)
            block = ph.open()

            @block.vector
            def _(dve):
                link = Links(dve, dlink)
                for k, d in enumerate((norm, dinv_t)):
                    nc.vector.tensor_scalar(some[0:P, k], d[0:P], 0.0, None, ALU.is_gt)
                    last = nc.vector.tensor_scalar(dg[0:P, k], d[0:P], TINY, None, ALU.max)
                last.then_inc(made, 1)
                dve.wait_ge(rooted, 1)
                link(nc.vector.reciprocal(dg[0:P], dg[0:P]))
                link(nc.vector.tensor_tensor(dg[0:P], dg[0:P], some[0:P], ALU.mult))
                link(nc.vector.tensor_tensor(norm[0:P], dg[0:P, 0], ew[0:P], ALU.mult))
                link(nc.vector.tensor_tensor(norm[0:P], norm[0:P], dg[0:P, 1], ALU.mult))

            @block.sync
            def _(sp):
                for tab, v in ((htab[2], x2t), (btab[2], x2s)):
                    sp.dma_start(tab.rearrange("(p t) f -> p t f", p=P)[:, :, F:2 * F], v[0:P]).then_inc(x2_stored, 16)
                sp.wait_ge(x2_stored, 32)

            @block.scalar
            def _(act):
                act.wait_ge(made, 1)
                nc.scalar.activation(dg[0:P], dg[0:P], ACT.Sqrt).then_inc(rooted, 1)

        hsp = sb("hsp", [128, T, H])
        for n in range(3):
            f, h, hp = fins[n], hs[n], hs[n - 1]
            W = K * h
            wide = F if n == 2 else 0
            with Phase(nc) as ph:
                nm = f"p{n}_"
                staged = [sem(f"{nm}staged{s}", ph) for s in range(2)]
                filled = [sem(f"{nm}filled{s}", ph) for s in range(2)]
                a_stored = [sem(f"{nm}a_stored{s}", ph) for s in range(2)]
                b_stored = [sem(f"{nm}b_stored{s}", ph) for s in range(2)]
                xs_made, turned, scanned, backed, a_taken, x_turned, x_taken, mult, relued, b_made = (
                    sem(nm + v, ph) for v in ("xs_made", "turned", "scanned", "backed", "a_taken", "x_turned",
                                              "x_taken", "mult", "relued", "b_made"))
                dlink = sem(nm + "link", ph)
                stg = sb(nm + "stg", [128, 2, C], I32, ph)
                gx = sb(nm + "gx", [128, 2, C, f], F32, ph)
                xs = sb(nm + "xs", [128, 2, C, f], F32, ph)
                xb = sb(nm + "xb", [128, 2, C, f + 1], F32, ph)
                sc = sb(nm + "sc", [f, 2, PG], F32, ph)
                arow = sb(nm + "arow", [128, 2, C, f], F32, ph)
                xf = sb(nm + "xf", [f + 1, 2, PG], F32, ph)
                hk = sb(nm + "hk", [128, 2, C, W], F32, ph)
                brow = sb(nm + "brow", [128, 2, C, h], F32, ph)
                p_t = pb(nm + "p_t", [128, 2, 512], ph)
                p_b = pb(nm + "p_b", [128, 512], ph)
                p_f = pb(nm + "p_f", [128, 512], ph)
                p_h = pb(nm + "p_h", [128, 2, 2, 512], ph)
                block = ph.open()

                @block.sync
                def _(sp):
                    if n == 0:
                        return
                    with sp.Fori(0, NG // 2) as i:
                        for s in range(2):
                            g = i * 2 + s
                            sp.wait_ge(xs_made, free(g))
                            sp.sem_inc(sp_tick, 1)
                            sp.dma_start(stg[0:P, s], slot_i[0:P, bass.ds(g * C, C)]).then_inc(staged[s], 16)
                            sp.dma_start(gx[0:P, s], rows(btab[n - 1], g)).then_inc(filled[s], 16)

                @block.gpsimd
                def _(pool):
                    if n == 0:
                        return
                    bound = pool.to_reg(E - 1)
                    with pool.Fori(0, NG // 2) as i:
                        for s in range(2):
                            pool.wait_ge(staged[s], (i + 1) * 16)
                            pool.wait_ge(filled[s], (i + 1) * 16)
                            pool.sem_inc(pool_tick, 1)
                            for c in range(C):
                                pool.indirect_dma_start(out=gx[0:P, s, c], out_offset=None, in_=htab[n - 1],
                                                        in_offset=bass.IndirectOffsetOnAxis(ap=stg[0:P, s, c:c + 1], axis=0),
                                                        bounds_check=bound, oob_is_err=False).then_inc(gathered[s], 16)

                @block.vector
                def _(dve):
                    link = Links(dve, dlink)
                    credit(dve, xs_made, scanned, b_made)
                    for s in range(2):
                        nc.vector.memset(xb[:, s, :, f:f + 1], 1.0)
                    link(nc.vector.memset(sc[:, 1, PG - 1:PG], 0.0))
                    link.base = 1

                    def inputs(g, s, k):
                        cols = bass.ds(g * C, C)
                        dve.wait_ge(turned, free(g))
                        dve.wait_ge(x_turned, free(g))
                        dve.sem_inc(dve_tick, 1)
                        if n:
                            dve.wait_ge(gathered[s], (k + 1) * C * 16 + g_base[s])
                            dve.sem_inc(dve_tick, 1)
                        x_in = gx[0:P, s] if n else x2s[0:P, cols, :]
                        nm_b = over(norm[0:P, cols], f)
                        nc.vector.tensor_scalar(xb[0:P, s, :, 0:f], x_in, 1.0, None, ALU.mult)
                        if n:
                            nc.vector.tensor_tensor(hsp[0:P, cols, :], x_in, nm_b, ALU.mult)
                        nc.vector.tensor_tensor(xs[0:P, s], x_in, nm_b, ALU.mult).then_inc(xs_made, 1)

                    def body(g, s, k, new, old, more):
                        if not old:
                            inputs(g, s, k)
                        if more:
                            inputs(g + 1, 1 - s, k + s)
                        if new:
                            dve.wait_ge(turned, done(g))
                            dve.wait_ge(backed, free(g))
                            dve.sem_inc(dve_tick, 1)
                            link(nc.vector.tensor_tensor_scan(sc[:, s], same_b[0:f, bass.ds(g * PG, PG)], p_t[0:f, s, 0:PG],
                                                              sc[:, 1 - s, PG - 1:PG], ALU.mult, ALU.add))
                            dve.sem_inc(scanned, 1)
                        if old:
                            o = 1 - s
                            dve.wait_ge(relued, done(g - 1))
                            dve.wait_ge(b_stored[o], (k + s) * 16)
                            dve.sem_inc(dve_tick, 1)
                            link(nc.vector.tensor_tensor(brow[0:P, o], hk[0:P, o, :, 0:h], hk[0:P, o, :, h:2 * h], ALU.add))
                            nc.vector.tensor_tensor(brow[0:P, o], brow[0:P, o], hk[0:P, o, :, 2 * h:3 * h], ALU.add).then_inc(b_made, 1)

                    skewed(dve, NG, body, link, lambda new, old, more: new + old)

                @block.tensor
                def _(pe):
                    credit(pe, turned, backed, x_turned, mult)

                    def body(g, s, k, new, old, more):
                        if new:
                            pe.wait_ge(xs_made, done(g))
                            pe.wait_ge(scanned, free(g))
                            pe.wait_ge(x_taken, free1(g))
                            pe.sem_inc(pe_tick, 1)
                            for c in range(C):
                                last = nc.tensor.transpose(p_f[0:f + 1, c * P:(c + 1) * P], xb[0:P, s, c], ident[0:P, 0:P])
                            last.then_inc(x_turned, 1)
                            for c in range(C):
                                last = nc.tensor.transpose(p_t[0:f, s, c * P:(c + 1) * P], xs[0:P, s, c], ident[0:P, 0:P])
                            last.then_inc(turned, 1)
                        if old:
                            pe.wait_ge(scanned, done(g - 1))
                            if not (isinstance(g, int) and g == 1):
                                pe.wait_ge(a_taken, free1(g - 1))
                            pe.sem_inc(pe_tick, 1)
                            for c in range(C):
                                last = nc.tensor.transpose(p_b[0:P, c * f:(c + 1) * f], sc[:, 1 - s, c * P:(c + 1) * P], ident[0:f, 0:f])
                            last.then_inc(backed, 1)
                        if new:
                            pe.wait_ge(x_taken, done(g))
                            pe.wait_ge(relued, free(g))
                            pe.sem_inc(pe_tick, 1)
                            for c in range(C):
                                last = nc.tensor.matmul(p_h[0:P, s, c // 2, c % 2 * W:(c % 2 + 1) * W], xf[:, s, c * P:(c + 1) * P],
                                                        wroot1[n][:], start=True, stop=True)
                            last.then_inc(mult, 1)

                    skewed(pe, NG, body)

                @block.scalar
                def _(act):
                    credit(act, a_taken, x_taken, relued)
                    for s in range(2):
                        act.sem_inc(a_stored[s], 16)
                        act.sem_inc(b_stored[s], 16)

                    def store_b(q, s):
                        act.wait_ge(b_made, done(q))
                        act.sem_inc(act_tick, 1)
                        act.dma_start(rows(btab[n], q)[:, :, 0:h], brow[0:P, s]).then_inc(b_stored[s], 16)

                    def body(g, s, k, new, old, more):
                        o = 1 - s
                        if new:
                            act.wait_ge(x_turned, done(g))
                            act.wait_ge(mult, free(g))
                            act.sem_inc(act_tick, 1)
                            nc.scalar.copy(xf[:, s], p_f[0:f + 1, 0:PG]).then_inc(x_taken, 1)
                        if old:
                            act.wait_ge(backed, done(g - 1))
                            act.wait_ge(a_stored[o], (k + s) * 16)
                            act.sem_inc(act_tick, 1)
                            nc.scalar.copy(arow[0:P, o], p_b[0:P, 0:C * f].rearrange("p (c f) -> p c f", c=C)).then_inc(a_taken, 1)
                        if new:
                            act.wait_ge(mult, done(g))
                            act.wait_ge(b_made, free(g))
                            act.sem_inc(act_tick, 1)
                            nc.scalar.activation(hk[0:P, s].rearrange("p (b c) w -> p b (c w)", b=2), p_h[0:P, s, :, 0:2 * W],
                                                 ACT.Relu).then_inc(relued, 1)
                        if old:
                            act.wait_ge(a_taken, done(g - 1))
                            act.sem_inc(act_tick, 1)
                            act.dma_start(rows(atab[n], g - 1), arow[0:P, o]).then_inc(a_stored[o], 16)
                            store_b(g - 1, o)

                    skewed(act, NG, body)
                    for s in range(2):
                        act.wait_ge(a_stored[s], (NG // 2 + 1) * 16)
                        act.wait_ge(b_stored[s], (NG // 2 + 1) * 16)

            if n:
                for s in range(2):
                    g_base[s] += NG // 2 * C * 16
            with Phase(nc) as ph:
                nm = f"e{n}_"
                M1 = 2 * h if h == H else W
                parts = [(0, M1)] + ([(M1, h)] if h == H else [])
                fx = (2 * F + 1) if n == 0 else f + 1
                staged = [sem(f"{nm}staged{s}", ph) for s in range(2)]
                t_loaded = [sem(f"{nm}t_loaded{s}", ph) for s in range(2)]
                h_stored = [sem(f"{nm}h_stored{s}", ph) for s in range(2)]
                xa_made, a_turned, t_turned, a_taken, t_taken, msg, relu0, scanned, mult, relued, h_made = (
                    sem(nm + v, ph) for v in ("xa_made", "a_turned", "t_turned", "a_taken", "t_taken", "msg", "relu0",
                                              "scanned", "mult", "relued", "h_made"))
                s_turned, s_taken = sem(nm + "s_turned", ph), sem(nm + "s_taken", ph)
                dlink = sem(nm + "link", ph)
                stg = sb(nm + "stg", [128, 2, C], I32, ph)
                ga = sb(nm + "ga", [128, 2, C, f], F32, ph)
                xa = sb(nm + "xa", [128, 2, C, fx], F32, ph)
                xh = sb(nm + "xh", [128, 2, C, f], F32, ph) if n else None
                xt = sb(nm + "xt", [128, 2, C, f + 1], F32, ph)
                fa = sb(nm + "fa", [fx, 2, PG], F32, ph)
                fh = sb(nm + "fh", [f, 2, PG], F32, ph) if n else None
                ft = sb(nm + "ft", [f + 1, 2, PG], F32, ph)
                m = [sb(f"{nm}m{k}", [w, PG], F32, ph) for k, (_, w) in enumerate(parts)]
                sc = [sb(f"{nm}sc{k}", [w, 2, PG], F32, ph) for k, (_, w) in enumerate(parts)]
                hk = sb(nm + "hk", [128, 2, C, W], F32, ph)
                hrow = sb(nm + "hrow", [128, 2, C, h], F32, ph)
                p_x = pb(nm + "p_x", [128, 2, 512], ph)
                p_o = [pb(f"{nm}p_o{k}", [128, 512], ph) for k in range(2)]
                p_h = pb(nm + "p_h", [128, 2, 2, 512], ph)
                block = ph.open()

                @block.sync
                def _(sp):
                    with sp.Fori(0, NG // 2) as i:
                        for s in range(2):
                            g = i * 2 + s
                            sp.wait_ge(xa_made, free(g))
                            sp.sem_inc(sp_tick, 1)
                            sp.dma_start(stg[0:P, s], slot_i[0:P, bass.ds(g * C, C)]).then_inc(staged[s], 16)
                            if n:
                                sp.wait_ge(t_turned, free(g))
                                sp.sem_inc(sp_tick, 1)
                                sp.dma_start(xt[0:P, s, :, 0:f], rows(htab[n - 1], g)).then_inc(t_loaded[s], 16)

                @block.gpsimd
                def _(pool):
                    with pool.Fori(0, NG // 2) as i:
                        for s in range(2):
                            g = i * 2 + s
                            pool.wait_ge(staged[s], (i + 1) * 16)
                            pool.wait_ge(xa_made, free(g))
                            pool.sem_inc(pool_tick, 1)
                            for c in range(C):
                                pool.indirect_dma_start(out=ga[0:P, s, c], out_offset=None, in_=atab[n],
                                                        in_offset=bass.IndirectOffsetOnAxis(ap=stg[0:P, s, c:c + 1], axis=0)
                                                        ).then_inc(gathered[s], 16)

                @block.vector
                def _(dve):
                    link = Links(dve, dlink)
                    credit(dve, xa_made, scanned, h_made)
                    for s in range(2):
                        nc.vector.memset(xt[:, s, :, f:f + 1], 1.0)
                    for k in range(len(parts)):
                        link(nc.vector.memset(sc[k][:, 1, PG - 1:PG], 0.0))
                    link.base = len(parts)

                    def inputs(g, s, k):
                        cols = bass.ds(g * C, C)
                        dve.wait_ge(gathered[s], (k + 1) * C * 16 + g_base[s])
                        dve.wait_ge(a_turned, free(g))
                        dve.wait_ge(s_turned if n else t_turned, free(g))
                        dve.sem_inc(dve_tick, 1)
                        nm_b = norm[0:P, cols]
                        if n == 0:
                            nc.vector.tensor_tensor(xa[0:P, s, :, 0:F], x2s[0:P, cols, :], over(nm_b, F), ALU.mult)
                            nc.vector.tensor_scalar(xt[0:P, s, :, 0:F], x2t[0:P, cols, :], 1.0, None, ALU.mult)
                        else:
                            nc.vector.tensor_scalar(xh[0:P, s], hsp[0:P, cols, :], 1.0, None, ALU.mult)
                        nc.vector.tensor_scalar(xa[0:P, s, :, fx - 1], nm_b, 1.0, None, ALU.mult)
                        nc.vector.tensor_tensor(xa[0:P, s, :, fx - 1 - f:fx - 1], ga[0:P, s], over(nm_b, f), ALU.mult).then_inc(xa_made, 1)

                    def body(g, s, k, new, old, more):
                        if not old:
                            inputs(g, s, k)
                        if more:
                            inputs(g + 1, 1 - s, k + s)
                        if old:
                            o = 1 - s
                            dve.wait_ge(relued, done(g - 1))
                            dve.wait_ge(h_stored[o], (k + s) * 16)
                            dve.sem_inc(dve_tick, 1)
                            link(nc.vector.tensor_tensor(hrow[0:P, o], hk[0:P, o, :, 0:h], hk[0:P, o, :, h:2 * h], ALU.add))
                            nc.vector.tensor_tensor(hrow[0:P, o], hrow[0:P, o], hk[0:P, o, :, 2 * h:3 * h], ALU.add).then_inc(h_made, 1)
                        if new:
                            dve.wait_ge(relu0, done(g))
                            dve.wait_ge(mult, free(g))
                            dve.sem_inc(dve_tick, 1)
                            for q, (_, w) in enumerate(parts):
                                link(nc.vector.tensor_tensor_scan(sc[q][:, s], same_b[0:w, bass.ds(g * PG, PG)], m[q][:],
                                                                  sc[q][:, 1 - s, PG - 1:PG], ALU.mult, ALU.add))
                            dve.sem_inc(scanned, 1)

                    skewed(dve, NG, body, link, lambda new, old, more: new * len(parts) + old)

                @block.tensor
                def _(pe):
                    credit(pe, a_turned, t_turned, s_turned, msg, mult)

                    def body(g, s, k, new, old, more):
                        if new:
                            pe.wait_ge(xa_made, done(g))
                            pe.wait_ge(s_taken if n else a_taken, free1(g))
                            pe.sem_inc(pe_tick, 1)
                            for c in range(C):
                                last = nc.tensor.transpose(p_x[0:fx, 0, c * P:(c + 1) * P], xa[0:P, s, c], ident[0:P, 0:P])
                            last.then_inc(a_turned, 1)
                            pe.wait_ge(t_taken, free1(g))
                            if n:
                                pe.wait_ge(t_loaded[s], (k + 1) * 16)
                            pe.sem_inc(pe_tick, 1)
                            for c in range(C):
                                last = nc.tensor.transpose(p_x[0:f + 1, 1, c * P:(c + 1) * P], xt[0:P, s, c], ident[0:P, 0:P])
                            last.then_inc(t_turned, 1)
                            if n:
                                pe.wait_ge(a_taken, done(g))
                                pe.sem_inc(pe_tick, 1)
                                for c in range(C):
                                    last = nc.tensor.transpose(p_x[0:f, 0, c * P:(c + 1) * P], xh[0:P, s, c], ident[0:P, 0:P])
                                last.then_inc(s_turned, 1)
                        if old:
                            o = 1 - s
                            pe.wait_ge(t_taken, done(g - 1))
                            pe.wait_ge(scanned, done(g - 1))
                            if not (isinstance(g, int) and g == 1):
                                pe.wait_ge(relued, free(g - 1))
                            pe.sem_inc(pe_tick, 1)
                            for c in range(C):
                                for q, (b, w) in enumerate(parts):
                                    to = p_h[0:P, o, c // 2, c % 2 * W + b:c % 2 * W + b + w]
                                    nc.tensor.matmul(to, ft[:, o, c * P:(c + 1) * P], wroot1[n][:, b:b + w], start=True, stop=False)
                                    last = nc.tensor.matmul(to, sc[q][:, o, c * P:(c + 1) * P], wblk[n][q][:], start=False, stop=True)
                            last.then_inc(mult, 1)
                        if new:
                            pe.wait_ge(s_taken if n else a_taken, done(g))
                            pe.wait_ge(relu0, free1(g))
                            pe.sem_inc(pe_tick, 1)
                            for q, (b, w) in enumerate(parts):
                                if n:
                                    nc.tensor.matmul(p_o[q][0:w, 0:PG], wroot0[n][:, b:b + w], fh[:, s], start=True, stop=False)
                                last = nc.tensor.matmul(p_o[q][0:w, 0:PG], wbias[n][:, b:b + w], fa[:, s], start=(n == 0), stop=True)
                            last.then_inc(msg, 1)

                    skewed(pe, NG, body)

                @block.scalar
                def _(act):
                    credit(act, a_taken, t_taken, s_taken, relu0, relued)
                    for s in range(2):
                        act.sem_inc(h_stored[s], 16)

                    def store(q, s):
                        act.wait_ge(h_made, done(q))
                        act.sem_inc(act_tick, 1)
                        act.dma_start(rows(htab[n], q)[:, :, 0:h], hrow[0:P, s]).then_inc(h_stored[s], 16)

                    def body(g, s, k, new, old, more):
                        o = 1 - s
                        if new:
                            act.wait_ge(a_turned, done(g))
                            act.wait_ge(msg, free(g))
                            act.sem_inc(act_tick, 1)
                            nc.scalar.copy(fa[:, s], p_x[0:fx, 0, 0:PG]).then_inc(a_taken, 1)
                            act.wait_ge(t_turned, done(g))
                            act.wait_ge(mult, free(g))
                            act.sem_inc(act_tick, 1)
                            nc.scalar.copy(ft[:, s], p_x[0:f + 1, 1, 0:PG]).then_inc(t_taken, 1)
                            if n:
                                act.wait_ge(s_turned, done(g))
                                act.sem_inc(act_tick, 1)
                                nc.scalar.copy(fh[:, s], p_x[0:f, 0, 0:PG]).then_inc(s_taken, 1)
                        if old:
                            act.wait_ge(mult, done(g - 1))
                            if not (isinstance(g, int) and g == 1):
                                act.wait_ge(h_made, free(g - 1))
                            act.sem_inc(act_tick, 1)
                            nc.scalar.activation(hk[0:P, o].rearrange("p (b c) w -> p b (c w)", b=2), p_h[0:P, o, :, 0:2 * W],
                                                 ACT.Relu).then_inc(relued, 1)
                        if new:
                            act.wait_ge(msg, done(g))
                            act.wait_ge(scanned, free1(g))
                            act.sem_inc(act_tick, 1)
                            for q, (_, w) in enumerate(parts):
                                last = nc.scalar.activation(m[q][:], p_o[q][0:w, 0:PG], ACT.Relu)
                            last.then_inc(relu0, 1)
                        if old:
                            store(g - 1, o)

                    skewed(act, NG, body)
                    for s in range(2):
                        act.wait_ge(h_stored[s], (NG // 2 + 1) * 16)

            for s in range(2):
                g_base[s] += NG // 2 * C * 16
        with Phase(nc) as ph:
            loaded, summed, dev, multd, dlink = (sem("b_" + v, ph) for v in ("loaded", "summed", "dev", "mult", "link"))
            h3t = sb("b_h3t", [128, T, F], F32, ph)
            last_m = sb("b_last_m", [128, T], F32, ph)
            part = sb("b_part", [128, 2, F], F32, ph)
            tot = sb("b_tot", [128, 2, F], F32, ph)
            p_s = pb("b_p_s", [128, 512], ph)
            block = ph.open()

            @block.sync
            def _(sp):
                sp.dma_start(h3t[0:P], htab[2].rearrange("(p t) f -> p t f", p=P)[:, :, 0:F]).then_inc(loaded, 16)

            @block.vector
            def _(dve):
                link = Links(dve, dlink)
                flat = lambda v: v.rearrange("p k f -> p (k f)")
                link(nc.vector.tensor_scalar(last_m[0:P], last_i[0:P], float(N), None, ALU.is_lt))
                dve.wait_ge(loaded, 16)
                link(nc.vector.tensor_tensor(hsp[0:P, :, 0:F], h3t[0:P], over(last_m[0:P], F), ALU.mult))
                link(nc.vector.tensor_tensor(hsp[0:P, :, F:2 * F], hsp[0:P, :, 0:F], h3t[0:P], ALU.mult))
                for k in range(2):
                    last = nc.vector.reduce_sum(part[0:P, k], hsp[0:P, :, k * F:(k + 1) * F].rearrange("p t f -> p f t"), AX)
                link(last)
                nc.vector.tensor_tensor(flat(part[0:P]), flat(part[0:P]), flat(stat[0:P]), ALU.add).then_inc(summed, 1)
                dve.wait_ge(multd, 1)
                link(nc.vector.tensor_scalar(flat(tot[:]), p_s[:, 0:2 * F], 1.0 / N, None, ALU.mult))
                link(nc.vector.tensor_tensor(part[:, 0], tot[:, 0], tot[:, 0], ALU.mult))
                link(nc.vector.tensor_tensor(tot[:, 1], tot[:, 1], part[:, 0], ALU.subtract))
                nc.vector.tensor_scalar(tot[:, 1], tot[:, 1], 0.0, None, ALU.max).then_inc(summed, 1)
                dve.wait_ge(dev, 1)
                link(nc.vector.reciprocal(part[:, 1], part[:, 1]))
                link(nc.vector.tensor_tensor(stat[:, 0], part[:, 1], gamma[:], ALU.mult))
                link(nc.vector.tensor_tensor(part[:, 0], stat[:, 0], tot[:, 0], ALU.mult))
                link(nc.vector.tensor_tensor(stat[:, 1], beta[:], part[:, 0], ALU.subtract))

            @block.tensor
            def _(pe):
                pe.wait_ge(summed, 1)
                nc.tensor.matmul(p_s[:, 0:2 * F], ones[0:P, :], part[0:P].rearrange("p k f -> p (k f)"), start=True, stop=True).then_inc(multd, 1)

            @block.scalar
            def _(act):
                act.wait_ge(summed, 2)
                nc.scalar.activation(part[:, 1], tot[:, 1], ACT.Sqrt, bias=epsc[:, 0:1]).then_inc(dev, 1)

        def bn(link, t, h, n):
            row = lambda k: stat[0:P, k].unsqueeze(1).broadcast_to([P, n, F])
            link(nc.vector.tensor_tensor(t, h, row(0), ALU.mult))
            link(nc.vector.tensor_tensor(t, t, row(1), ALU.add))

        with Phase(nc) as ph:
            loaded = [sem(f"f_loaded{s}", ph) for s in range(2)]
            stored = [sem(f"f_stored{s}", ph) for s in range(2)]
            var_made, dev_made, read, out_made, bn_made, dlink, plink = (
                sem("f_" + v, ph) for v in ("var_made", "dev_made", "read", "out_made", "bn_made", "link", "pool_link"))
            R = SUB * C
            xin = sb("f_xin", [128, 2, R, F], F32, ph)
            hin = sb("f_hin", [128, 2, R, F], F32, ph)
            sq = sb("f_sq", [128, R, F], F32, ph)
            cb, u = (sb(f"f_{v}", [128, 2, R, F], F32, ph) for v in ("cb", "u"))
            sm, va, sd, rc = (sb(f"f_{v}", [128, 2, R], F32, ph) for v in ("sm", "va", "sd", "rc"))
            xo = sb("f_xo", [128, 2, R, F], F32, ph)
            block = ph.open()

            @block.sync
            def _(sp):
                with sp.Fori(0, ND // 2) as i:
                    for s in range(2):
                        g = i * 2 + s
                        sp.wait_ge(read, free(g))
                        sp.sem_inc(sp_tick, 1)
                        sp.dma_start(xin[0:P, s], nodes(x2d, g)).then_inc(loaded[s], 16)
                        sp.dma_start(hin[0:P, s], nodes(h3d, g)).then_inc(loaded[s], 16)

            @block.gpsimd
            def _(pool):
                link = Links(pool, plink)
                row = lambda k: stat[0:P, k].unsqueeze(1).broadcast_to([P, R, F])
                with pool.Fori(0, ND // 2) as i:
                    link.turn(i, 2 * 2)
                    for s in range(2):
                        pool.wait_ge(loaded[s], (i + 1) * 32)
                        pool.sem_inc(pool_tick, 1)
                        link(nc.gpsimd.tensor_tensor(hin[0:P, s], hin[0:P, s], row(0), ALU.mult))
                        link(nc.gpsimd.tensor_tensor(hin[0:P, s], hin[0:P, s], row(1), ALU.add))
                        pool.sem_inc(bn_made, 1)
                link.end(ND // 2)

            @block.vector
            def _(dve):
                link = Links(dve, dlink)
                credit(dve, read)

                def first_residual(g, s, k):
                    dve.wait_ge(loaded[s], (k + 1) * 32)
                    dve.wait_ge(bn_made, g + 1)
                    dve.sem_inc(dve_tick, 1)
                    link(nc.vector.scalar_tensor_tensor(u[0:P, 0], hin[0:P, s], 0.0, xin[0:P, s], ALU.max, ALU.add))
                    dve.sem_inc(read, 1)
                    center(link, cb[0:P, 0], sm[0:P, 0], sq[0:P], va[0:P, 0], u[0:P, 0]).then_inc(var_made, 1)

                def body(g, s, k, new, old, more):
                    if not old:
                        first_residual(g, s, k)
                    if new:
                        dve.wait_ge(dev_made, g * 2 + 1)
                        dve.sem_inc(dve_tick, 1)
                        link(nc.vector.reciprocal(rc[0:P, 0], sd[0:P, 0]))
                        link(nc.vector.tensor_tensor(u[0:P, 1], cb[0:P, 0], over(rc[0:P, 0], F), ALU.mult))
                        center(link, cb[0:P, 1], sm[0:P, 1], sq[0:P], va[0:P, 1], u[0:P, 1]).then_inc(var_made, 1)
                    if more:
                        first_residual(g + 1, 1 - s, k + s)
                    if new:
                        dve.wait_ge(dev_made, g * 2 + 2)
                        dve.wait_ge(stored[s], (k + 1) * 16)
                        dve.sem_inc(dve_tick, 1)
                        link(nc.vector.reciprocal(rc[0:P, 1], sd[0:P, 1]))
                        nc.vector.tensor_tensor(xo[0:P, s], cb[0:P, 1], over(rc[0:P, 1], F), ALU.mult).then_inc(out_made, 1)

                skewed(dve, ND, body, link, lambda new, old, more: 6 * new + 4 * more + 4 * (not old))

            @block.scalar
            def _(act):
                for s in range(2):
                    act.sem_inc(stored[s], 16)

                def norm_deviation(q, n):
                    act.wait_ge(var_made, n)
                    act.sem_inc(act_tick, 1)
                    deviation(sd[0:P, q], va[0:P, q]).then_inc(dev_made, 1)

                def body(g, s, k, new, old, more):
                    if not old:
                        norm_deviation(0, 1)
                    if new:
                        norm_deviation(1, g * 2 + 2)
                    if more:
                        norm_deviation(0, g * 2 + 3)
                    if new:
                        act.wait_ge(out_made, g + 1)
                        act.sem_inc(act_tick, 1)
                        act.dma_start(nodes(out, g), xo[0:P, s]).then_inc(stored[s], 16)

                skewed(act, ND, body)
                for s in range(2):
                    act.wait_ge(stored[s], (ND // 2 + 1) * 16)

        s_base = T * 16
        with Phase(nc) as ph:
            staged = [sem(f"j_staged{s}", ph) for s in range(2)]
            staged_o = [sem(f"j_staged_o{s}", ph) for s in range(2)]
            filled = [sem(f"j_filled{s}", ph) for s in range(2)]
            attrs = [sem(f"j_attrs{s}", ph) for s in range(2)]
            (var_made, dev_made, e_turned, e_taken, hid, h_taken, w_mult, w_used, out_sum, tanhed, f_made,
             f_turned, scanned, backed, u_made, x4_made, placed, read) = (
                sem("j_" + v, ph) for v in ("var_made", "dev_made", "e_turned", "e_taken", "hid", "h_taken",
                                            "w_mult", "w_used", "out_sum", "tanhed", "f_made", "f_turned", "scanned",
                                            "backed", "u_made", "x4_made", "placed", "read"))
            dlink = sem("j_link", ph)
            M2 = 2 * MUL
            gx = sb("j_gx", [128, 2, 2 * C, 2 * F], F32, ph)
            stg = sb("j_stg", [128, 2, 2, C], I32, ph)
            stg_o = sb("j_stg_o", [128, 2, C], I32, ph)
            e3 = sb("j_e3", [128, 2, C, 3], F32, ph)
            e10 = sb("j_e10", [128, 2, C, 10], F32, ph)
            cb = sb("j_cb", [128, 2 * C, F], F32, ph)
            sq = sb("j_sq", [128, 2 * C, F], F32, ph)
            u = sb("j_u", [128, 2 * C, F], F32, ph)
            sm = sb("j_sm", [128, 2 * C], F32, ph)
            va = sb("j_va", [128, 2 * C], F32, ph)
            sd = sb("j_sd", [128, 2 * C], F32, ph)
            rc = sb("j_rc", [128, 2 * C], F32, ph)
            n2 = sb("j_n2", [128, C], F32, ph)
            nd = sb("j_nd", [128, C], F32, ph)
            nr = sb("j_nr", [128, C], F32, ph)
            e3q = sb("j_e3q", [128, C, 3], F32, ph)
            nv = sb("j_nv", [128, C, 3], F32, ph)
            x3 = sb("j_x3", [128, 2, 2 * C, F], F32, ph)
            ad = sb("j_ad", [128, C, M2], F32, ph)
            xv = sb("j_xv", [128, C, 3, MUL], F32, ph)
            xn = sb("j_xn", [128, C, 3, MUL], F32, ph)
            ef = sb("j_ef", [10, 2, PG], F32, ph)
            hf = sb("j_hf", [MUL, 2, PG], F32, ph)
            pr1 = sb("j_pr1", [128, 2, 2, 12, M2], F32, ph)
            pr2 = sb("j_pr2", [128, 2, 3, MOUT, MUL], F32, ph)
            o1 = sb("j_o1", [128, C, 24], F32, ph)
            o3 = sb("j_o3", [128, C, 3, MOUT], F32, ph)
            th = sb("j_th", [128, C, MUL], F32, ph)
            ew2 = sb("j_ew2", [128, C], F32, ph)
            vv = sb("j_vv", [128, C, MOUT, 3], F32, ph)
            fr = sb("j_fr", [128, 2, C, F], F32, ph)
            sc = sb("j_sc", [F, 2, PG], F32, ph)
            x4 = sb("j_x4", [128, 2, C, F], F32, ph)
            p_e = pb("j_p_e", [128, 512], ph)
            p_h = pb("j_p_h", [128, 512], ph)
            p_w = pb("j_p_w", [128, 2, 2, 512], ph)
            p_f = pb("j_p_f", [128, 512], ph)
            p_b = pb("j_p_b", [128, 512], ph)
            block = ph.open()
            GAIN = 1.593
            WC = 2 * C

            @block.sync
            def _(sp):
                edges = lambda v, g: v.rearrange("(t p) f -> p t f", p=P)[:, bass.ds(g * C, C), :]
                with sp.Fori(0, NG // 2) as i:
                    for s in range(2):
                        g = i * 2 + s
                        sp.wait_ge(read, free(g))
                        sp.wait_ge(e_turned, free(g))
                        sp.sem_inc(sp_tick, 1)
                        sp.dma_start(stg[0:P, s, 0], slot_i[0:P, bass.ds(g * C, C)]).then_inc(staged[s], 16)
                        sp.dma_start(stg[0:P, s, 1], slot_t[0:P, bass.ds(g * C, C)]).then_inc(staged[s], 16)
                        sp.dma_start(gx[0:P, s, 0:C], rows(btab[2], g)).then_inc(filled[s], 16)
                        sp.dma_start(e3[0:P, s], edges(attr3, g)).then_inc(attrs[s], 16)
                        sp.dma_start(e10[0:P, s], edges(attr10, g)).then_inc(attrs[s], 16)
                        sp.wait_ge(placed, free(g))
                        sp.sem_inc(sp_tick, 1)
                        sp.dma_start(stg_o[0:P, s], last_i[0:P, bass.ds(g * C, C)]).then_inc(staged_o[s], 16)

            @block.gpsimd
            def _(pool):
                pool.sem_inc(placed, LEAD)
                b_e, b_n = pool.to_reg(E - 1), pool.to_reg(N - 1)

                def gather(s, k):
                    pool.wait_ge(staged[s], (k + 1) * 32)
                    pool.wait_ge(filled[s], (k + 1) * 16)
                    pool.sem_inc(pool_tick, 1)
                    for q in range(2):
                        for c in range(C):
                            pool.indirect_dma_start(out=gx[0:P, s, q * C + c], out_offset=None, in_=htab[2],
                                                    in_offset=bass.IndirectOffsetOnAxis(ap=stg[0:P, s, q, c:c + 1], axis=0),
                                                    bounds_check=b_e, oob_is_err=False).then_inc(gathered[s], 16)

                def place(g, s, k):
                    pool.wait_ge(staged_o[s], (k + 1) * 16)
                    pool.wait_ge(x4_made, g + 1)
                    pool.sem_inc(pool_tick, 1)
                    for c in range(C):
                        pool.indirect_dma_start(out=out, out_offset=bass.IndirectOffsetOnAxis(ap=stg_o[0:P, s, c:c + 1], axis=0),
                                                in_=x4[0:P, s, c], in_offset=None, bounds_check=b_n,
                                                oob_is_err=False).then_inc(slotted, 16)
                    pool.wait_ge(slotted, g * C * 16 + C * 16 + s_base)
                    pool.sem_inc(pool_tick, 1)
                    pool.sem_inc(placed, 1)

                for s in range(2):
                    gather(s, 0)
                with pool.Fori(0, NG // 2 - 1) as i:
                    for s in range(2):
                        gather(s, i + 1)
                        place(i * 2 + s, s, i)
                for s in range(2):
                    place(NG - 2 + s, s, NG // 2 - 1)

            @block.vector
            def _(dve):
                link = Links(dve, dlink)
                link(nc.vector.memset(sc[:, 1, PG - 1:PG], 0.0))
                link.base = 1
                credit(dve, read, w_used, scanned, f_made, u_made)

                def residual(s, k):
                    dve.wait_ge(gathered[s], (k + 1) * 2 * C * 16 + g_base[s])
                    dve.wait_ge(attrs[s], (k + 1) * 32)
                    dve.sem_inc(dve_tick, 1)
                    bn(link, u[0:P], gx[0:P, s, :, 0:F], 2 * C)
                    link(nc.vector.scalar_tensor_tensor(u[0:P], u[0:P], 0.0, gx[0:P, s, :, F:2 * F], ALU.max, ALU.add))
                    link(nc.vector.tensor_tensor(e3q[0:P], e3[0:P, s], e3[0:P, s], ALU.mult))
                    nc.vector.reduce_sum(n2[0:P], e3q[0:P], AX)
                    center(link, cb[0:P], sm[0:P], sq[0:P], va[0:P], u[0:P]).then_inc(var_made, 1)

                def features(s, n_dev):
                    dve.wait_ge(dev_made, n_dev)
                    dve.sem_inc(dve_tick, 1)
                    nc.vector.reciprocal(nr[0:P], nd[0:P])
                    link(nc.vector.reciprocal(rc[0:P], sd[0:P]))
                    nc.vector.tensor_tensor(nv[0:P], e3[0:P, s], over(nr[0:P], 3), ALU.mult)
                    link(nc.vector.tensor_tensor(x3[0:P, s], cb[0:P], over(rc[0:P], F), ALU.mult))
                    dve.sem_inc(read, 1)
                    for q in range(2):
                        half = slice(q * 8, q * 8 + 8)
                        nc.vector.tensor_copy(ad[0:P, :, half], x3[0:P, s, q * C:(q + 1) * C, 0:8])
                        last = nc.vector.tensor_copy(xv[0:P, :, :, half], x3[0:P, s, q * C:(q + 1) * C, 8:F].rearrange("p c (u k) -> p c k u", k=3))
                    link(last)
                    link(nc.vector.tensor_tensor(xn[0:P], xv[0:P], over(nv[0:P], MUL), ALU.mult))
                    link(nc.vector.reduce_sum(ad[0:P, :, MUL:M2], xn[0:P].rearrange("p c k u -> p c u k"), AX))

                def weighted(g, c):
                    b = c % 2
                    dve.wait_ge(w_mult, g * C + c + 1 + WC)
                    dve.sem_inc(dve_tick, 1)
                    nc.vector.tensor_tensor(pr1[0:P, b], p_w[0:P, b, :, 0:384].rearrange("p b (o u) -> p b o u", u=M2),
                                            ad[0:P, c].unsqueeze(1).unsqueeze(1).broadcast_to([P, 2, 12, M2]), ALU.mult)
                    link(nc.vector.tensor_tensor(pr2[0:P, b],
                                                 p_w[0:P, b, 1, 384:512].rearrange("p (w u) -> p w u", u=MUL).unsqueeze(1).broadcast_to([P, 3, MOUT, MUL]),
                                                 xv[0:P, c].unsqueeze(2).broadcast_to([P, 3, MOUT, MUL]), ALU.mult))
                    dve.sem_inc(w_used, 1)
                    nc.vector.reduce_sum(o1[0:P, c], pr1[0:P, b].rearrange("p b o u -> p (b o) u"), AX)
                    link(nc.vector.reduce_sum(o3[0:P, c], pr2[0:P, b], AX))

                def vectors(g):
                    link(nc.vector.tensor_tensor(vv[0:P], over(o1[0:P, :, MUL:24], 3), nv[0:P].unsqueeze(2).broadcast_to([P, C, MOUT, 3]), ALU.mult))
                    nc.vector.tensor_scalar(ew2[0:P], ew[0:P, bass.ds(g * C, C)], GAIN, None, ALU.mult)
                    link(nc.vector.tensor_tensor(vv[0:P], vv[0:P], o3[0:P].rearrange("p c k w -> p c w k"), ALU.add))

                def messages(g, s):
                    dve.wait_ge(tanhed, g + 1)
                    dve.wait_ge(f_turned, free(g))
                    dve.sem_inc(dve_tick, 1)
                    link(nc.vector.tensor_tensor(th[0:P], th[0:P], over(ew2[0:P], MUL), ALU.mult))
                    nc.vector.tensor_copy(fr[0:P, s, :, 0:MOUT], th[0:P, :, 0:MOUT])
                    nc.vector.tensor_tensor(fr[0:P, s, :, MOUT:F].rearrange("p c (w k) -> p c w k", k=3), vv[0:P],
                                            over(th[0:P, :, MOUT:MUL], 3), ALU.mult).then_inc(f_made, 1)

                def sums(q, s):
                    dve.wait_ge(f_turned, done(q))
                    if not (isinstance(q, int) and q == 0):
                        dve.wait_ge(backed, free(q))
                    dve.sem_inc(dve_tick, 1)
                    link(nc.vector.tensor_tensor_scan(sc[:, s], same_b[0:F, bass.ds(q * PG, PG)], p_f[0:F, 0:PG],
                                                      sc[:, 1 - s, PG - 1:PG], ALU.mult, ALU.add))
                    dve.sem_inc(scanned, 1)

                def last_residual(q, s):
                    dve.wait_ge(backed, done(q))
                    dve.sem_inc(dve_tick, 1)
                    link(nc.vector.tensor_tensor(u[0:P, 0:C], p_b[0:P, 0:C * F].rearrange("p (c f) -> p c f", c=C), x3[0:P, s, C:2 * C], ALU.add))
                    dve.sem_inc(u_made, 1)
                    center(link, cb[0:P, 0:C], sm[0:P, 0:C], sq[0:P, 0:C], va[0:P, 0:C], u[0:P, 0:C]).then_inc(var_made, 1)

                def results(q, s, n_dev):
                    dve.wait_ge(dev_made, n_dev)
                    dve.wait_ge(placed, free(q) if not (isinstance(q, int) and q == 0) else LEAD - 1)
                    dve.sem_inc(dve_tick, 1)
                    link(nc.vector.reciprocal(rc[0:P, 0:C], sd[0:P, 0:C]))
                    link(nc.vector.tensor_tensor(x4[0:P, s], cb[0:P, 0:C], over(rc[0:P, 0:C], F), ALU.mult))
                    dve.sem_inc(x4_made, 1)

                def body(g, s, k, new, old, more):
                    o = 1 - s
                    if not old:
                        residual(s, k)
                        features(s, 1)
                    if new:
                        weighted(g, 0)
                    if old:
                        sums(g - 1, o)
                    if new:
                        weighted(g, 1)
                    if old:
                        last_residual(g - 1, o)
                    if new:
                        weighted(g, 2)
                    if old:
                        results(g - 1, o, g * 2 + new)
                    if more:
                        residual(o, k + s)
                    if new:
                        weighted(g, 3)
                        dve.sem_inc(out_sum, 1)
                        vectors(g)
                    if more:
                        features(o, g * 2 + 2)
                    if new:
                        messages(g, s)

                skewed(dve, NG, body, link, lambda new, old, more: 11 * new + 7 * old + 12 * more + 12 * (not old))

            @block.tensor
            def _(pe):
                credit(pe, e_turned, hid, f_turned, backed)
                pe.sem_inc(w_mult, WC)

                def hidden(g, s, k):
                    pe.wait_ge(attrs[s], (k + 1) * 32)
                    pe.wait_ge(e_taken, free1(g))
                    pe.sem_inc(pe_tick, 1)
                    for c in range(C):
                        last = nc.tensor.transpose(p_e[0:10, c * P:(c + 1) * P], e10[0:P, s, c], ident[0:P, 0:P])
                    last.then_inc(e_turned, 1)
                    pe.wait_ge(e_taken, done(g))
                    pe.wait_ge(h_taken, free1(g))
                    pe.sem_inc(pe_tick, 1)
                    nc.tensor.matmul(p_h[0:MUL, 0:PG], wl1[:], ef[:, s], start=True, stop=True).then_inc(hid, 1)

                def weights(g, s, c):
                    pe.wait_ge(w_used, g * C + c - 1 + LEAD)
                    pe.sem_inc(pe_tick, 1)
                    hc = hf[:, s, c * P:(c + 1) * P]
                    nc.tensor.matmul(p_w[0:P, c % 2, 0, 0:384], hc, wmix[:, 0:384], start=True, stop=True)
                    nc.tensor.matmul(p_w[0:P, c % 2, 1, 0:384], hc, wmix[:, 384:768], start=True, stop=True)
                    nc.tensor.matmul(p_w[0:P, c % 2, 1, 384:512], hc, wvec[:], start=True, stop=True).then_inc(w_mult, 1)

                def body(g, s, k, new, old, more):
                    o = 1 - s
                    if not old:
                        hidden(g, s, k)
                    if new:
                        pe.wait_ge(h_taken, done(g))
                        pe.sem_inc(pe_tick, 1)
                        weights(g, s, 0)
                        weights(g, s, 1)
                    if old:
                        pe.wait_ge(f_made, done(g - 1))
                        pe.wait_ge(scanned, free1(g - 1))
                        pe.sem_inc(pe_tick, 1)
                        for c in range(C):
                            last = nc.tensor.transpose(p_f[0:F, c * P:(c + 1) * P], fr[0:P, o, c], ident[0:P, 0:P])
                        last.then_inc(f_turned, 1)
                    if more:
                        hidden(g + 1, o, k + s)
                    if new:
                        weights(g, s, 2)
                    if old:
                        pe.wait_ge(scanned, done(g - 1))
                        pe.wait_ge(u_made, free1(g - 1))
                        pe.sem_inc(pe_tick, 1)
                        for c in range(C):
                            last = nc.tensor.transpose(p_b[0:P, c * F:(c + 1) * F], sc[:, o, c * P:(c + 1) * P], ident[0:F, 0:F])
                        last.then_inc(backed, 1)
                    if new:
                        weights(g, s, 3)

                skewed(pe, NG, body)

            @block.scalar
            def _(act):
                credit(act, e_taken, h_taken)

                def hidden(g, s):
                    act.wait_ge(e_turned, done(g))
                    act.wait_ge(hid, free(g))
                    act.sem_inc(act_tick, 1)
                    nc.scalar.copy(ef[:, s], p_e[0:10, 0:PG]).then_inc(e_taken, 1)
                    act.wait_ge(hid, done(g))
                    act.wait_ge(w_mult, g * C - C + WC)
                    act.sem_inc(act_tick, 1)
                    nc.scalar.activation(hf[:, s], p_h[0:MUL, 0:PG], ACT.Relu).then_inc(h_taken, 1)

                def first_deviation(n):
                    act.wait_ge(var_made, n)
                    act.sem_inc(act_tick, 1)
                    nc.scalar.activation(nd[0:P], n2[0:P], ACT.Sqrt)
                    deviation(sd[0:P], va[0:P]).then_inc(dev_made, 1)

                def body(g, s, k, new, old, more):
                    if not old:
                        hidden(g, s)
                        first_deviation(1)
                    if more:
                        hidden(g + 1, 1 - s)
                    if old:
                        act.wait_ge(var_made, g * 2 + new)
                        act.sem_inc(act_tick, 1)
                        deviation(sd[0:P, 0:C], va[0:P, 0:C]).then_inc(dev_made, 1)
                    if more:
                        first_deviation(g * 2 + 2)
                    if new:
                        act.wait_ge(out_sum, g + 1)
                        act.sem_inc(act_tick, 1)
                        nc.scalar.activation(th[0:P], o1[0:P, :, 0:MUL], ACT.Tanh).then_inc(tanhed, 1)

                skewed(act, NG, body)


def kernel(**inputs):
    import numpy as np
    import concourse.bacc as bacc
    from concourse.bass_utils import run_bass_kernel_spmd

    nc = bacc.Bacc("TRN2", target_bir_lowering=False, num_devices=1)
    arrays, args = {}, {}
    for name, value in inputs.items():
        value = np.ascontiguousarray(value)
        arrays["in_" + name] = value
        args[name] = nc.dram_tensor("in_" + name, value.shape, mybir.dt.from_np(value.dtype), kind="ExternalInput").ap()
    shape = inputs["x"].shape
    out = nc.dram_tensor("out_0", shape, F32, kind="ExternalOutput").ap()
    gnn_kernel(nc, args, out)
    return run_bass_kernel_spmd(nc, [arrays], core_ids=[0]).results[0]["out_0"]
```
